# Optimizing a Trainium2 kernel written in Bass

```python
import numpy as np
import jax
import jax.numpy as jnp

def _softmax(x, axis=-1):
    return jax.nn.softmax(x, axis=axis)

def _gelu(x):
    return jax.nn.gelu(x, approximate=True)

def _silu(x):
    return jax.nn.silu(x)

def _sigmoid(x):
    return jax.nn.sigmoid(x)

def _layernorm(x, axis=-1, eps=1e-05):
    m = jnp.mean(x, axis=axis, keepdims=True)
    v = jnp.var(x, axis=axis, keepdims=True)
    return (x - m) / jnp.sqrt(v + eps)

def _scatter_add(tgt, idx, src, axis=0):
    return tgt.at[idx].add(src)

def _segment_sum(src, seg, n):
    return jax.ops.segment_sum(src, seg, n)
kernel_name = 'mk_recurrent_d2_jaxref_r8_3ecdf3'

def setup_inputs(seed: int=0):
    np.random.seed(seed)
    _w = jnp.asarray

    def _L0_attn_setup():
        import jax, jax.numpy as jnp
        import numpy as np
        from jax import lax
        H, P, N, G, K, CHUNK = (64, 64, 128, 1, 4, 32)
        D_MODEL = 256
        D_INNER = H * P
        CONV_DIM = D_INNER + 2 * G * N
        EPS = 1e-05

        def _mamba2_forward(hidden_states, in_proj_w, conv_w, conv_b, dt_bias, A_log, D_param, norm_w, out_proj_w):
            b, l, _ = hidden_states.shape
            c = l // CHUNK
            proj = hidden_states @ in_proj_w
            gate = proj[..., :D_INNER]
            hbc = proj[..., D_INNER:D_INNER + CONV_DIM]
            dt = proj[..., D_INNER + CONV_DIM:]
            xt = hbc.transpose(0, 2, 1)
            y = lax.conv_general_dilated(xt, conv_w[:, None, :], window_strides=(1,), padding=[(K - 1, 0)], feature_group_count=CONV_DIM, dimension_numbers=('NCH', 'OIH', 'NCH'))
            hbc = jax.nn.silu(y + conv_b[None, :, None]).transpose(0, 2, 1)
            per_g = D_INNER // G
            hg = hbc.reshape(b, l, G, per_g + 2 * N)
            x = hg[..., :per_g].reshape(b, l, H, P)
            Bm = hg[..., per_g:per_g + N]
            Cm = hg[..., per_g + N:]
            hpg = H // G
            Bh = jnp.repeat(Bm, hpg, axis=2)
            Ch = jnp.repeat(Cm, hpg, axis=2)
            dt = jax.nn.softplus(dt + dt_bias)
            A = -jnp.exp(A_log)
            x_c = x.reshape(b, c, CHUNK, H, P)
            B_c = Bh.reshape(b, c, CHUNK, H, N)
            C_c = Ch.reshape(b, c, CHUNK, H, N)
            dt_c = dt.reshape(b, c, CHUNK, H)
            dA = dt_c * A[None, None, None, :]
            cum = jnp.cumsum(dA, axis=2)
            diff = cum[:, :, :, None, :] - cum[:, :, None, :, :]
            i = jnp.arange(CHUNK)
            mask = i[:, None] >= i[None, :]
            decay = jnp.exp(jnp.where(mask[None, None, :, :, None], diff, -jnp.inf))
            scores = jnp.einsum('bcihn,bcjhn->bcijh', C_c, B_c) * decay * dt_c[:, :, None, :, :]
            Y_diag = jnp.einsum('bcijh,bcjhp->bcihp', scores, x_c)
            decay_states = jnp.exp(cum[:, :, -1:, :] - cum)
            states = jnp.einsum('bclh,bclhn,bclhp->bchpn', decay_states * dt_c, B_c, x_c)
            chunk_decay = jnp.exp(cum[:, :, -1, :])

            def step(prev, inp):
                st, cd = inp
                new = cd[:, :, None, None] * prev + st
                return (new, prev)
            init = jnp.zeros((b, H, P, N), hidden_states.dtype)
            _, prev_states = lax.scan(step, init, (jnp.moveaxis(states, 1, 0), jnp.moveaxis(chunk_decay, 1, 0)))
            prev_states = jnp.moveaxis(prev_states, 0, 1)
            state_decay_out = jnp.exp(cum)
            Y_off = jnp.einsum('bclhn,bchpn,bclh->bclhp', C_c, prev_states, state_decay_out)
            yh = (Y_diag + Y_off).reshape(b, l, H, P) + D_param[None, None, :, None] * x
            yr = yh.reshape(b, l, D_INNER)
            hidden = yr * jax.nn.silu(gate)
            var = jnp.mean(hidden * hidden, axis=-1, keepdims=True)
            hidden = hidden * lax.rsqrt(var + EPS) * norm_w
            return hidden @ out_proj_w
        key = jax.random.key(seed)
        ks = jax.random.split(key, 6)
        s = lambda k, shape, scale: jax.random.normal(k, shape, jnp.float32) * scale
        return {'hidden_states': s(ks[0], (2, 256, D_MODEL), 1.0), 'in_proj_w': s(ks[1], (D_MODEL, D_INNER + CONV_DIM + H), D_MODEL ** (-0.5)), 'conv_w': s(ks[2], (CONV_DIM, K), K ** (-0.5)), 'conv_b': jnp.zeros((CONV_DIM,), jnp.float32), 'dt_bias': jnp.ones((H,), jnp.float32), 'A_log': jnp.log(jnp.arange(1, H + 1, dtype=jnp.float32)), 'D_param': jnp.ones((H,), jnp.float32), 'norm_w': jnp.ones((D_INNER,), jnp.float32), 'out_proj_w': s(ks[3], (D_INNER, D_MODEL), D_INNER ** (-0.5))}
    _L0_attn_in = _L0_attn_setup()

    def _L0_ffn_setup():
        import jax, jax.numpy as jnp
        import numpy as np
        HIDDEN = 256
        INTER = 1024
        BATCH, LOCAL_SEQ = (2, 512)
        key = jax.random.key(seed)
        k1, k2, k3 = jax.random.split(key, 3)
        h_shard = jax.random.normal(k1, (BATCH, LOCAL_SEQ, HIDDEN), dtype=jnp.float32)
        w_gate_up = jax.random.normal(k2, (2 * INTER, HIDDEN), dtype=jnp.float32) * 0.02
        w_down = jax.random.normal(k3, (HIDDEN, INTER), dtype=jnp.float32) * 0.02
        return {'h_shard': h_shard, 'w_gate_up': w_gate_up, 'w_down': w_down}
    _L0_ffn_in = _L0_ffn_setup()

    def _L1_attn_setup():
        import jax, jax.numpy as jnp
        import numpy as np
        import math
        HIDDEN = 256
        NUM_HEADS = 16
        HEAD_SIZE = HIDDEN // NUM_HEADS
        BATCH = 2
        SEQ = 256
        key = jax.random.key(seed)
        k_x, k_wq, k_bq, k_wo, k_bo = jax.random.split(key, 5)
        scale_in = 1.0 / math.sqrt(HIDDEN)
        return {'x': jax.random.normal(k_x, (BATCH, SEQ, HIDDEN), dtype=jnp.float32), 'Wqkv': jax.random.normal(k_wq, (HIDDEN, 3 * HIDDEN), dtype=jnp.float32) * scale_in, 'bqkv': jax.random.normal(k_bq, (3 * HIDDEN,), dtype=jnp.float32) * 0.01, 'Wo': jax.random.normal(k_wo, (HIDDEN, HIDDEN), dtype=jnp.float32) * scale_in, 'bo': jax.random.normal(k_bo, (HIDDEN,), dtype=jnp.float32) * 0.01}
    _L1_attn_in = _L1_attn_setup()

    def _L1_ffn_setup():
        import jax, jax.numpy as jnp
        import numpy as np
        NUM_EXPERTS = 32
        TOP_K = 4
        HIDDEN = 256
        INTER = 96
        key = jax.random.key(seed)
        k1, k2, k3, k4 = jax.random.split(key, 4)
        hidden_states = jax.random.normal(k1, (4, 64, HIDDEN), dtype=jnp.float32)
        gate = jax.random.normal(k2, (HIDDEN, NUM_EXPERTS), dtype=jnp.float32) * 0.02
        gate_up_proj = jax.random.normal(k3, (NUM_EXPERTS, HIDDEN, 2 * INTER), dtype=jnp.float32) * 0.02
        down_proj = jax.random.normal(k4, (NUM_EXPERTS, INTER, HIDDEN), dtype=jnp.float32) * 0.02
        return {'hidden_states': hidden_states, 'gate': gate, 'gate_up_proj': gate_up_proj, 'down_proj': down_proj}
    _L1_ffn_in = _L1_ffn_setup()
    _d = {'L0_attn_hidden_states': _L0_attn_in['hidden_states'], 'L0_attn_in_proj_w': _L0_attn_in['in_proj_w'], 'L0_attn_conv_w': _L0_attn_in['conv_w'], 'L0_attn_conv_b': _L0_attn_in['conv_b'], 'L0_attn_dt_bias': _L0_attn_in['dt_bias'], 'L0_attn_A_log': _L0_attn_in['A_log'], 'L0_attn_D_param': _L0_attn_in['D_param'], 'L0_attn_norm_w': _L0_attn_in['norm_w'], 'L0_attn_out_proj_w': _L0_attn_in['out_proj_w'], 'L0_ffn_w_gate_up': _L0_ffn_in['w_gate_up'], 'L0_ffn_w_down': _L0_ffn_in['w_down'], 'L1_attn_Wqkv': _L1_attn_in['Wqkv'], 'L1_attn_bqkv': _L1_attn_in['bqkv'], 'L1_attn_Wo': _L1_attn_in['Wo'], 'L1_attn_bo': _L1_attn_in['bo'], 'L1_ffn_gate': _L1_ffn_in['gate'], 'L1_ffn_gate_up_proj': _L1_ffn_in['gate_up_proj'], 'L1_ffn_down_proj': _L1_ffn_in['down_proj']}
    _x0 = _d['L0_attn_hidden_states']
    _d['L0_attn_hidden_states'] = jax.random.normal(jax.random.fold_in(jax.random.key(seed), 1), (4, 512, 256), dtype=_x0.dtype)
    del _x0
    return _d

def reference(L0_attn_hidden_states, L0_attn_in_proj_w, L0_attn_conv_w, L0_attn_conv_b, L0_attn_dt_bias, L0_attn_A_log, L0_attn_D_param, L0_attn_norm_w, L0_attn_out_proj_w, L0_ffn_w_gate_up, L0_ffn_w_down, L1_attn_Wqkv, L1_attn_bqkv, L1_attn_Wo, L1_attn_bo, L1_ffn_gate, L1_ffn_gate_up_proj, L1_ffn_down_proj):

    def _L0_attn_ref(hidden_states, in_proj_w, conv_w, conv_b, dt_bias, A_log, D_param, norm_w, out_proj_w):
        import jax, jax.numpy as jnp
        import numpy as np
        from jax import lax
        H, P, N, G, K, CHUNK = (64, 64, 128, 1, 4, 32)
        D_MODEL = 256
        D_INNER = H * P
        CONV_DIM = D_INNER + 2 * G * N
        EPS = 1e-05

        def _mamba2_forward(hidden_states, in_proj_w, conv_w, conv_b, dt_bias, A_log, D_param, norm_w, out_proj_w):
            b, l, _ = hidden_states.shape
            c = l // CHUNK
            proj = hidden_states @ in_proj_w
            gate = proj[..., :D_INNER]
            hbc = proj[..., D_INNER:D_INNER + CONV_DIM]
            dt = proj[..., D_INNER + CONV_DIM:]
            xt = hbc.transpose(0, 2, 1)
            y = lax.conv_general_dilated(xt, conv_w[:, None, :], window_strides=(1,), padding=[(K - 1, 0)], feature_group_count=CONV_DIM, dimension_numbers=('NCH', 'OIH', 'NCH'))
            hbc = jax.nn.silu(y + conv_b[None, :, None]).transpose(0, 2, 1)
            per_g = D_INNER // G
            hg = hbc.reshape(b, l, G, per_g + 2 * N)
            x = hg[..., :per_g].reshape(b, l, H, P)
            Bm = hg[..., per_g:per_g + N]
            Cm = hg[..., per_g + N:]
            hpg = H // G
            Bh = jnp.repeat(Bm, hpg, axis=2)
            Ch = jnp.repeat(Cm, hpg, axis=2)
            dt = jax.nn.softplus(dt + dt_bias)
            A = -jnp.exp(A_log)
            x_c = x.reshape(b, c, CHUNK, H, P)
            B_c = Bh.reshape(b, c, CHUNK, H, N)
            C_c = Ch.reshape(b, c, CHUNK, H, N)
            dt_c = dt.reshape(b, c, CHUNK, H)
            dA = dt_c * A[None, None, None, :]
            cum = jnp.cumsum(dA, axis=2)
            diff = cum[:, :, :, None, :] - cum[:, :, None, :, :]
            i = jnp.arange(CHUNK)
            mask = i[:, None] >= i[None, :]
            decay = jnp.exp(jnp.where(mask[None, None, :, :, None], diff, -jnp.inf))
            scores = jnp.einsum('bcihn,bcjhn->bcijh', C_c, B_c) * decay * dt_c[:, :, None, :, :]
            Y_diag = jnp.einsum('bcijh,bcjhp->bcihp', scores, x_c)
            decay_states = jnp.exp(cum[:, :, -1:, :] - cum)
            states = jnp.einsum('bclh,bclhn,bclhp->bchpn', decay_states * dt_c, B_c, x_c)
            chunk_decay = jnp.exp(cum[:, :, -1, :])

            def step(prev, inp):
                st, cd = inp
                new = cd[:, :, None, None] * prev + st
                return (new, prev)
            init = jnp.zeros((b, H, P, N), hidden_states.dtype)
            _, prev_states = lax.scan(step, init, (jnp.moveaxis(states, 1, 0), jnp.moveaxis(chunk_decay, 1, 0)))
            prev_states = jnp.moveaxis(prev_states, 0, 1)
            state_decay_out = jnp.exp(cum)
            Y_off = jnp.einsum('bclhn,bchpn,bclh->bclhp', C_c, prev_states, state_decay_out)
            yh = (Y_diag + Y_off).reshape(b, l, H, P) + D_param[None, None, :, None] * x
            yr = yh.reshape(b, l, D_INNER)
            hidden = yr * jax.nn.silu(gate)
            var = jnp.mean(hidden * hidden, axis=-1, keepdims=True)
            hidden = hidden * lax.rsqrt(var + EPS) * norm_w
            return hidden @ out_proj_w
        return _mamba2_forward(hidden_states, in_proj_w, conv_w, conv_b, dt_bias, A_log, D_param, norm_w, out_proj_w)

    def _L0_ffn_ref(h_shard, w_gate_up, w_down):
        import jax, jax.numpy as jnp
        import numpy as np
        HIDDEN = 256
        INTER = 1024
        BATCH, LOCAL_SEQ = (2, 512)
        batch, local_seq, hidden = h_shard.shape
        gate_up = jnp.einsum('bsh,oh->bso', h_shard, w_gate_up)
        gate, up = jnp.split(gate_up, 2, axis=-1)
        h = jax.nn.silu(gate) * up
        out = jnp.einsum('bsi,hi->bsh', h, w_down)
        return out

    def _L1_attn_ref(x, Wqkv, bqkv, Wo, bo):
        import jax, jax.numpy as jnp
        import numpy as np
        import math
        HIDDEN = 256
        NUM_HEADS = 16
        HEAD_SIZE = HIDDEN // NUM_HEADS
        BATCH = 2
        SEQ = 256
        b, s, _ = x.shape
        kqv = x @ Wqkv + bqkv
        kqv = kqv.reshape(b, s, 3, NUM_HEADS, HEAD_SIZE)
        q = kqv[:, :, 0]
        k = kqv[:, :, 1]
        v = kqv[:, :, 2]
        scores = jnp.einsum('bsnh,btnh->bnst', k, q) / math.sqrt(HEAD_SIZE)
        ones = jnp.ones_like(scores)
        scores = jnp.triu(scores) + -10000.0 * jnp.tril(ones, k=-1)
        attn = jax.nn.softmax(scores, axis=2)
        out = jnp.einsum('bnkq,bknh->bqnh', attn, v)
        out = out.reshape(b, s, NUM_HEADS * HEAD_SIZE)
        return out @ Wo + bo

    def _L1_ffn_ref(hidden_states, gate, gate_up_proj, down_proj):
        import jax, jax.numpy as jnp
        import numpy as np
        NUM_EXPERTS = 32
        TOP_K = 4
        HIDDEN = 256
        INTER = 96
        batch_size = hidden_states.shape[0]
        x = hidden_states.reshape(-1, HIDDEN)
        num_tokens = x.shape[0]
        router_logits = jnp.einsum('TD,DE->TE', x, gate)
        routing_weights = jax.nn.softmax(router_logits.astype(jnp.float32), axis=-1)
        top_k_weights, top_k_indices = jax.lax.top_k(routing_weights, TOP_K)
        top_k_weights = top_k_weights / top_k_weights.sum(axis=-1, keepdims=True)
        top_k_weights = top_k_weights.astype(x.dtype)
        router_weights = jnp.zeros((num_tokens, NUM_EXPERTS), dtype=x.dtype)
        token_indices = jnp.broadcast_to(jnp.arange(num_tokens)[:, None], top_k_indices.shape)
        router_weights = router_weights.at[token_indices, top_k_indices].set(top_k_weights)
        gate_up = jnp.einsum('TD,EDF->TEF', x, gate_up_proj)
        g, u = jnp.split(gate_up, 2, axis=-1)
        gated = u * jax.nn.silu(g)
        next_states = jnp.einsum('TEF,EFD->TED', gated, down_proj)
        next_states = (next_states * router_weights[..., None]).sum(axis=1)
        return next_states.reshape(batch_size, -1, HIDDEN)
    x = L0_attn_hidden_states
    xn = _layernorm(x, axis=-1)
    s = _L0_attn_ref(xn, L0_attn_in_proj_w, L0_attn_conv_w, L0_attn_conv_b, L0_attn_dt_bias, L0_attn_A_log, L0_attn_D_param, L0_attn_norm_w, L0_attn_out_proj_w)
    g = _silu(_L0_ffn_ref(xn, L0_ffn_w_gate_up, L0_ffn_w_down))
    x = x + s * g
    xn = _layernorm(x, axis=-1)
    s = _L1_attn_ref(xn, L1_attn_Wqkv, L1_attn_bqkv, L1_attn_Wo, L1_attn_bo)
    g = _silu(_L1_ffn_ref(xn, L1_ffn_gate, L1_ffn_gate_up_proj, L1_ffn_down_proj))
    x = x + s * g
    return x

_drawn_inputs = setup_inputs


def setup_inputs(seed=0):
    import zlib

    import numpy as np

    out = dict(_drawn_inputs(seed))
    spreads = {'L0_attn_conv_b': (0.0, 0.8),
     'L0_attn_dt_bias': (1.0, 0.6),
     'L0_attn_D_param': (1.0, 0.6),
     'L0_attn_norm_w': (1.0, 0.6)}
    factors = {'L0_attn_conv_w': 2.689,
     'L0_attn_A_log': 8.0,
     'L0_ffn_w_gate_up': 2.809,
     'L1_attn_Wqkv': 8.0,
     'L1_attn_bqkv': 8.0,
     'L1_attn_Wo': 8.0,
     'L1_attn_bo': 200.0,
     'L1_ffn_gate': 8.0,
     'L1_ffn_gate_up_proj': 8.0,
     'L1_ffn_down_proj': 8.0}
    for name, (base, spread) in spreads.items():
        noise = np.random.default_rng([zlib.crc32(name.encode()), seed]).standard_normal(out[name].shape)
        drawn = base * np.exp(spread * noise) if base else spread * noise
        out[name] = jnp.asarray(drawn.astype(out[name].dtype))
    for name, factor in factors.items():
        out[name] = (out[name] * factor).astype(out[name].dtype)
    return out
```

```python
import concourse.bass as bass
from concourse import mybir
from contextlib import ExitStack, contextmanager

F32 = mybir.dt.float32
F32R = mybir.dt.float32r
ALU = mybir.AluOpType
ACT = mybir.ActivationFunctionType
AX = mybir.AxisListType

P = 128
BATCH, SEQ, DM = 4, 512, 256
T = BATCH * SEQ
NT = T // P
KT = DM // P
CPB = SEQ // P
HEADS, HD, NS = 64, 64, 128
DI = HEADS * HD
PAIRS = HEADS // 2
EPS = 1e-5
MASKED = -3.0e38


@contextmanager
def phase_semaphores(nc, tag):
    taken = []

    def sem(name):
        taken.append(nc.alloc_semaphore(f"{tag}_{name}"))
        return taken[-1]
    yield sem
    nc.clear_and_free_semaphores(taken)
    nc.all_engine_barrier()


def split_matmuls(pe, out, w_hi, w_lo, x_hi, x_lo, seeded=False):
    n = len(w_hi)
    for k in range(n):
        pe.matmul(out, w_hi[k], x_hi[k], start=(k == 0 and not seeded), stop=False, skip_group_check=seeded)
        pe.matmul(out, w_hi[k], x_lo[k], start=False, stop=False, skip_group_check=seeded)
        last = pe.matmul(out, w_lo[k], x_hi[k], start=False, stop=(k == n - 1), skip_group_check=seeded)
    return last


def layernorm_phase(nc, tag, x_dram, ident, xt_hi, xt_lo):
    G = 4
    PAIRT = NT // 2
    with ExitStack() as ctx:
        sb = lambda n, s, d=F32: ctx.enter_context(nc.sbuf_tensor(f"{tag}_{n}", s, d))
        sem = ctx.enter_context(phase_semaphores(nc, tag))
        x = sb("x", [P, NT, DM])
        xn = sb("xn", [P, NT, DM])
        stats = sb("stats", [P, NT, 6])
        mv = sb("mv", [P, NT, 2])
        veps = sb("veps", [P, NT])
        std = sb("std", [P, NT])
        rstd = sb("rstd", [P, NT])
        pt = ctx.enter_context(nc.psum_tensor(f"{tag}_pt", [P, 2, KT, 2 * P], F32))
        x_in = [sem(f"x_in{g}") for g in range(NT // G)]
        stats_done, veps_done, std_done = sem("stats_done"), sem("veps_done"), sem("std_done")
        xn_done, transposed, hi_done, lo_done = sem("xn_done"), sem("transposed"), sem("hi_done"), sem("lo_done")
        block = ctx.enter_context(nc.Block())
        xv = x_dram.rearrange("(t p) d -> p t d", p=P)

        @block.sync
        def _(sp):
            for g in range(NT // G):
                sp.dma_start(x[:, g * G:(g + 1) * G, :], xv[:, g * G:(g + 1) * G, :]).then_inc(x_in[g], 16)

        @block.vector
        def _(dve):
            for t in range(NT):
                if t % G == 0:
                    dve.wait_ge(x_in[t // G], 16)
                dve.bn_stats(stats[:, t, :], x[:, t, :]).then_inc(stats_done, 1)
            dve.wait_ge(stats_done, NT)
            for t in range(NT):
                dve.bn_aggr(mv[:, t, :], stats[:, t, :]).then_inc(stats_done, 1)
            dve.wait_ge(stats_done, 2 * NT)
            dve.tensor_scalar(veps[:, :], mv[:, :, 1], EPS, None, ALU.add).then_inc(veps_done, 1)
            dve.wait_ge(std_done, 1)
            dve.reciprocal(rstd[:, :], std[:, :]).then_inc(veps_done, 1)
            dve.wait_ge(veps_done, 2)

            def low_part(g):
                dve.wait_ge(hi_done, g + 1)
                dve.tensor_tensor(xt_lo[:, :, g * 2 * P:(g + 1) * 2 * P], pt[:, g % 2, :, :],
                                  xt_hi[:, :, g * 2 * P:(g + 1) * 2 * P].bitcast(F32),
                                  ALU.subtract).then_inc(lo_done, 1)

            for g in range(PAIRT):
                for t in (2 * g, 2 * g + 1):
                    dve.tensor_scalar(xn[:, t, :], x[:, t, :], mv[:, t, 0:1], rstd[:, t:t + 1],
                                      ALU.subtract, ALU.mult).then_inc(xn_done, 1)
                if g:
                    low_part(g - 1)
            low_part(PAIRT - 1)

        @block.tensor
        def _(pe):
            for g in range(PAIRT):
                pe.wait_ge(xn_done, 2 * g + 2)
                if g >= 2:
                    pe.wait_ge(lo_done, g - 1)
                for k in range(KT):
                    for t in range(2):
                        last = pe.transpose(pt[:, g % 2, k, t * P:(t + 1) * P],
                                            xn[:, 2 * g + t, k * P:(k + 1) * P], ident[:, :])
                last.then_inc(transposed, 1)

        @block.scalar
        def _(act):
            act.wait_ge(veps_done, 1)
            act.activation(std[:, :], veps[:, :], ACT.Sqrt).then_inc(std_done, 1)
            for g in range(PAIRT):
                act.wait_ge(transposed, g + 1)
                act.activation(xt_hi[:, :, g * 2 * P:(g + 1) * 2 * P], pt[:, g % 2, :, :],
                               ACT.Copy).then_inc(hi_done, 1)


def gated_ffn_phase(nc, tag, mt, wg_dram, wu_dram, wd_dram, xt_hi, xt_lo, gate_out, router=None):
    with ExitStack() as ctx:
        sb = lambda n, s, d=F32: ctx.enter_context(nc.sbuf_tensor(f"{tag}_{n}", s, d))
        sem = ctx.enter_context(phase_semaphores(nc, tag))
        CH = 512
        NCH = 2 * KT * mt * P // CH
        w_hi = sb("w_hi", [P, 2 * KT, mt * P], F32R)
        w_lo = sb("w_lo", [P, 2 * KT, mt * P], F32R)
        w_raw = sb("w_raw", [P, 4, CH])
        wd = sb("wd", [P, mt, DM])
        sg = sb("sg", [P, 2, SEQ])
        h = sb("h", [P, 2, SEQ])
        og = sb("og", [P, CPB, DM])
        wb = sb("wb", [P, 2, SEQ]) if router else None
        pg = ctx.enter_context(nc.psum_tensor(f"{tag}_pg", [P, 2, SEQ], F32))
        pu = ctx.enter_context(nc.psum_tensor(f"{tag}_pu", [P, 2, SEQ], F32))
        po = ctx.enter_context(nc.psum_tensor(f"{tag}_po", [P, CPB, 512], F32))
        raw_in = [sem(f"raw_in{i}") for i in range(4)]
        wd_in = sem("wd_in")
        w_hi_done, w_lo_done = sem("w_hi_done"), sem("w_lo_done")
        gate_ready, up_ready = sem("gate_ready"), sem("up_ready")
        silu_done = sem("silu_done")
        up_used = sem("up_used")
        h_ready = sem("h_ready") if router else up_used
        down_done = sem("down_done")
        out_ready = sem("out_ready")
        out_used = sem("out_used")
        out_stored = sem("out_stored")
        wb_in = [sem(f"wb_in{i}") for i in range(2)] if router else None
        block = ctx.enter_context(nc.Block())

        chunks = [(s, k, c) for c in range(mt * P // CH) for s in range(2) for k in range(KT)]
        tiles_of = CH // P
        wsrc = [wg_dram, wu_dram]
        out_v = gate_out.rearrange("(b t p) d -> b p t d", b=BATCH, p=P)

        def pieces(m):
            width, r, out = router[1], m * P, []
            while r < (m + 1) * P:
                e = r // width
                end = min((e + 1) * width, (m + 1) * P)
                out.append((r - m * P, end - r, e))
                r = end
            return out

        arrived = [0, 0]
        wb_at = []
        for m in range(mt if router else 0):
            arrived[m % 2] += 16 * len(pieces(m))
            wb_at.append(arrived[m % 2])

        @block.sync
        def _(sp):
            for n, (s, k, c) in enumerate(chunks):
                if n >= 4:
                    sp.wait_ge(w_lo_done, n - 3)
                sp.dma_start(w_raw[:, n % 4, :], wsrc[s][k * P:(k + 1) * P, c * CH:(c + 1) * CH])\
                  .then_inc(raw_in[n % 4], 16)
                if n == 3:
                    sp.dma_start(wd[:, :, :], wd_dram.rearrange("(m p) d -> p m d", p=P)).then_inc(wd_in, 16)
            if router:
                with sp.Fori(0, BATCH) as b:
                    for m in range(mt):
                        sp.wait_ge(h_ready, b * mt + m + 1)
                        for r, n, e in pieces(m):
                            sp.dma_start(wb[r:r + n, m % 2, :],
                                         router[0][e:e + 1, bass.ds(b * SEQ, SEQ)].broadcast_to([n, SEQ]))\
                              .then_inc(wb_in[m % 2], 16)

        @block.tensor
        def _(pe):
            pe.sem_inc(silu_done, 2)
            pe.sem_inc(up_used, 2)
            pe.sem_inc(down_done, 2)
            pe.sem_inc(out_used, 1)
            if router:
                pe.sem_inc(h_ready, 2)

            def hidden(b, m):
                c = slice(m * P, (m + 1) * P)
                xs_hi = [xt_hi[:, k, bass.ds(b * SEQ, SEQ)] for k in range(KT)]
                xs_lo = [xt_lo[:, k, bass.ds(b * SEQ, SEQ)] for k in range(KT)]
                pe.wait_ge(silu_done, b * mt + m + 1)
                split_matmuls(pe, pg[:, m % 2, :], [w_hi[:, k, c] for k in range(KT)],
                              [w_lo[:, k, c] for k in range(KT)], xs_hi, xs_lo).then_inc(gate_ready, 1)
                pe.wait_ge(up_used, b * mt + m + 1)
                split_matmuls(pe, pu[:, m % 2, :], [w_hi[:, KT + k, c] for k in range(KT)],
                              [w_lo[:, KT + k, c] for k in range(KT)], xs_hi, xs_lo).then_inc(up_ready, 1)

            def down(b, m):
                pe.wait_ge(h_ready, b * mt + m + 3)
                if m == 0:
                    pe.wait_ge(out_used, b + 1)
                for t in range(CPB):
                    last = pe.matmul(po[:, t, 0:DM], h[:, m % 2, t * P:(t + 1) * P], wd[:, m, :],
                                     start=(m == 0), stop=(m == mt - 1))
                last.then_inc(down_done, 1)
                return last

            pe.wait_ge(w_lo_done, NCH)
            pe.wait_ge(wd_in, 16)
            with pe.Fori(0, BATCH) as b:
                for m in range(mt):
                    hidden(b, m)
                    if m:
                        down(b, m - 1)
                down(b, mt - 1)

        @block.scalar
        def _(act):
            for n, (s, k, c) in enumerate(chunks):
                act.wait_ge(raw_in[n % 4], 16 * (n // 4 + 1))
                act.activation(w_hi[:, s * KT + k, c * CH:(c + 1) * CH], w_raw[:, n % 4, :], ACT.Copy)\
                   .then_inc(w_hi_done, 1)
            act.sem_inc(out_stored, 16)
            with act.Fori(0, BATCH) as b:
                for m in range(mt):
                    act.wait_ge(gate_ready, b * mt + m + 1)
                    act.wait_ge(up_used, b * mt + m + 1)
                    act.activation(sg[:, m % 2, :], pg[:, m % 2, :], ACT.Silu).then_inc(silu_done, 1)
                act.wait_ge(down_done, (b + 1) * mt + 2)
                act.wait_ge(out_stored, 16 * b + 16)
                act.activation(og[:, :, :], po[:, :, 0:DM], ACT.Silu).then_inc(out_used, 1)
                act.wait_ge(out_used, b + 2)
                act.dma_start(out_v[bass.ds(b, 1)].rearrange("b p t d -> (b p) t d"), og[:, :, :])\
                   .then_inc(out_stored, 16)
            act.wait_ge(out_stored, 16 * (BATCH + 1))

        @block.vector
        def _(dve):
            for n, (s, k, c) in enumerate(chunks):
                dve.wait_ge(w_hi_done, n + 1)
                dve.tensor_tensor(w_lo[:, s * KT + k, c * CH:(c + 1) * CH], w_raw[:, n % 4, :],
                                  w_hi[:, s * KT + k, c * CH:(c + 1) * CH].bitcast(F32), ALU.subtract)\
                   .then_inc(w_lo_done, 1)
            with dve.Fori(0, BATCH) as b:
                for m in range(mt):
                    dve.wait_ge(up_ready, b * mt + m + 1)
                    dve.wait_ge(silu_done, b * mt + m + 3)
                    dve.wait_ge(down_done, b * mt + m + 1)
                    dve.tensor_tensor(h[:, m % 2, :], pu[:, m % 2, :], sg[:, m % 2, :], ALU.mult)\
                       .then_inc(up_used, 1)
                    if router:
                        dve.wait_ge(up_used, b * mt + m + 3)
                        dve.wait_ge(wb_in[m % 2], b * arrived[m % 2] + wb_at[m])
                        dve.tensor_tensor(h[:, m % 2, :], h[:, m % 2, :], wb[:, m % 2, :], ALU.mult)\
                           .then_inc(h_ready, 1)


def dynamics_phase(nc, xt_hi, xt_lo, w_bcdt, conv_bc, dt_prm, ident, causal, b_tok, c_t, cb_m, scratch):
    cum_d, ecum_d, last_d, tab_d = scratch
    with ExitStack() as ctx:
        sb = lambda n, s, d=F32: ctx.enter_context(nc.sbuf_tensor(f"dyn_{n}", s, d))
        sem = ctx.enter_context(phase_semaphores(nc, "dyn"))
        W = 3 * P
        w_raw = sb("w_raw", [P, KT, W])
        w_hi = sb("w_hi", [P, KT, W], F32R)
        w_lo = sb("w_lo", [P, KT, W], F32R)
        cp = sb("cp", [P, 2, 5])
        dp = sb("dp", [HEADS, 2])
        a_neg = sb("a_neg", [HEADS, 1])
        y = sb("y", [P, 2, SEQ])
        b_t = sb("b_t", [P, T])
        v = sb("v", [HEADS, T])
        av = sb("av", [HEADS, T])
        u = sb("u", [HEADS, T])
        z = sb("z", [HEADS, T])
        dt_t = sb("dt_t", [HEADS, T])
        keep = sb("keep", [HEADS, T])
        cum = sb("cum", [HEADS, T])
        ecum = sb("ecum", [HEADS, T])
        wst = sb("wst", [HEADS, T])
        last = sb("last", [HEADS, NT])
        last_b = sb("last_b", [P, HEADS, NT])
        tab = sb("tab", [P, PAIRS, BATCH, 4, CPB, 2])
        pp = [ctx.enter_context(nc.psum_tensor(f"dyn_pp{i}", [P, SEQ], F32)) for i in range(3)]
        pt = [ctx.enter_context(nc.psum_tensor(f"dyn_pt{i}", [P, SEQ], F32)) for i in range(4)]
        w_in, prm_in = sem("w_in"), sem("prm_in")
        whi, wlo, proj = sem("whi"), sem("wlo"), sem("proj")
        conv0, taps, bc_ready, v_ready = sem("conv0"), sem("taps"), sem("bc_ready"), sem("v_ready")
        scal, vec = sem("scal"), sem("vec")
        keep_done, tr, ev, cbd, cbe = sem("keep_done"), sem("tr"), sem("ev"), sem("cbd"), sem("cbe")
        out_c, last_in = sem("out_c"), sem("last_in")
        block = ctx.enter_context(nc.Block())
        chunks = lambda ap: ap.rearrange("p (c t) -> p c t", t=P)

        SC_AEXP, SC_ABS, SC_EXP, SC_LN, SC_ECUM, SC_WST, SC_LAST = range(1, 8)
        (VEC_ANEG, VEC_U, VEC_D, VEC_Z, VEC_NUM, VEC_DEN, VEC_REC, VEC_NUM2, VEC_Q, VEC_DT, VEC_DA,
         VEC_CUM, VEC_DIFF) = range(1, 14)

        @block.sync
        def _(sp):
            sp.dma_start(w_raw[:, :, :], w_bcdt.rearrange("(k p) n -> p k n", p=P)).then_inc(w_in, 16)
            sp.dma_start(cp[:, :, :], conv_bc.rearrange("(s p) n -> p s n", p=P)).then_inc(prm_in, 16)
            sp.dma_start(dp[:, :], dt_prm).then_inc(prm_in, 16)
            sp.wait_ge(vec, VEC_CUM)
            sp.dma_start(cum_d, cum[:, :]).then_inc(out_c, 16)
            sp.wait_ge(scal, SC_LAST)
            sp.dma_start(last_d, last[:, :]).then_inc(out_c, 16)
            sp.dma_start(ecum_d, ecum[:, :]).then_inc(out_c, 16)
            sp.wait_ge(out_c, 48)
            sp.dma_start(last_b[:, :, :].rearrange("p h c -> p (h c)"),
                         last_d.rearrange("(a h) c -> a (h c)", a=1).broadcast_to([P, HEADS * NT])).then_inc(last_in, 16)
            sp.wait_ge(ev, 4 * BATCH)
            sp.dma_start(tab_d, tab[:, :, :, :, :, :].rearrange("p k b f c e -> p (k b f c e)")).then_inc(out_c, 16)
            sp.wait_ge(out_c, 64)

        @block.gpsimd
        def _(pool):
            pool.memset(keep[:, :], 1.0).then_inc(keep_done, 1)
            pool.wait_ge(keep_done, 1)
            pool.memset(chunks(keep[:, :])[:, :, 0:1], 0.0).then_inc(keep_done, 1)

        @block.tensor
        def _(pe):
            pe.wait_ge(wlo, 1)
            for b in range(BATCH):
                xs = slice(b * SEQ, (b + 1) * SEQ)
                for s in range(3):
                    if b:
                        pe.wait_ge(*((taps, 3 * (2 * (b - 1) + s + 1)) if s < 2 else (v_ready, b)))
                    c = slice(s * P, (s + 1) * P)
                    split_matmuls(pe, pp[s][:, :], [w_hi[:, k, c] for k in range(KT)],
                                  [w_lo[:, k, c] for k in range(KT)], [xt_hi[:, k, xs] for k in range(KT)],
                                  [xt_lo[:, k, xs] for k in range(KT)]).then_inc(proj, 1)
            for b in range(BATCH):
                pe.wait_ge(bc_ready, 2 * b + 2)
                if b >= 2:
                    pe.wait_ge(cbe, 2 * (b - 1))
                for c in range(CPB):
                    t = slice((b * CPB + c) * P, (b * CPB + c + 1) * P)
                    m = pe.transpose(pt[b % 2][:, c * P:(c + 1) * P], b_t[:, t], ident[:, :])
                m.then_inc(cbd, 1)
                for c in range(CPB):
                    t = slice((b * CPB + c) * P, (b * CPB + c + 1) * P)
                    m = pe.matmul(pt[2 + b % 2][:, c * P:(c + 1) * P], b_t[:, t], c_t[:, t], start=True, stop=True)
                m.then_inc(cbd, 1)
            n = 0
            pe.wait_ge(cbe, 2 * BATCH)
            for f, (src, sm, at) in enumerate(((cum, vec, VEC_CUM), (dt_t, vec, VEC_DT), (wst, scal, SC_WST))):
                pe.wait_ge(sm, at)
                for b in range(BATCH):
                    if n >= 4:
                        pe.wait_ge(ev, n - 3)
                    for c in range(CPB):
                        t = slice((b * CPB + c) * P, (b * CPB + c + 1) * P)
                        m = pe.transpose(pt[n % 4][:, c * HEADS:(c + 1) * HEADS], src[:, t], ident[0:HEADS, 0:HEADS])
                    m.then_inc(tr, 1)
                    n += 1

        @block.scalar
        def _(act):
            act.wait_ge(w_in, 16)
            act.activation(w_hi[:, :, :], w_raw[:, :, :], ACT.Copy).then_inc(whi, 1)
            act.wait_ge(prm_in, 32)
            act.activation(a_neg[:, :], dp[:, 1:2], ACT.Exp).then_inc(scal, 1)

            def conv_silu(b, s):
                n = 2 * b + s
                act.wait_ge(taps, 3 * (n + 1))
                act.activation((b_t if s == 0 else c_t)[:, b * SEQ:(b + 1) * SEQ], y[:, s, :], ACT.Silu)\
                   .then_inc(bc_ready, 1)

            for b in range(BATCH):
                for s in range(2):
                    act.wait_ge(proj, 3 * b + s + 1)
                    if b:
                        act.wait_ge(bc_ready, 2 * (b - 1) + s + 1)
                    act.activation(y[:, s, :], pp[s][:, :], ACT.Identity, bias=cp[:, s, 4:5], scale=cp[:, s, 3:4])\
                       .then_inc(conv0, 1)
                act.wait_ge(proj, 3 * b + 3)
                act.activation(v[:, b * SEQ:(b + 1) * SEQ], pp[2][0:HEADS, :], ACT.Identity, bias=dp[:, 0:1])\
                   .then_inc(v_ready, 1)
                conv_silu(b, 0)
                conv_silu(b, 1)
            act.wait_ge(v_ready, BATCH)
            act.activation(av[:, :], v[:, :], ACT.Abs).then_inc(scal, 1)
            act.wait_ge(scal, SC_ABS)
            act.activation(av[:, :], av[:, :], ACT.Exp, scale=-1.0).then_inc(scal, 1)
            act.wait_ge(vec, VEC_U)
            act.activation(z[:, :], u[:, :], ACT.Ln).then_inc(scal, 1)
            act.wait_ge(vec, VEC_CUM)
            act.activation(ecum[:, :], cum[:, :], ACT.Exp).then_inc(scal, 1)
            act.wait_ge(vec, VEC_DIFF)
            act.activation(wst[:, :], wst[:, :], ACT.Exp).then_inc(scal, 1)
            act.activation(last[:, :], chunks(cum[:, :])[:, :, P - 1], ACT.Exp).then_inc(scal, 1)
            for n in range(BATCH):
                act.wait_ge(tr, n + 1)
                src = pt[n % 4][:, 0:CPB * HEADS].rearrange("p (c k e) -> p c k e", c=CPB, e=2)
                act.activation(tab[:, :, n, 0, :, :].rearrange("p k c e -> p c k e"), src, ACT.Copy, scale=-1.0)\
                   .then_inc(ev, 1)

        @block.vector
        def _(dve):
            dve.wait_ge(whi, 1)
            dve.tensor_tensor(w_lo[:, :, :], w_raw[:, :, :], w_hi[:, :, :].bitcast(F32), ALU.subtract).then_inc(wlo, 1)
            dve.wait_ge(scal, SC_AEXP)
            dve.tensor_scalar(a_neg[:, :], a_neg[:, :], -1.0, None, ALU.mult).then_inc(vec, 1)
            for b in range(BATCH):
                for s in range(2):
                    n = 2 * b + s
                    dve.wait_ge(conv0, n + 1)
                    for j in range(1, 4):
                        if j > 1:
                            dve.wait_ge(taps, 3 * n + j - 1)
                        dve.scalar_tensor_tensor(y[:, s, j:SEQ], pp[s][:, 0:SEQ - j], cp[:, s, 3 - j:4 - j],
                                                 y[:, s, j:SEQ], ALU.mult, ALU.add).then_inc(taps, 1)
            for b in range(BATCH):
                dve.wait_ge(cbd, 2 * b + 1)
                dve.tensor_copy(b_tok[:, b * CPB:(b + 1) * CPB, :],
                                pt[b % 2][:, :].rearrange("p (c n) -> p c n", n=NS)).then_inc(cbe, 1)
                dve.wait_ge(cbd, 2 * b + 2)
                dve.tensor_tensor(cb_m[:, b * CPB:(b + 1) * CPB, :],
                                  pt[2 + b % 2][:, :].rearrange("p (c n) -> p c n", n=P),
                                  causal[:, :].unsqueeze(1).broadcast_to([P, CPB, P]), ALU.mult).then_inc(cbe, 1)
            dve.wait_ge(scal, SC_EXP)
            dve.tensor_scalar(u[:, :], av[:, :], 1.0, None, ALU.add).then_inc(vec, 1)
            dve.wait_ge(scal, SC_LN)
            dve.wait_ge(vec, VEC_U)
            dve.tensor_scalar(u[:, :], u[:, :], 1.0, None, ALU.subtract).then_inc(vec, 1)
            dve.wait_ge(vec, VEC_D)
            dve.tensor_scalar(cum[:, :], u[:, :], 0.0, None, ALU.is_equal).then_inc(vec, 1)
            dve.wait_ge(vec, VEC_Z)
            dve.tensor_tensor(z[:, :], z[:, :], cum[:, :], ALU.add).then_inc(vec, 1)
            dve.tensor_tensor(u[:, :], u[:, :], cum[:, :], ALU.add).then_inc(vec, 1)
            dve.wait_ge(vec, VEC_DEN)
            dve.reciprocal(u[:, :], u[:, :]).then_inc(vec, 1)
            dve.tensor_tensor(z[:, :], z[:, :], av[:, :], ALU.mult).then_inc(vec, 1)
            dve.wait_ge(vec, VEC_NUM2)
            dve.tensor_tensor(z[:, :], z[:, :], u[:, :], ALU.mult).then_inc(vec, 1)
            dve.wait_ge(vec, VEC_Q)
            dve.scalar_tensor_tensor(dt_t[:, :], v[:, :], 0.0, z[:, :], ALU.max, ALU.add).then_inc(vec, 1)
            dve.wait_ge(vec, VEC_DT)
            dve.tensor_scalar(v[:, :], dt_t[:, :], a_neg[:, :], None, ALU.mult).then_inc(vec, 1)
            dve.wait_ge(vec, VEC_DA)
            dve.wait_ge(keep_done, 2)
            dve.tensor_tensor_scan(cum[:, :], keep[:, :], v[:, :], 0.0, ALU.mult, ALU.add).then_inc(vec, 1)
            dve.wait_ge(vec, VEC_CUM)
            cc = chunks(cum[:, :])
            dve.tensor_tensor(chunks(wst[:, :]), cc[:, :, P - 1:P].broadcast_to([HEADS, NT, P]), cc,
                              ALU.subtract).then_inc(vec, 1)
            for n in range(BATCH, 3 * BATCH):
                dve.wait_ge(tr, n + 1)
                dve.wait_ge(ev, n)
                src = pt[n % 4][:, 0:CPB * HEADS].rearrange("p (c k e) -> p c k e", c=CPB, e=2)
                dve.tensor_copy(tab[:, :, n % BATCH, n // BATCH, :, :].rearrange("p k c e -> p c k e"), src)\
                   .then_inc(ev, 1)
            dve.wait_ge(last_in, 16)
            for b in range(BATCH):
                src = last_b[:, :, b * CPB:(b + 1) * CPB].rearrange("p (k e) c -> p c k e", e=2)
                dve.tensor_copy(tab[:, :, b, 3, :, :].rearrange("p k c e -> p c k e"), src).then_inc(ev, 1)


def wait(eng, sem, count):
    if not isinstance(count, int) or count > 0:
        eng.wait_ge(sem, count)


def pipeline(eng, *stages):
    def slots(k):
        for b in range(BATCH):
            for stage, lag in stages:
                q, s = divmod(b - lag, BATCH)
                pair = k + q
                if not isinstance(k, int) or 0 <= pair < PAIRS:
                    stage(pair, s)
    for k in (-1, 0, 1):
        slots(k)
    with eng.Fori(2, PAIRS - 1) as k:
        slots(k)
    slots(PAIRS - 1)
    slots(PAIRS)


def ssm_phase(nc, xt_hi, xt_lo, w_dram, wo_dram, prm_dram, ident, b_tok, c_t, cb_m, scratch, out_acc, sq_acc):
    cum_d, ecum_d, last_d, tab_d = scratch
    with ExitStack() as ctx:
        sb = lambda n, s, d=F32: ctx.enter_context(nc.sbuf_tensor(f"ssm_{n}", s, d))
        sem = ctx.enter_context(phase_semaphores(nc, "ssm"))
        pb = lambda n, w=SEQ: ctx.enter_context(nc.psum_tensor(f"ssm_{n}", [P, w], F32))
        R = BATCH
        w_raw = sb("w_raw", [P, KT, 2 * P])
        w_hi = sb("w_hi", [P, KT, 2 * P], F32R)
        w_lo = sb("w_lo", [P, KT, 2 * P], F32R)
        wo_raw = sb("wo_raw", [P, DM + 1])
        wo = sb("wo", [P, DM])
        prm = sb("prm", [P, R, 6])
        tab = sb("tab", [P, R, 4, CPB * 2])
        cm = sb("cm", [P, R, 2, SEQ])
        er = sb("er", [P, R, SEQ - P])
        y = sb("y", [P, 2, SEQ])
        xs = sb("xs", [P, R, SEQ])
        sg = sb("sg", [P, R, SEQ])
        xdt = sb("xdt", [P, 2, SEQ])
        xw = sb("xw", [P, 2, SEQ - P])
        S = sb("S", [P, 2, CPB - 1, P])
        t1 = sb("t1", [P, 2, SEQ - P])
        t2 = sb("t2", [P, 2, SEQ])
        h = sb("h", [P, 2, SEQ])
        sq = sb("sq", [P, 2, SEQ])
        px, pg, pt, pyd, pst, pyo = (pb(n) for n in ("px", "pg", "pt", "pyd", "pst", "pyo"))
        po = pb("po", CPB * DM)
        names = ("w_in wo_in w_hi_done w_ready wo_ready x_ready g_ready conv0_done taps_done gate_done xs_ready "
                 "tr_done xdt_ready xw_ready masked exp_done m_ready yd_done st_done s1_done rec_done yo_done "
                 "t2_done t1_done hs_done h_ready sq_done acc_done out_done oacc_done zeroed mask_begun")
        (w_in, wo_in, w_hi_done, w_ready, wo_ready, x_ready, g_ready, conv0_done, taps_done, gate_done, xs_ready,
         tr_done, xdt_ready, xw_ready, masked, exp_done, m_ready, yd_done, st_done, s1_done, rec_done, yo_done,
         t2_done, t1_done, hs_done, h_ready, sq_done, acc_done, out_done, oacc_done, zeroed, mask_begun) = map(sem, names.split())
        prm_in, tab_in, cm_in, er_in = ([sem(f"{n}{b}") for b in range(R)] for n in ("prm_in", "tab_in", "cm_in", "er_in"))
        block = ctx.enter_context(nc.Block())
        N = lambda k, b: BATCH * k + b + 1

        @block.sync
        def _(sp):
            def weights(k, b):
                if b == 0:
                    wait(sp, w_ready, k)
                    sp.dma_start(w_raw[:, :, :].rearrange("p k n -> p (k n)"), w_dram[bass.ds(k, 1)].rearrange("a p n -> (a p) n"))\
                      .then_inc(w_in, 16)

            def out_weights(k, b):
                if b == 1:
                    wait(sp, wo_ready, k)
                    sp.dma_start(wo_raw[:, :], wo_dram[bass.ds(k, 1)].rearrange("a p n -> (a p) n")).then_inc(wo_in, 16)

            def tables(k, b):
                n = N(k, b)
                wait(sp, rec_done, 2 * (n - R))
                wait(sp, t2_done, n - R)
                sp.dma_start(prm[:, b, :], prm_dram[bass.ds(k, 1)].rearrange("a p n -> (a p) n")).then_inc(prm_in[b], 16)
                sp.dma_start(tab[:, b].rearrange("p f n -> p (f n)"),
                             tab_d[:, bass.ds((k * BATCH + b) * 32, 32)]).then_inc(tab_in[b], 16)
                wait(sp, yd_done, n - R)
                sp.dma_start(cm[:, b, :, :], cum_d[bass.ds(2 * k, 2), b * SEQ:(b + 1) * SEQ].unsqueeze(0)
                             .broadcast_to([P, 2, SEQ])).then_inc(cm_in[b], 16)
                wait(sp, t1_done, n - R)
                for e in range(2):
                    sp.dma_start(er[e * HD:(e + 1) * HD, b, :],
                                 ecum_d[bass.ds(2 * k + e, 1), b * SEQ + P:(b + 1) * SEQ].broadcast_to([HD, SEQ - P]))\
                      .then_inc(er_in[b], 16)

            pipeline(sp, (weights, -4), (out_weights, 0), (tables, 0))

        @block.tensor
        def _(pe):
            def project(k, b):
                n = N(k, b)
                if b == 0:
                    pe.wait_ge(w_ready, k + 1)
                cols = slice(b * SEQ, (b + 1) * SEQ)
                for s, (bank, done, used, at) in enumerate(((px, x_ready, taps_done, 3 * (n - 1)),
                                                            (pg, g_ready, gate_done, n - 1))):
                    c = slice(s * P, (s + 1) * P)
                    wait(pe, used, at)
                    split_matmuls(pe, bank[:, :], [w_hi[:, j, c] for j in range(KT)],
                                  [w_lo[:, j, c] for j in range(KT)], [xt_hi[:, j, cols] for j in range(KT)],
                                  [xt_lo[:, j, cols] for j in range(KT)]).then_inc(done, 1)

            def transposes(k, b):
                n = N(k, b)
                pe.wait_ge(xs_ready, n)
                wait(pe, xdt_ready, n - 1)
                for c in range(CPB):
                    last = pe.transpose(pt[:, c * P:(c + 1) * P], xs[:, b, c * P:(c + 1) * P], ident[:, :])
                last.then_inc(tr_done, 1)

            def y_diag(k, b):
                n = N(k, b)
                pe.wait_ge(m_ready, n)
                pe.wait_ge(xdt_ready, n)
                wait(pe, t2_done, n - 1)
                for c in range(CPB):
                    for e in range(2):
                        t = slice(c * P, (c + 1) * P)
                        last = pe.matmul(pyd[e * HD:(e + 1) * HD, t], xdt[:, b % 2, c * P + e * HD:c * P + (e + 1) * HD],
                                         cm[:, b, e, t], start=True, stop=True)
                last.then_inc(yd_done, 1)

            def states(k, b):
                n = N(k, b)
                pe.wait_ge(xw_ready, n)
                wait(pe, rec_done, 2 * (n - 1))
                wait(pe, s1_done, n - 1)
                for c in range(CPB - 1):
                    t = slice(c * P, (c + 1) * P)
                    last = pe.matmul(pst[:, t], b_tok[:, b * CPB + c, :], xw[:, b % 2, t], start=True, stop=True)
                last.then_inc(st_done, 1)

            def y_off(k, b):
                n = N(k, b)
                pe.wait_ge(rec_done, 2 * n)
                pe.wait_ge(s1_done, n)
                wait(pe, t1_done, n - 1)
                for c in range(1, CPB):
                    last = pe.matmul(pyo[:, (c - 1) * P:c * P], S[:, b % 2, c - 1, :],
                                     c_t[:, b * SEQ + c * P:b * SEQ + (c + 1) * P], start=True, stop=True)
                last.then_inc(yo_done, 1)

            def project_out(k, b):
                n = N(k, b)
                if b == 0:
                    pe.wait_ge(wo_ready, k + 1)
                pe.wait_ge(h_ready, n)
                wait(pe, oacc_done, n - 1)
                for c in range(CPB):
                    last = pe.matmul(po[:, c * DM:(c + 1) * DM], h[:, b % 2, c * P:(c + 1) * P], wo[:, :],
                                     start=True, stop=True)
                last.then_inc(out_done, 1)

            pipeline(pe, (project, 0), (transposes, 1), (y_diag, 2), (states, 2), (y_off, 3), (project_out, 4))

        @block.scalar
        def _(act):
            def split_high(k, b):
                if b == 0:
                    act.wait_ge(w_in, 16 * (k + 1))
                    wait(act, g_ready, BATCH * k)
                    act.activation(w_hi[:, :, :], w_raw[:, :, :], ACT.Copy).then_inc(w_hi_done, 1)

            def conv_first(k, b):
                n = N(k, b)
                act.wait_ge(x_ready, n)
                act.wait_ge(prm_in[b], 16 * (k + 1))
                wait(act, xs_ready, n - 2)
                act.activation(y[:, b % 2, :], px[:, :], ACT.Identity, bias=prm[:, b, 4:5], scale=prm[:, b, 3:4])\
                   .then_inc(conv0_done, 1)

            def gate(k, b):
                n = N(k, b)
                act.wait_ge(g_ready, n)
                wait(act, h_ready, n - R)
                act.activation(sg[:, b, :], pg[:, :], ACT.Silu).then_inc(gate_done, 1)

            def conv_silu(k, b):
                n = N(k, b)
                act.wait_ge(taps_done, 3 * n)
                wait(act, t2_done, n - R)
                act.activation(xs[:, b, :], y[:, b % 2, :], ACT.Silu).then_inc(xs_ready, 1)

            def decay(k, b):
                n = N(k, b)
                act.wait_ge(masked, n)
                act.wait_ge(tab_in[b], 16 * (k + 1))
                for e in range(2):
                    for c in range(CPB):
                        t = slice(c * P, (c + 1) * P)
                        last = act.activation(cm[:, b, e, t], cm[:, b, e, t], ACT.Exp,
                                              bias=tab[:, b, 0, 2 * c + e:2 * c + e + 1])
                last.then_inc(exp_done, 1)

            def first_state(k, b):
                n = N(k, b)
                act.wait_ge(st_done, n)
                wait(act, yo_done, n - 2)
                act.activation(S[:, b % 2, 0, :], pst[:, 0:P], ACT.Copy).then_inc(s1_done, 1)

            def squares(k, b):
                n = N(k, b)
                act.wait_ge(h_ready, n)
                wait(act, acc_done, n - 2)
                act.activation(sq[:, b % 2, :], h[:, b % 2, :], ACT.Square).then_inc(sq_done, 1)

            pipeline(act, (conv_first, 0), (gate, 0), (split_high, -1), (first_state, 2), (conv_silu, 0),
                     (decay, 0), (squares, 4))

        @block.vector
        def _(dve):
            def split_low(k, b):
                if b == 0:
                    dve.wait_ge(w_hi_done, k + 1)
                    dve.tensor_tensor(w_lo[:, :, :], w_raw[:, :, :], w_hi[:, :, :].bitcast(F32), ALU.subtract)\
                       .then_inc(w_ready, 1)

            def scale_out_weights(k, b):
                if b == 3:
                    dve.wait_ge(wo_in, 16 * (k + 1))
                    wait(dve, out_done, BATCH * k)
                    dve.tensor_scalar(wo[:, :], wo_raw[:, 0:DM], wo_raw[:, DM:DM + 1], None, ALU.mult)\
                       .then_inc(wo_ready, 1)

            def conv_taps(k, b):
                n = N(k, b)
                dve.wait_ge(conv0_done, n)
                for j in range(1, 4):
                    if j > 1:
                        dve.wait_ge(taps_done, 3 * (n - 1) + j - 1)
                    dve.scalar_tensor_tensor(y[:, b % 2, j:SEQ], px[:, 0:SEQ - j], prm[:, b, 3 - j:4 - j],
                                             y[:, b % 2, j:SEQ], ALU.mult, ALU.add).then_inc(taps_done, 1)

            def x_times_dt(k, b):
                n = N(k, b)
                dve.wait_ge(tr_done, n)
                dve.wait_ge(tab_in[b], 16 * (k + 1))
                wait(dve, yd_done, n - 2)
                wait(dve, xw_ready, n - 2)
                dve.tensor_tensor(xdt[:, b % 2, :].rearrange("p (n d) -> p n d", d=HD),
                                  pt[:, :].rearrange("p (n d) -> p n d", d=HD),
                                  tab[:, b, 1, :].unsqueeze(2).broadcast_to([P, 2 * CPB, HD]), ALU.mult)\
                   .then_inc(xdt_ready, 1)

            def scores(k, b):
                dve.wait_ge(exp_done, N(k, b))
                for e in range(2):
                    last = dve.tensor_tensor(cm[:, b, e, :], cm[:, b, e, :],
                                             cb_m[:, b * CPB:(b + 1) * CPB, :].rearrange("p c i -> p (c i)"), ALU.mult)
                last.then_inc(m_ready, 1)

            def direct_term(k, b):
                n = N(k, b)
                dve.wait_ge(yd_done, n)
                wait(dve, h_ready, n - 2)
                dve.scalar_tensor_tensor(t2[:, b % 2, :], xs[:, b, :], prm[:, b, 5:6], pyd[:, :], ALU.mult, ALU.add)\
                   .then_inc(t2_done, 1)

            def recurrence(k, b):
                n = N(k, b)
                dve.wait_ge(s1_done, n)
                for c in range(1, CPB - 1):
                    if c > 1:
                        dve.wait_ge(rec_done, 2 * (n - 1) + c - 1)
                    for e in range(2):
                        d = slice(e * HD, (e + 1) * HD)
                        last = dve.scalar_tensor_tensor(S[:, b % 2, c, d], S[:, b % 2, c - 1, d],
                                                        tab[:, b, 3, 2 * c + e:2 * c + e + 1],
                                                        pst[:, c * P + e * HD:c * P + (e + 1) * HD], ALU.mult, ALU.add)
                    last.then_inc(rec_done, 1)

            def off_term(k, b):
                n = N(k, b)
                dve.wait_ge(yo_done, n)
                dve.wait_ge(er_in[b], 32 * (k + 1))
                wait(dve, hs_done, n - 2)
                dve.tensor_tensor(t1[:, b % 2, :], pyo[:, 0:SEQ - P], er[:, b, :], ALU.mult).then_inc(t1_done, 1)

            def add_out(k, b):
                n = N(k, b)
                dve.wait_ge(out_done, n)
                wait(dve, oacc_done, n - R)
                acc = out_acc[:, b * CPB:(b + 1) * CPB, :].rearrange("p c d -> p (c d)")
                dve.tensor_tensor(acc, po[:, :], acc, ALU.add).then_inc(oacc_done, 1)

            dve.memset(out_acc[:, :, :], 0.0).then_inc(zeroed, 1)
            dve.memset(sq_acc[:, :, :], 0.0).then_inc(zeroed, 1)
            dve.wait_ge(zeroed, 2)
            pipeline(dve, (x_times_dt, 1), (conv_taps, 0), (split_low, -1), (scores, 1), (direct_term, 2),
                     (recurrence, 2), (off_term, 3), (add_out, 4), (scale_out_weights, 0))

        @block.gpsimd
        def _(pool):
            def mask(k, b):
                pool.wait_ge(cm_in[b], 16 * (k + 1))
                pool.sem_inc(mask_begun, 1)
                m = cm[:, b, :, :].rearrange("p e (c i) -> p (e c) i", i=P)
                pool.affine_select(out=m, in_=m, compare_op=ALU.is_ge, fill=masked_value, base=0,
                                   pattern=[[0, 2 * CPB], [1, P]], channel_multiplier=-1).then_inc(masked, 1)

            def x_to_state(k, b):
                n = N(k, b)
                pool.wait_ge(xdt_ready, n)
                wait(pool, st_done, n - 2)
                pool.tensor_tensor(xw[:, b % 2, :].rearrange("p (n d) -> p n d", d=HD),
                                   xdt[:, b % 2, 0:SEQ - P].rearrange("p (n d) -> p n d", d=HD),
                                   tab[:, b, 2, 0:2 * (CPB - 1)].unsqueeze(2).broadcast_to([P, 2 * (CPB - 1), HD]),
                                   ALU.mult).then_inc(xw_ready, 1)

            def gated(k, b):
                n = N(k, b)
                pool.wait_ge(t1_done, n)
                pool.wait_ge(t2_done, n)
                pool.tensor_tensor(t2[:, b % 2, P:SEQ], t2[:, b % 2, P:SEQ], t1[:, b % 2, :], ALU.add).then_inc(hs_done, 1)
                pool.wait_ge(hs_done, n)
                pool.wait_ge(gate_done, n)
                wait(pool, out_done, n - 2)
                wait(pool, sq_done, n - 2)
                pool.tensor_tensor(h[:, b % 2, :], t2[:, b % 2, :], sg[:, b, :], ALU.mult).then_inc(h_ready, 1)

            def add_squares(k, b):
                n = N(k, b)
                pool.wait_ge(sq_done, n)
                wait(pool, acc_done, n - R)
                pool.tensor_tensor(sq_acc[:, b, :], sq_acc[:, b, :], sq[:, b % 2, :], ALU.add).then_inc(acc_done, 1)

            masked_value = pool.to_reg(MASKED)
            pool.wait_ge(zeroed, 2)
            pipeline(pool, (mask, 0), (x_to_state, 1), (gated, 3), (add_squares, 4))


def mamba_output_phase(nc, x_dram, gate_dram, out_acc, sq_acc, x1_dram):
    with ExitStack() as ctx:
        sb = lambda n, s, d=F32: ctx.enter_context(nc.sbuf_tensor(f"mo_{n}", s, d))
        sem = ctx.enter_context(phase_semaphores(nc, "mo"))
        x = sb("x", [P, NT, DM])
        g = sb("g", [P, NT, DM])
        ones = sb("ones", [P, 1])
        var = sb("var", [P, NT])
        std = sb("std", [P, NT])
        rstd = sb("rstd", [P, NT])
        pv = ctx.enter_context(nc.psum_tensor("mo_pv", [P, NT], F32))
        x_in, g_in, ones_done, sums, var_done, std_done = map(sem, "x_in g_in ones_done sums var_done std_done".split())
        rstd_done, scaled, added, stored = map(sem, "rstd_done scaled added stored".split())
        block = ctx.enter_context(nc.Block())

        @block.sync
        def _(sp):
            sp.dma_start(g[:, :, :], gate_dram.rearrange("(t p) d -> p t d", p=P)).then_inc(g_in, 16)
            sp.dma_start(x[:, :, :], x_dram.rearrange("(t p) d -> p t d", p=P)).then_inc(x_in, 16)
            ov = x1_dram.rearrange("(t p) d -> p t d", p=P)
            for q in range(4):
                sp.wait_ge(added, 4 * (q + 1))
                sp.dma_start(ov[:, 4 * q:4 * q + 4, :], x[:, 4 * q:4 * q + 4, :]).then_inc(stored, 16)
            sp.wait_ge(stored, 64)

        @block.tensor
        def _(pe):
            pe.wait_ge(ones_done, 1)
            for t in range(NT):
                m = pe.matmul(pv[:, t:t + 1], sq_acc[:, t // CPB, (t % CPB) * P:(t % CPB + 1) * P], ones[:, :],
                              start=True, stop=True)
            m.then_inc(sums, 1)

        @block.scalar
        def _(act):
            act.wait_ge(var_done, 1)
            act.activation(std[:, :], var[:, :], ACT.Sqrt).then_inc(std_done, 1)

        @block.vector
        def _(dve):
            dve.memset(ones[:, :], 1.0).then_inc(ones_done, 1)
            dve.wait_ge(sums, 1)
            dve.tensor_scalar(var[:, :], pv[:, :], 1.0 / DI, EPS, ALU.mult, ALU.add).then_inc(var_done, 1)
            dve.wait_ge(std_done, 1)
            dve.reciprocal(rstd[:, :], std[:, :]).then_inc(rstd_done, 1)
            dve.wait_ge(rstd_done, 1)
            dve.wait_ge(g_in, 16)
            for t in range(NT):
                dve.scalar_tensor_tensor(g[:, t, :], out_acc[:, t, :], rstd[:, t:t + 1], g[:, t, :], ALU.mult, ALU.mult)\
                   .then_inc(scaled, 1)
            dve.wait_ge(x_in, 16)
            for t in range(NT):
                dve.wait_ge(scaled, t + 1)
                dve.tensor_tensor(x[:, t, :], x[:, t, :], g[:, t, :], ALU.add).then_inc(added, 1)


def constants_phase(nc, ident, causal):
    with ExitStack() as ctx:
        ready = ctx.enter_context(phase_semaphores(nc, "const"))("ready")
        block = ctx.enter_context(nc.Block())

        @block.gpsimd
        def _(pool):
            pool.memset(ident[:, :], 0.0).then_inc(ready, 1)
            pool.memset(causal[:, :], 1.0).then_inc(ready, 1)
            pool.wait_ge(ready, 2)
            pool.affine_select(out=ident[:, :], in_=ident[:, :], compare_op=ALU.not_equal, fill=1.0, base=0,
                               pattern=[[-1, P]], channel_multiplier=1).then_inc(ready, 1)
            pool.affine_select(out=causal[:, :], in_=causal[:, :], compare_op=ALU.is_ge, fill=0.0, base=0,
                               pattern=[[1, P]], channel_multiplier=-1).then_inc(ready, 1)


HN, HW = 16, 16
GROUP = 4
MASK_SCORE = 10000.0


def attention_constants_phase(nc, ident_b, block_b, head_mask, later, ones, count, floor):
    with ExitStack() as ctx:
        sem = ctx.enter_context(phase_semaphores(nc, "ac"))
        s1, s2 = sem("ready"), sem("count")
        ci = ctx.enter_context(nc.sbuf_tensor("ac_ci", [P, CPB], mybir.dt.int32))
        block = ctx.enter_context(nc.Block())

        @block.gpsimd
        def _(pool):
            for m, value in ((ident_b, 0.0), (block_b, 0.0), (head_mask, 1.0), (later, 1.0), (ones, 1.0),
                             (floor, MASK_SCORE)):
                pool.memset(m[:, :], value).then_inc(s1, 1)
            pool.wait_ge(s1, 6)
            pool.affine_select(out=ident_b[:, :], in_=ident_b[:, :], compare_op=ALU.not_equal, fill=1.0, base=0,
                               pattern=[[-1, P]], channel_multiplier=1).then_inc(s1, 1)
            pool.affine_select(out=block_b[:, :], in_=block_b[:, :], compare_op=ALU.is_ge, fill=MASKED, base=0,
                               pattern=[[-1, P]], channel_multiplier=1).then_inc(s1, 1)
            pool.affine_select(out=later[:, :], in_=later[:, :], compare_op=ALU.is_ge, fill=0.0, base=-1,
                               pattern=[[-1, P]], channel_multiplier=1).then_inc(s1, 1)
            pool.affine_select(out=head_mask[:, :], in_=head_mask[:, :], compare_op=ALU.is_ge, fill=0.0, base=0,
                               pattern=[[-HW, P // HW]], channel_multiplier=1).then_inc(s1, 1)
            pool.wait_ge(s1, 10)
            pool.affine_select(out=head_mask[:, :], in_=head_mask[:, :], compare_op=ALU.is_ge, fill=0.0, base=HW - 1,
                               pattern=[[HW, P // HW]], channel_multiplier=-1).then_inc(s1, 1)
            pool.affine_select(out=floor[:, :], in_=floor[:, :], compare_op=ALU.is_ge, fill=-MASKED, base=SEQ - 2,
                               pattern=[[-P, CPB]], channel_multiplier=-1).then_inc(s1, 1)
            pool.iota(ci[:, :], pattern=[[-P, CPB]], base=SEQ - 1, channel_multiplier=-1).then_inc(s2, 1)

        @block.vector
        def _(dve):
            dve.wait_ge(s2, 1)
            dve.tensor_copy(count[:, :], ci[:, :]).then_inc(s2, 1)


def attention_phase(nc, xt_hi, xt_lo, w_dram, b_dram, bv_dram, wo_dram, bo_dram, ident, s1):
    with ExitStack() as ctx:
        sb = lambda n, s, d=F32: ctx.enter_context(nc.sbuf_tensor(f"at_{n}", s, d))
        sem = ctx.enter_context(phase_semaphores(nc, "at"))
        BF = mybir.dt.bfloat16
        ident_b, block_b = sb("ident_b", [P, P], BF), sb("block_b", [P, P], BF)
        head_mask = sb("head_mask", [P, P // HW])
        later, ones = sb("later", [P, P]), sb("ones", [P, P])
        count, floor = sb("count", [P, CPB]), sb("floor", [P, CPB])
        attention_constants_phase(nc, ident_b, block_b, head_mask, later, ones, count, floor)
        W = 3 * DM
        GROUPS = HN // GROUP
        UNITS = HN * CPB
        w_raw = sb("w_raw", [P, KT, W])
        w_hi, w_lo = sb("w_hi", [P, KT, W], F32R), sb("w_lo", [P, KT, W], F32R)
        bias = sb("bias", [P, 2 * KT])
        bv, bo = sb("bv", [P, DM]), sb("bo", [P, DM])
        wo = sb("wo", [P, KT, DM])
        full = sb("full", [P, 2 * KT, SEQ])
        qk_hi, qk_lo = sb("qk_hi", [P, 2 * KT, SEQ], F32R), sb("qk_lo", [P, 2 * KT, SEQ], F32R)
        k_hi, k_lo = sb("k_hi", [P, 4, SEQ], F32R), sb("k_lo", [P, 4, SEQ], F32R)
        vp = sb("vp", [P, CPB, HN, 32])
        sv = sb("sv", [P, CPB, DM])
        pe_ = sb("pe_", [P, 4, SEQ])
        pt_ = sb("pt_", [P, 2, GROUP, CPB, SEQ])
        mx = sb("mx", [P, CPB, HN])
        nm = sb("nm", [P, CPB, HN])
        rs = sb("rs", [P, CPB, HN])
        em = sb("em", [P, CPB, HN])
        den = sb("den", [P, CPB, HN])
        pvs = sb("pvs", [P, 2, SEQ])
        o = sb("o", [P, CPB, DM])
        ot = full[:, 0:KT, :]
        sc = [ctx.enter_context(nc.psum_tensor(f"at_sc{i}", [P, SEQ], F32)) for i in range(4)]
        tp = [ctx.enter_context(nc.psum_tensor(f"at_tp{i}", [P, SEQ], F32)) for i in range(2)]
        pv = ctx.enter_context(nc.psum_tensor("at_pv", [P, SEQ], F32))
        px = ctx.enter_context(nc.psum_tensor("at_px", [P, SEQ], F32))
        names = ("w_in prm_in w_hi_done w_lo_done bias_done pad_done qk_done full_done qk_hi_done qk_lo_done "
                 "v_done vp_done sv_done svs_done k_masked score_done max_done nm_done exp_done tp_done pt_act pt_dve "
                 "pv_done pvs_done px_done em_in em_done den_done o_step ot_ready ot_act ot_dve proj_done s1_done")
        (w_in, prm_in, w_hi_done, w_lo_done, bias_done, pad_done, qk_done, full_done, qk_hi_done, qk_lo_done,
         v_done, vp_done, sv_done, svs_done, k_masked, score_done, max_done, nm_done, exp_done, tp_done, pt_act, pt_dve,
         pv_done, pvs_done, px_done, em_in, em_done, den_done, o_step, ot_ready, ot_act, ot_dve, proj_done,
         s1_done) = map(sem, names.split())
        block = ctx.enter_context(nc.Block())
        def full_v(m):
            return pe_[:, m, :]

        LAG_T, LAG_PV, LAG_X = 3, 6, 8
        END = UNITS + LAG_X + 1

        @block.sync
        def _(sp):
            sp.dma_start(w_raw[:, :, :], w_dram.rearrange("(k p) n -> p k n", p=P)).then_inc(w_in, 16)
            sp.dma_start(bias[:, :], b_dram).then_inc(prm_in, 16)
            sp.dma_start(bv[:, :], bv_dram.broadcast_to([P, DM])).then_inc(prm_in, 16)
            sp.dma_start(bo[:, :], bo_dram.broadcast_to([P, DM])).then_inc(prm_in, 16)
            sp.dma_start(wo[:, :, :], wo_dram.rearrange("(k p) n -> p k n", p=P)).then_inc(prm_in, 16)

        @block.tensor
        def _(pe):
            pe.wait_ge(w_lo_done, 1)
            with pe.Fori(0, BATCH) as b:
                toks = bass.ds(b * SEQ, SEQ)
                for m in range(2 * KT):
                    c = slice(m * P, (m + 1) * P)
                    split_matmuls(pe, sc[m][:, :], [w_hi[:, j, c] for j in range(KT)], [w_lo[:, j, c] for j in range(KT)],
                                  [xt_hi[:, j, toks] for j in range(KT)], [xt_lo[:, j, toks] for j in range(KT)])\
                        .then_inc(qk_done, 1)
                for m in range(KT):
                    c = slice((2 * KT + m) * P, (2 * KT + m + 1) * P)
                    split_matmuls(pe, tp[m][:, :], [w_hi[:, j, c] for j in range(KT)], [w_lo[:, j, c] for j in range(KT)],
                                  [xt_hi[:, j, toks] for j in range(KT)], [xt_lo[:, j, toks] for j in range(KT)])\
                        .then_inc(qk_done, 1)
                for m in range(KT):
                    pe.wait_ge(v_done, 2 * b + m + 1)
                    for t in range(CPB):
                        last = pe.transpose((pv, px)[m][:, t * P:(t + 1) * P], full_v(m)[:, t * P:(t + 1) * P], ident[:, :])
                    last.then_inc(qk_done, 1)
                pe.wait_ge(vp_done, 2 * b + 2)
                pe.wait_ge(full_done, 4 * b + 4)
                for i in range(CPB):
                    for j in range(i, CPB):
                        last = pe.matmul(sc[i][:, 0:DM], (later if j == i else ones)[:, :], vp[:, j, :, 0:HW],
                                         start=(j == i), stop=(j == CPB - 1))
                last.then_inc(sv_done, 1)
                pe.wait_ge(qk_lo_done, 4 * b + 4)
                pe.wait_ge(svs_done, b + 1)

                def scores(u):
                    h, i = divmod(u, CPB)
                    g = h // 8
                    pe.wait_ge(k_masked, b * HN + h + 1)
                    if u >= 4:
                        pe.wait_ge(exp_done, b * UNITS + u - 3)
                    n = (i + 1) * P
                    out, t = sc[u % 4][:, 0:n], slice(i * P, (i + 1) * P)
                    pe.matmul(sc[u % 4][:, i * P:n], ident_b[:, :], block_b[:, :], start=True, stop=False,
                              skip_group_check=True)
                    split_matmuls(pe, out, [qk_hi[:, g, t]], [qk_lo[:, g, t]], [k_hi[:, h % 4, 0:n]], [k_lo[:, h % 4, 0:n]],
                                  seeded=True).then_inc(score_done, 1)

                def transposes(u):
                    h, i = divmod(u, CPB)
                    pe.wait_ge(exp_done, b * UNITS + u + 1)
                    if i < 2 and h:
                        pe.wait_ge(pt_act, b * UNITS // 2 + 2 * h + i - 1)
                    if i >= 2:
                        pe.wait_ge(pt_dve, b * UNITS // 2 + 2 * h + i - 1)
                    for j in range(i + 1):
                        last = pe.transpose(tp[u % 2][:, j * P:(j + 1) * P], pe_[:, u % 4, j * P:(j + 1) * P], ident[:, :])
                    last.then_inc(tp_done, 1)

                def products(g):
                    pe.wait_ge(pt_act, b * UNITS // 2 + 2 * GROUP * (g + 1))
                    pe.wait_ge(pt_dve, b * UNITS // 2 + 2 * GROUP * (g + 1))
                    if g:
                        pe.wait_ge(pvs_done, b * GROUPS + g)
                    for j in range(CPB):
                        for q in range(GROUP):
                            last = pe.matmul(pv[32 * q:32 * q + 32, j * P:SEQ], vp[:, j, GROUP * g + q, :],
                                             pt_[:, g % 2, q, j, j * P:SEQ], start=(j == 0), stop=(j == CPB - 1))
                    last.then_inc(pv_done, 1)

                def turn_back(g):
                    pe.wait_ge(pvs_done, b * GROUPS + g + 1)
                    if g:
                        pe.wait_ge(o_step, 3 * (b * GROUPS + g - 1) + 2)
                    for i in range(CPB):
                        last = pe.transpose(px[:, i * P:(i + 1) * P], pvs[:, g % 2, i * P:(i + 1) * P], ident[:, :])
                    last.then_inc(px_done, 1)

                for n in range(END):
                    if n < UNITS:
                        scores(n)
                    if 0 <= n - LAG_T < UNITS:
                        transposes(n - LAG_T)
                    g, r = divmod(n - LAG_PV + 1, GROUP * CPB)
                    if r == 0 and 0 < g <= GROUPS:
                        products(g - 1)
                    g, r = divmod(n - LAG_X + 1, GROUP * CPB)
                    if r == 0 and 0 < g <= GROUPS:
                        turn_back(g - 1)
                pe.wait_ge(o_step, 3 * (b * GROUPS + GROUPS))
                for k in range(KT):
                    for i in range(CPB):
                        last = pe.transpose(sc[k][:, i * P:(i + 1) * P], o[:, i, k * P:(k + 1) * P], ident[:, :])
                    last.then_inc(ot_ready, 1)
                pe.wait_ge(ot_act, b + 1)
                pe.wait_ge(ot_dve, b + 1)
                for i in range(CPB):
                    for k in range(KT):
                        last = pe.matmul((sc[2], sc[3], tp[0], tp[1])[i][:, 0:DM],
                                         ot[:, k, i * P:(i + 1) * P], wo[:, k, :], start=(k == 0), stop=(k == KT - 1))
                last.then_inc(proj_done, 1)
                pe.wait_ge(s1_done, b + 1)

        def p_tile(u):
            h, i = divmod(u, CPB)
            return (pt_[:, h // GROUP % 2, h % GROUP, 0:i + 1, i * P:(i + 1) * P],
                    tp[u % 2][:, 0:(i + 1) * P].rearrange("p (j t) -> p j t", t=P))

        @block.scalar
        def _(act):
            act.wait_ge(w_in, 16)
            act.activation(w_hi[:, :, :], w_raw[:, :, :], ACT.Copy).then_inc(w_hi_done, 1)
            act.wait_ge(bias_done, 1)
            with act.Fori(0, BATCH) as b:
                for m in range(2 * KT):
                    act.wait_ge(qk_done, b * 4 * KT + m + 1)
                    act.activation(full[:, m, :], sc[m][:, :], ACT.Identity, bias=bias[:, m:m + 1],
                                   scale=0.25 if m < KT else 1.0).then_inc(full_done, 1)
                for m in range(KT):
                    act.wait_ge(qk_done, b * 4 * KT + 2 * KT + m + 1)
                    act.activation(full_v(m), tp[m][:, :], ACT.Copy).then_inc(v_done, 1)
                for m in range(2 * KT):
                    act.wait_ge(full_done, b * 2 * KT + m + 1)
                    act.activation(qk_hi[:, m, :], full[:, m, :], ACT.Copy).then_inc(qk_hi_done, 1)
                act.wait_ge(sv_done, b + 1)
                for i in range(CPB):
                    last = act.activation(sv[:, i, :], sc[i][:, 0:DM], ACT.Copy)
                last.then_inc(svs_done, 1)

                def exps(u):
                    h, i = divmod(u, CPB)
                    act.wait_ge(nm_done, b * UNITS + u + 1)
                    if u >= 4:
                        act.wait_ge(tp_done, b * UNITS + u - 3)
                    n = (i + 1) * P
                    act.activation(pe_[:, u % 4, 0:n], sc[u % 4][:, 0:n], ACT.Exp, bias=nm[:, i, h:h + 1],
                                   accum_out=rs[:, i, h:h + 1]).then_inc(exp_done, 1)

                def evacuate(u):
                    h, i = divmod(u, CPB)
                    if i >= 2:
                        act.wait_ge(tp_done, b * UNITS + u + 1)
                        if h >= 2 * GROUP and h % GROUP == 0:
                            act.wait_ge(pv_done, b * GROUPS + h // GROUP - 1)
                        act.activation(*p_tile(u), ACT.Copy).then_inc(pt_act, 1)

                def mask_shares(g):
                    act.wait_ge(em_in, b * GROUPS + g + 1)
                    hs = slice(g * GROUP, (g + 1) * GROUP)
                    act.activation(em[:, :, hs], em[:, :, hs], ACT.Exp).then_inc(em_done, 1)

                for n in range(END):
                    if n < UNITS:
                        exps(n)
                    if 0 <= n - LAG_T < UNITS:
                        evacuate(n - LAG_T)
                    g, r = divmod(n - LAG_PV + 1, GROUP * CPB)
                    if r == 0 and 0 < g <= GROUPS:
                        mask_shares(g - 1)
                        act.wait_ge(pv_done, b * GROUPS + g)
                        if g >= 3:
                            act.wait_ge(px_done, b * GROUPS + g - 2)
                        act.activation(pvs[:, (g - 1) % 2, :], pv[:, :], ACT.Copy).then_inc(pvs_done, 1)
                act.wait_ge(ot_ready, 2 * b + 1)
                act.activation(ot[:, 0, :], sc[0][:, :], ACT.Copy).then_inc(ot_act, 1)

        @block.vector
        def _(dve):
            dve.memset(vp[:, :, :, :], 0.0).then_inc(pad_done, 1)
            dve.wait_ge(w_hi_done, 1)
            dve.tensor_tensor(w_lo[:, :, :], w_raw[:, :, :], w_hi[:, :, :].bitcast(F32), ALU.subtract).then_inc(w_lo_done, 1)
            dve.wait_ge(prm_in, 64)
            dve.tensor_scalar(bias[:, 0:KT], bias[:, 0:KT], 0.25, None, ALU.mult).then_inc(bias_done, 1)
            dve.wait_ge(pad_done, 1)
            with dve.Fori(0, BATCH) as b:
                for m in range(KT):
                    dve.wait_ge(qk_done, b * 4 * KT + 3 * KT + m + 1)
                    hs = slice(m * HN // 2, (m + 1) * HN // 2)
                    dve.tensor_tensor(vp[:, :, hs, 0:HW],
                                      (pv, px)[m][:, :].rearrange("p (t h d) -> p t h d", t=CPB, d=HW),
                                      bv[:, m * P:(m + 1) * P].rearrange("p (h d) -> p h d", d=HW).unsqueeze(1)
                                      .broadcast_to([P, CPB, HN // 2, HW]), ALU.add).then_inc(vp_done, 1)
                for m in range(2 * KT):
                    dve.wait_ge(qk_hi_done, b * 2 * KT + m + 1)
                    dve.tensor_tensor(qk_lo[:, m, :], full[:, m, :], qk_hi[:, m, :].bitcast(F32), ALU.subtract)\
                       .then_inc(qk_lo_done, 1)
                dve.wait_ge(qk_lo_done, b * 2 * KT + 2 * KT)

                def mask_k(h):
                    if h >= 4:
                        dve.wait_ge(score_done, b * UNITS + (h - 3) * CPB)
                    m, col = KT + h // 8, head_mask[:, h % 8:h % 8 + 1]
                    for dst, src in ((k_hi, qk_hi), (k_lo, qk_lo)):
                        last = dve.tensor_scalar(dst[:, h % 4, :], src[:, m, :].bitcast(F32), col, None, ALU.mult)
                    last.then_inc(k_masked, 1)

                def maxima(u):
                    h, i = divmod(u, CPB)
                    dve.wait_ge(score_done, b * UNITS + u + 1)
                    dve.reduce_max(mx[:, i, h:h + 1], sc[u % 4][:, 0:(i + 1) * P], AX.X).then_inc(max_done, 1)
                    dve.wait_ge(max_done, b * UNITS + u + 1)
                    dve.scalar_tensor_tensor(nm[:, i, h:h + 1], mx[:, i, h:h + 1], -1.0, floor[:, i:i + 1],
                                             ALU.mult, ALU.min).then_inc(nm_done, 1)

                def evacuate(u):
                    h, i = divmod(u, CPB)
                    if i < 2:
                        dve.wait_ge(tp_done, b * UNITS + u + 1)
                        if h >= 2 * GROUP and h % GROUP == 0:
                            dve.wait_ge(pv_done, b * GROUPS + h // GROUP - 1)
                        dve.tensor_copy(*p_tile(u)).then_inc(pt_dve, 1)

                def shares_in(g):
                    hs = slice(g * GROUP, (g + 1) * GROUP)
                    dve.wait_ge(nm_done, b * UNITS + (g + 1) * GROUP * CPB)
                    dve.tensor_scalar(em[:, :, hs], nm[:, :, hs], MASK_SCORE, MASK_SCORE, ALU.min, ALU.subtract)\
                       .then_inc(em_in, 1)

                def combine(g):
                    n = b * GROUPS + g
                    hs = slice(g * GROUP, (g + 1) * GROUP)
                    cols = slice(g * GROUP * HW, (g + 1) * GROUP * HW)
                    quad = [P, CPB, GROUP, HW]
                    dve.wait_ge(em_done, n + 1)
                    dve.tensor_tensor(den[:, :, hs], em[:, :, hs], count[:, :].unsqueeze(2).broadcast_to([P, CPB, GROUP]),
                                      ALU.mult).then_inc(den_done, 1)
                    ov = o[:, :, cols].rearrange("p i (h d) -> p i h d", d=HW)
                    dve.tensor_tensor(ov, sv[:, :, cols].rearrange("p i (h d) -> p i h d", d=HW),
                                      em[:, :, hs].unsqueeze(3).broadcast_to(quad), ALU.mult).then_inc(o_step, 1)
                    dve.wait_ge(den_done, 3 * n + 1)
                    dve.tensor_tensor(den[:, :, hs], den[:, :, hs], rs[:, :, hs], ALU.add).then_inc(den_done, 1)
                    dve.wait_ge(px_done, n + 1)
                    dve.wait_ge(o_step, 3 * n + 1)
                    dve.tensor_tensor(ov, px[:, :].rearrange("p (i h d) -> p i h d", i=CPB, h=GROUP)[:, :, :, 0:HW],
                                      ov, ALU.add).then_inc(o_step, 1)
                    dve.wait_ge(den_done, 3 * n + 2)
                    dve.reciprocal(den[:, :, hs], den[:, :, hs]).then_inc(den_done, 1)
                    dve.wait_ge(den_done, 3 * n + 3)
                    dve.wait_ge(o_step, 3 * n + 2)
                    dve.tensor_tensor(ov, ov, den[:, :, hs].unsqueeze(3).broadcast_to(quad), ALU.mult).then_inc(o_step, 1)

                mask_k(0)
                mask_k(1)
                for n in range(END):
                    if n % CPB == 0 and n // CPB + 2 < HN:
                        mask_k(n // CPB + 2)
                    if n < UNITS:
                        maxima(n)
                    if 0 <= n - LAG_T < UNITS:
                        evacuate(n - LAG_T)
                    g, r = divmod(n + 1, GROUP * CPB)
                    if r == 0 and 0 < g <= GROUPS:
                        shares_in(g - 1)
                    g, r = divmod(n - LAG_X + 1, GROUP * CPB)
                    if r == 0 and 0 < g <= GROUPS:
                        combine(g - 1)
                dve.wait_ge(ot_ready, 2 * b + 2)
                dve.tensor_copy(ot[:, 1, :], sc[1][:, :]).then_inc(ot_dve, 1)
                dve.wait_ge(proj_done, b + 1)
                for i in range(CPB):
                    last = dve.tensor_tensor(s1[:, bass.ds(b * CPB + i, 1), :], (sc[2], sc[3], tp[0], tp[1])[i][:, 0:DM].unsqueeze(1),
                                             bo[:, :].unsqueeze(1), ALU.add)
                last.then_inc(s1_done, 1)


EXPERTS, TOPK, FW = 32, 4, 96
INTER = 1024


def router_phase(nc, xt_hi, xt_lo, wg_dram, ident, wt_dram):
    with ExitStack() as ctx:
        sb = lambda n, s, d=F32: ctx.enter_context(nc.sbuf_tensor(f"ro_{n}", s, d))
        sem = ctx.enter_context(phase_semaphores(nc, "ro"))
        wr = sb("wr", [P, KT, EXPERTS])
        w_hi, w_lo = sb("w_hi", [P, KT, EXPERTS], F32R), sb("w_lo", [P, KT, EXPERTS], F32R)
        full = [P, NT, EXPERTS]
        l, gt, eq, pre = sb("l", full), sb("gt", full), sb("eq", full), sb("pre", full)
        keep = sb("keep", full)
        m8 = sb("m8", [P, NT, 8])
        m, s, need = sb("m", [P, NT]), sb("s", [P, NT]), sb("need", [P, NT])
        wt = sb("wt", [EXPERTS, T])
        pl = ctx.enter_context(nc.psum_tensor("ro_pl", full, F32))
        pw = [ctx.enter_context(nc.psum_tensor(f"ro_pw{i}", [EXPERTS, SEQ], F32)) for i in range(4)]
        bc = lambda ap: ap.unsqueeze(2).broadcast_to([P, NT, EXPERTS])
        STEP_WT = 19
        w_in, w_hi_done, w_lo_done, logits, step, max_done, exp_done, keep_done, turned, wt_done, stored = map(
            sem, "w_in w_hi_done w_lo_done logits step max_done exp_done keep_done turned wt_done stored".split())
        block = ctx.enter_context(nc.Block())

        @block.sync
        def _(sp):
            sp.dma_start(wr[:, :, :], wg_dram.rearrange("(k p) n -> p k n", p=P)).then_inc(w_in, 16)
            sp.wait_ge(wt_done, 4)
            sp.dma_start(wt_dram, wt[:, :]).then_inc(stored, 16)
            sp.wait_ge(stored, 16)

        @block.gpsimd
        def _(pool):
            pool.memset(keep[:, :, :], 1.0).then_inc(keep_done, 1)
            pool.wait_ge(keep_done, 1)
            pool.memset(keep[:, :, 0:1], 0.0).then_inc(keep_done, 1)

        @block.tensor
        def _(pe):
            pe.wait_ge(w_lo_done, 1)
            for t in range(NT):
                ts = slice(t * P, (t + 1) * P)
                last = split_matmuls(pe, pl[:, t, :], [xt_hi[:, k, ts] for k in range(KT)], [xt_lo[:, k, ts] for k in range(KT)],
                                     [w_hi[:, k, :] for k in range(KT)], [w_lo[:, k, :] for k in range(KT)])
            last.then_inc(logits, 1)
            pe.wait_ge(step, STEP_WT)
            for t in range(NT):
                last = pe.transpose(pw[t // 4][:, (t % 4) * P:(t % 4 + 1) * P], l[:, t, :], ident[:, :])
                if t % 4 == 3:
                    last.then_inc(turned, 1)

        @block.scalar
        def _(act):
            act.wait_ge(w_in, 16)
            act.activation(w_hi[:, :, :], wr[:, :, :], ACT.Copy).then_inc(w_hi_done, 1)
            act.wait_ge(step, 2)
            act.activation(l[:, :, :], l[:, :, :], ACT.Exp).then_inc(exp_done, 1)
            for q in range(4):
                act.wait_ge(turned, q + 1)
                act.activation(wt[:, q * SEQ:(q + 1) * SEQ], pw[q][:, :], ACT.Copy).then_inc(wt_done, 1)

        @block.vector
        def _(dve):
            n = [0]

            def then(ins):
                n[0] += 1
                ins.then_inc(step, 1)
                dve.wait_ge(step, n[0])

            dve.wait_ge(w_hi_done, 1)
            dve.tensor_tensor(w_lo[:, :, :], wr[:, :, :], w_hi[:, :, :].bitcast(F32), ALU.subtract).then_inc(w_lo_done, 1)
            dve.wait_ge(logits, 1)
            then(dve.reduce_max(m[:, :], pl[:, :, :], AX.X))
            then(dve.tensor_tensor(l[:, :, :], pl[:, :, :], bc(m[:, :]), ALU.subtract))
            dve.wait_ge(exp_done, 1)
            then(dve.reduce_sum(s[:, :], l[:, :, :], AX.X))
            then(dve.reciprocal(s[:, :], s[:, :]))
            then(dve.tensor_tensor(l[:, :, :], l[:, :, :], bc(s[:, :]), ALU.mult))
            for t in range(NT):
                last = dve.max(m8[:, t, :], l[:, t, :])
            then(last)
            fourth = m8[:, :, TOPK - 1]
            then(dve.tensor_copy(m[:, :], fourth))
            then(dve.tensor_tensor(gt[:, :, :], l[:, :, :], bc(m[:, :]), ALU.is_gt))
            then(dve.tensor_tensor(eq[:, :, :], l[:, :, :], bc(m[:, :]), ALU.is_equal))
            then(dve.reduce_sum(need[:, :], gt[:, :, :], AX.X))
            then(dve.tensor_scalar(need[:, :], need[:, :], -1.0, float(TOPK), ALU.mult, ALU.add))
            dve.wait_ge(keep_done, 2)
            flat = lambda ap: ap[:, :, :].rearrange("p t e -> p (t e)")
            then(dve.tensor_tensor_scan(flat(pre), flat(keep), flat(eq), 0.0, ALU.mult, ALU.add))
            then(dve.tensor_tensor(pre[:, :, :], pre[:, :, :], bc(need[:, :]), ALU.is_le))
            then(dve.tensor_tensor(eq[:, :, :], eq[:, :, :], pre[:, :, :], ALU.mult))
            then(dve.tensor_tensor(gt[:, :, :], gt[:, :, :], eq[:, :, :], ALU.add))
            then(dve.tensor_tensor(l[:, :, :], l[:, :, :], gt[:, :, :], ALU.mult))
            then(dve.reduce_sum(s[:, :], l[:, :, :], AX.X))
            then(dve.reciprocal(s[:, :], s[:, :]))
            then(dve.tensor_tensor(l[:, :, :], l[:, :, :], bc(s[:, :]), ALU.mult))
            assert n[0] == STEP_WT


def output_phase(nc, x1_dram, gate_dram, s1, out_dram):
    with ExitStack() as ctx:
        sb = lambda n, s, d=F32: ctx.enter_context(nc.sbuf_tensor(f"out_{n}", s, d))
        sem = ctx.enter_context(phase_semaphores(nc, "out"))
        x, g = sb("x", [P, NT, DM]), sb("g", [P, NT, DM])
        x_in, g_in = [sem(f"x_in{q}") for q in range(4)], [sem(f"g_in{q}") for q in range(4)]
        scaled, added, stored = map(sem, "scaled added stored".split())
        block = ctx.enter_context(nc.Block())
        tiles = lambda d: d.rearrange("(t p) d -> p t d", p=P)

        @block.sync
        def _(sp):
            for q in range(4):
                t = slice(q * CPB, (q + 1) * CPB)
                sp.dma_start(g[:, t, :], tiles(gate_dram)[:, t, :]).then_inc(g_in[q], 16)
                sp.dma_start(x[:, t, :], tiles(x1_dram)[:, t, :]).then_inc(x_in[q], 16)
            for q in range(4):
                t = slice(q * CPB, (q + 1) * CPB)
                sp.wait_ge(added, q + 1)
                sp.dma_start(tiles(out_dram)[:, t, :], x[:, t, :]).then_inc(stored, 16)
            sp.wait_ge(stored, 64)

        @block.vector
        def _(dve):
            for q in range(4):
                t = slice(q * CPB, (q + 1) * CPB)
                dve.wait_ge(g_in[q], 16)
                dve.tensor_tensor(g[:, t, :], s1[:, t, :], g[:, t, :], ALU.mult).then_inc(scaled, 1)
                dve.wait_ge(scaled, q + 1)
                dve.wait_ge(x_in[q], 16)
                dve.tensor_tensor(x[:, t, :], x[:, t, :], g[:, t, :], ALU.add).then_inc(added, 1)


def recurrent_layers(nc, x, w_xg, w_bcdt, conv_bc, dt_prm, prm, w_out, f0_gate, f0_up, f0_down,
                     w_qkv, b_qk, b_v, w_o, b_o, w_router, f1_gate, f1_up, f1_down, out):
    dram = lambda n, s: nc.dram_tensor(n, s, F32).ap()
    scratch = (dram("cum", [HEADS, T]), dram("ecum", [HEADS, T]), dram("last", [HEADS, NT]),
               dram("tables", [P, PAIRS * BATCH * 4 * CPB * 2]))
    gate0, gate1, x1, w_tok = dram("gate0", [T, DM]), dram("gate1", [T, DM]), dram("x1", [T, DM]), dram("w_tok", [EXPERTS, T])
    with ExitStack() as ctx:
        sb = lambda c, n, s, d=F32: c.enter_context(nc.sbuf_tensor(n, s, d))
        ident, causal = sb(ctx, "ident", [P, P]), sb(ctx, "causal", [P, P])
        xt_hi, xt_lo = sb(ctx, "xt_hi", [P, KT, T], F32R), sb(ctx, "xt_lo", [P, KT, T], F32R)
        constants_phase(nc, ident, causal)
        layernorm_phase(nc, "ln0", x, ident, xt_hi, xt_lo)
        gated_ffn_phase(nc, "ffn", INTER // P, f0_gate, f0_up, f0_down, xt_hi, xt_lo, gate0)
        with ExitStack() as mamba:
            out_acc, sq_acc = sb(mamba, "out_acc", [P, NT, DM]), sb(mamba, "sq_acc", [P, BATCH, SEQ])
            with ExitStack() as ssm:
                b_tok, c_t, cb_m = sb(ssm, "b_tok", [P, NT, NS]), sb(ssm, "c_t", [P, T]), sb(ssm, "cb_m", [P, NT, P])
                dynamics_phase(nc, xt_hi, xt_lo, w_bcdt, conv_bc, dt_prm, ident, causal, b_tok, c_t, cb_m, scratch)
                ssm_phase(nc, xt_hi, xt_lo, w_xg, w_out, prm, ident, b_tok, c_t, cb_m, scratch, out_acc, sq_acc)
            mamba_output_phase(nc, x, gate0, out_acc, sq_acc, x1)
        s1 = sb(ctx, "s1", [P, NT, DM])
        layernorm_phase(nc, "ln1", x1, ident, xt_hi, xt_lo)
        attention_phase(nc, xt_hi, xt_lo, w_qkv, b_qk, b_v, w_o, b_o, ident, s1)
        router_phase(nc, xt_hi, xt_lo, w_router, ident, w_tok)
        gated_ffn_phase(nc, "moe", EXPERTS * FW // P, f1_gate, f1_up, f1_down, xt_hi, xt_lo, gate1, router=(w_tok, FW))
        output_phase(nc, x1, gate1, s1, out)


def kernel(**inputs):
    import numpy as np
    import concourse.bacc as bacc
    from concourse.bass_utils import run_bass_kernel_spmd

    a = {n: np.asarray(v) for n, v in inputs.items()}
    w = a["L0_attn_in_proj_w"]
    conv = np.concatenate([a["L0_attn_conv_w"], a["L0_attn_conv_b"][:, None]], 1)
    xg = np.concatenate([w[:, DI:2 * DI].reshape(KT, P, PAIRS, P), w[:, :DI].reshape(KT, P, PAIRS, P)], 3)
    w_dt = w[:, 2 * DI + 2 * NS:]
    d_rows = np.repeat(a["L0_attn_D_param"], HD)[:, None]
    gu0, gu1 = a["L0_ffn_w_gate_up"], a["L1_ffn_gate_up_proj"]
    laid = {
        "x": a["L0_attn_hidden_states"].reshape(T, DM),
        "w_xg": xg.transpose(2, 1, 0, 3).reshape(PAIRS, P, KT * 2 * P),
        "w_bcdt": np.concatenate([w[:, 2 * DI:2 * DI + 2 * NS], w_dt, w_dt], 1),
        "conv_bc": conv[DI:],
        "dt_prm": np.stack([a["L0_attn_dt_bias"], a["L0_attn_A_log"]], 1),
        "prm": np.concatenate([conv[:DI], d_rows], 1).reshape(PAIRS, P, 6),
        "w_out": np.concatenate([a["L0_attn_out_proj_w"], a["L0_attn_norm_w"][:, None]], 1).reshape(PAIRS, P, DM + 1),
        "f0_gate": gu0[:INTER].T, "f0_up": gu0[INTER:].T, "f0_down": a["L0_ffn_w_down"].T,
        "w_qkv": a["L1_attn_Wqkv"],
        "b_qk": a["L1_attn_bqkv"][:2 * DM].reshape(2 * KT, P).T, "b_v": a["L1_attn_bqkv"][2 * DM:][None],
        "w_o": a["L1_attn_Wo"], "b_o": a["L1_attn_bo"][None],
        "w_router": a["L1_ffn_gate"],
        "f1_gate": gu1[:, :, :FW].transpose(1, 0, 2).reshape(DM, EXPERTS * FW),
        "f1_up": gu1[:, :, FW:].transpose(1, 0, 2).reshape(DM, EXPERTS * FW),
        "f1_down": a["L1_ffn_down_proj"].reshape(EXPERTS * FW, DM),
    }
    nc = bacc.Bacc("TRN2", target_bir_lowering=False, num_devices=1)
    arrays, args = {}, []
    for name, v in laid.items():
        v = np.ascontiguousarray(v)
        arrays[f"in_{name}"] = v
        args.append(nc.dram_tensor(f"in_{name}", v.shape, mybir.dt.from_np(v.dtype), kind="ExternalInput").ap())
    args.append(nc.dram_tensor("result", (T, DM), F32, kind="ExternalOutput").ap())
    recurrent_layers(nc, *args)
    r = run_bass_kernel_spmd(nc, [arrays], core_ids=[0])
    return r.results[0]["result"].reshape(BATCH, SEQ, DM)
```

```python
import concourse.bass as bass
from concourse import mybir
from contextlib import ExitStack, contextmanager

F32 = mybir.dt.float32
F32R = mybir.dt.float32r
ALU = mybir.AluOpType
ACT = mybir.ActivationFunctionType
AX = mybir.AxisListType

P = 128
BATCH, SEQ, DM = 4, 512, 256
T = BATCH * SEQ
NT = T // P
KT = DM // P
CPB = SEQ // P
HEADS, HD, NS = 64, 64, 128
DI = HEADS * HD
PAIRS = HEADS // 2
DUOS = PAIRS // 2
UNITS = 2 * BATCH
EPS = 1e-5
MASKED = -3.0e38


@contextmanager
def phase_semaphores(nc, tag):
    taken = []

    def sem(name):
        taken.append(nc.alloc_semaphore(f"{tag}_{name}"))
        return taken[-1]
    yield sem
    nc.clear_and_free_semaphores(taken)
    nc.all_engine_barrier()


def split_matmuls(pe, out, w_hi, w_lo, x_hi, x_lo, seeded=False, more=False):
    n = len(w_hi)
    part = seeded or more
    for k in range(n):
        pe.matmul(out, w_hi[k], x_hi[k], start=(k == 0 and not seeded), stop=False, skip_group_check=part)
        pe.matmul(out, w_hi[k], x_lo[k], start=False, stop=False, skip_group_check=part)
        last = pe.matmul(out, w_lo[k], x_hi[k], start=False, stop=(k == n - 1 and not more), skip_group_check=part)
    return last


def layernorm_phase(nc, tag, x_dram, ident, xt_hi, xt_lo):
    G = 4
    PAIRT = NT // 2
    with ExitStack() as ctx:
        sb = lambda n, s, d=F32: ctx.enter_context(nc.sbuf_tensor(f"{tag}_{n}", s, d))
        sem = ctx.enter_context(phase_semaphores(nc, tag))
        x = sb("x", [P, NT, DM])
        xn = sb("xn", [P, NT, DM])
        stats = sb("stats", [P, NT, 6])
        mv = sb("mv", [P, NT, 2])
        veps = sb("veps", [P, NT])
        std = sb("std", [P, NT])
        rstd = sb("rstd", [P, NT])
        pt = ctx.enter_context(nc.psum_tensor(f"{tag}_pt", [P, 2, KT, 2 * P], F32))
        x_in = [sem(f"x_in{g}") for g in range(NT // G)]
        stats_done, veps_done, std_done = sem("stats_done"), sem("veps_done"), sem("std_done")
        xn_done, transposed, hi_done, lo_done = sem("xn_done"), sem("transposed"), sem("hi_done"), sem("lo_done")
        block = ctx.enter_context(nc.Block())
        xv = x_dram.rearrange("(t p) d -> p t d", p=P)

        @block.sync
        def _(sp):
            for g in range(NT // G):
                sp.dma_start(x[:, g * G:(g + 1) * G, :], xv[:, g * G:(g + 1) * G, :]).then_inc(x_in[g], 16)

        @block.vector
        def _(dve):
            for t in range(NT):
                if t % G == 0:
                    dve.wait_ge(x_in[t // G], 16)
                dve.bn_stats(stats[:, t, :], x[:, t, :]).then_inc(stats_done, 1)
            dve.wait_ge(stats_done, NT)
            for t in range(NT):
                dve.bn_aggr(mv[:, t, :], stats[:, t, :]).then_inc(stats_done, 1)
            dve.wait_ge(stats_done, 2 * NT)
            dve.tensor_scalar(veps[:, :], mv[:, :, 1], EPS, None, ALU.add).then_inc(veps_done, 1)
            dve.wait_ge(std_done, 1)
            dve.reciprocal(rstd[:, :], std[:, :]).then_inc(veps_done, 1)
            dve.wait_ge(veps_done, 2)

            def low_part(g):
                dve.wait_ge(hi_done, g + 1)
                dve.tensor_tensor(xt_lo[:, :, g * 2 * P:(g + 1) * 2 * P], pt[:, g % 2, :, :],
                                  xt_hi[:, :, g * 2 * P:(g + 1) * 2 * P].bitcast(F32),
                                  ALU.subtract).then_inc(lo_done, 1)

            for g in range(PAIRT):
                for t in (2 * g, 2 * g + 1):
                    dve.tensor_scalar(xn[:, t, :], x[:, t, :], mv[:, t, 0:1], rstd[:, t:t + 1],
                                      ALU.subtract, ALU.mult).then_inc(xn_done, 1)
                if g:
                    low_part(g - 1)
            low_part(PAIRT - 1)

        @block.tensor
        def _(pe):
            for g in range(PAIRT):
                pe.wait_ge(xn_done, 2 * g + 2)
                if g >= 2:
                    pe.wait_ge(lo_done, g - 1)
                for k in range(KT):
                    for t in range(2):
                        last = pe.transpose(pt[:, g % 2, k, t * P:(t + 1) * P],
                                            xn[:, 2 * g + t, k * P:(k + 1) * P], ident[:, :])
                last.then_inc(transposed, 1)

        @block.scalar
        def _(act):
            act.wait_ge(veps_done, 1)
            act.activation(std[:, :], veps[:, :], ACT.Sqrt).then_inc(std_done, 1)
            for g in range(PAIRT):
                act.wait_ge(transposed, g + 1)
                act.activation(xt_hi[:, :, g * 2 * P:(g + 1) * 2 * P], pt[:, g % 2, :, :],
                               ACT.Copy).then_inc(hi_done, 1)


def gated_ffn_phase(nc, tag, mt, wg_dram, wu_dram, wd_dram, xt_hi, xt_lo, gate_out, router=None, residual=None):
    with ExitStack() as ctx:
        sb = lambda n, s, d=F32: ctx.enter_context(nc.sbuf_tensor(f"{tag}_{n}", s, d))
        sem = ctx.enter_context(phase_semaphores(nc, tag))
        CH = 512
        TILES = CH // P
        w_hi = sb("w_hi", [P, 2 * KT, mt * P], F32R)
        w_lo = sb("w_lo", [P, 2 * KT, mt * P], F32R)
        wd_hi = sb("wd_hi", [P, mt, DM], F32R)
        wd_lo = sb("wd_lo", [P, mt, DM], F32R)
        RAW = 3
        w_raw = sb("w_raw", [P, RAW, CH])
        h = sb("h", [P, 2, SEQ])
        h_hi = sb("h_hi", [P, 2, SEQ], F32R)
        h_lo = sb("h_lo", [P, 2, SEQ], F32R)
        og = sb("og", [P, CPB, DM])
        wb = sb("wb", [P, 2, SEQ]) if router else None
        res = sb("res", [P, CPB, DM]) if residual else None
        pg = ctx.enter_context(nc.psum_tensor(f"{tag}_pg", [P, 2, SEQ], F32))
        pu = ctx.enter_context(nc.psum_tensor(f"{tag}_pu", [P, 2, SEQ], F32))
        po = ctx.enter_context(nc.psum_tensor(f"{tag}_po", [P, CPB, 512], F32))
        raw_in = [sem(f"raw_in{i}") for i in range(RAW)]
        w_hi_done, w_lo_done = sem("w_hi_done"), sem("w_lo_done")
        gate_ready, up_ready = sem("gate_ready"), sem("up_ready")
        silu_done = sem("silu_done")
        up_used = sem("up_used")
        h_ready = sem("h_ready") if router else up_used
        h_hi_done = sem("h_hi_done")
        h_lo_done = sem("h_lo_done")
        down_done = sem("down_done")
        out_used = sem("out_used")
        out_stored = sem("out_stored")
        wb_in = [sem(f"wb_in{i}") for i in range(2)] if router else None
        s_in, x_in, scaled, added = (sem(n) for n in ("s_in", "x_in", "scaled", "added"))
        block = ctx.enter_context(nc.Block())

        loads = []
        for c in range(mt // TILES):
            cols = slice(c * CH, (c + 1) * CH)
            for s in range(2):
                for k in range(KT):
                    i = s * KT + k
                    loads.append(((wg_dram, wu_dram)[s][k * P:(k + 1) * P, cols], w_hi[:, i, cols], w_lo[:, i, cols]))
            for m in range(c * TILES, (c + 1) * TILES, CH // DM):
                ms = slice(m, m + CH // DM)
                loads.append((wd_dram.rearrange("(m p) d -> p m d", p=P)[:, ms, :],
                              wd_hi[:, ms, :].rearrange("p m d -> p (m d)"), wd_lo[:, ms, :].rearrange("p m d -> p (m d)")))
        PER = len(loads) * TILES // mt
        batch_of = lambda dram, b: (dram.rearrange("(b t p) d -> b p t d", b=BATCH, p=P)[bass.ds(b, 1)]
                                    .rearrange("b p t d -> (b p) t d"))

        def due(m):
            c, q = divmod(m, TILES)
            return range(min(len(loads), PER * (c + 1) + -(-PER * q // TILES)),
                         min(len(loads), PER * (c + 1) + -(-PER * (q + 1) // TILES)))

        def pieces(m):
            width, r, out = router[1], m * P, []
            while r < (m + 1) * P:
                e = r // width
                end = min((e + 1) * width, (m + 1) * P)
                out.append((r - m * P, end - r, e))
                r = end
            return out

        arrived = [0, 0]
        wb_at = []
        for m in range(mt if router else 0):
            arrived[m % 2] += 16 * len(pieces(m))
            wb_at.append(arrived[m % 2])

        SCALE_AT, X_AT, ADD_AT, STORE_AT, S_AT = 0, 2, 4, 6, 8

        @block.sync
        def _(sp):
            def load(n):
                if n >= RAW:
                    sp.wait_ge(w_lo_done, n - RAW + 1)
                dst = w_raw[:, n % RAW, :]
                if n % PER >= 2 * KT:
                    dst = dst.rearrange("p (m d) -> p m d", d=DM)
                sp.dma_start(dst, loads[n][0]).then_inc(raw_in[n % RAW], 16)

            def router_weights(b, m):
                sp.wait_ge(h_ready, b * mt + m + 1)
                for r, n, e in pieces(m):
                    sp.dma_start(wb[r:r + n, m % 2, :], router[0][e:e + 1, bass.ds(b * SEQ, SEQ)].broadcast_to([n, SEQ]))\
                      .then_inc(wb_in[m % 2], 16)

            for n in range(PER):
                load(n)
            for m in range(mt):
                for n in due(m):
                    load(n)
                if router:
                    router_weights(0, m)
            if router:
                with sp.Fori(1, BATCH) as b:
                    for m in range(mt):
                        router_weights(b, m)

        @block.tensor
        def _(pe):
            pe.sem_inc(silu_done, 2)
            pe.sem_inc(up_used, 2)
            pe.sem_inc(down_done, 2)
            pe.sem_inc(h_lo_done, 2)
            pe.sem_inc(out_used, 1)
            if router:
                pe.sem_inc(h_ready, 2)

            def hidden(b, m):
                c = slice(m * P, (m + 1) * P)
                xs_hi = [xt_hi[:, k, bass.ds(b * SEQ, SEQ)] for k in range(KT)]
                xs_lo = [xt_lo[:, k, bass.ds(b * SEQ, SEQ)] for k in range(KT)]
                for s, (bank, used, ready) in enumerate(((pg, silu_done, gate_ready), (pu, up_used, up_ready))):
                    if isinstance(b, int) and m % TILES == 0:
                        pe.wait_ge(w_lo_done, PER * (m // TILES) + (s + 1) * KT)
                    pe.wait_ge(used, b * mt + m + 1)
                    split_matmuls(pe, bank[:, m % 2, :], [w_hi[:, s * KT + k, c] for k in range(KT)],
                                  [w_lo[:, s * KT + k, c] for k in range(KT)], xs_hi, xs_lo).then_inc(ready, 1)

            def down(b, m):
                if isinstance(b, int):
                    pe.wait_ge(w_lo_done, PER * (m // TILES) + 2 * KT + m % TILES * DM // CH + 1)
                pe.wait_ge(h_lo_done, b * mt + m + 3)
                if m == 0:
                    pe.wait_ge(out_used, b + 1)
                for t in range(CPB):
                    ts = slice(t * P, (t + 1) * P)
                    last = split_matmuls(pe, po[:, t, 0:DM], [h_hi[:, m % 2, ts]], [h_lo[:, m % 2, ts]],
                                         [wd_hi[:, m, :]], [wd_lo[:, m, :]], seeded=(m > 0), more=(m < mt - 1))
                last.then_inc(down_done, 1)

            def batch(b):
                for m in range(mt):
                    hidden(b, m)
                    if m:
                        down(b, m - 1)
                down(b, mt - 1)

            batch(0)
            with pe.Fori(1, BATCH) as b:
                batch(b)

        @block.scalar
        def _(act):
            def split_high(n):
                act.wait_ge(raw_in[n % RAW], 16 * (n // RAW + 1))
                act.activation(loads[n][1], w_raw[:, n % RAW, :], ACT.Copy).then_inc(w_hi_done, 1)

            def load_s(b):
                if not isinstance(b, int) or b > 0:
                    act.wait_ge(added, b)
                act.dma_start(res[:, :, :], batch_of(residual[1], b)).then_inc(s_in, 16)

            def load_x(b):
                act.wait_ge(scaled, b + 1)
                act.dma_start(res[:, :, :], batch_of(residual[0], b)).then_inc(x_in, 16)

            def store(b):
                act.wait_ge(added if residual else out_used, b + (1 if residual else 2))
                act.dma_start(batch_of(gate_out, b), og[:, :, :]).then_inc(out_stored, 16)

            def batch(b):
                for m in range(mt):
                    act.wait_ge(gate_ready, b * mt + m + 1)
                    act.wait_ge(h_lo_done, b * mt + m + 1)
                    act.activation(h[:, m % 2, :], pg[:, m % 2, :], ACT.Silu).then_inc(silu_done, 1)
                    act.wait_ge(h_ready, b * mt + m + 3)
                    act.wait_ge(down_done, b * mt + m + 1)
                    act.activation(h_hi[:, m % 2, :], h[:, m % 2, :], ACT.Copy).then_inc(h_hi_done, 1)
                    if isinstance(b, int):
                        for n in due(m):
                            split_high(n)
                    if residual:
                        if m == X_AT and not isinstance(b, int):
                            load_x(b - 1)
                        if m == STORE_AT and not isinstance(b, int):
                            store(b - 1)
                        if m == S_AT:
                            load_s(b)
                act.wait_ge(down_done, b * mt + mt + 2)
                act.wait_ge(out_stored, 16 * b + 16)
                act.activation(og[:, :, :], po[:, :, 0:DM], ACT.Silu).then_inc(out_used, 1)
                if not residual:
                    store(b)

            act.sem_inc(out_stored, 16)
            for n in range(PER):
                split_high(n)
            batch(0)
            with act.Fori(1, BATCH) as b:
                batch(b)
            if residual:
                load_x(BATCH - 1)
                store(BATCH - 1)
            act.wait_ge(out_stored, 16 * (BATCH + 1))

        @block.vector
        def _(dve):
            def split_low(n):
                dve.wait_ge(w_hi_done, n + 1)
                dve.tensor_tensor(loads[n][2], w_raw[:, n % RAW, :], loads[n][1].bitcast(F32), ALU.subtract)\
                   .then_inc(w_lo_done, 1)

            def scale(b):
                dve.wait_ge(out_used, b + 2)
                dve.wait_ge(s_in, 16 * (b + 1))
                dve.tensor_tensor(og[:, :, :], og[:, :, :], res[:, :, :], ALU.mult).then_inc(scaled, 1)

            def add(b):
                dve.wait_ge(scaled, b + 1)
                dve.wait_ge(x_in, 16 * (b + 1))
                dve.tensor_tensor(og[:, :, :], og[:, :, :], res[:, :, :], ALU.add).then_inc(added, 1)

            def batch(b):
                for m in range(mt):
                    dve.wait_ge(up_ready, b * mt + m + 1)
                    dve.wait_ge(silu_done, b * mt + m + 3)
                    dve.tensor_tensor(h[:, m % 2, :], pu[:, m % 2, :], h[:, m % 2, :], ALU.mult).then_inc(up_used, 1)
                    if router:
                        dve.wait_ge(up_used, b * mt + m + 3)
                        dve.wait_ge(wb_in[m % 2], b * arrived[m % 2] + wb_at[m])
                        dve.tensor_tensor(h[:, m % 2, :], h[:, m % 2, :], wb[:, m % 2, :], ALU.mult)\
                           .then_inc(h_ready, 1)
                    dve.wait_ge(h_hi_done, b * mt + m + 1)
                    dve.wait_ge(down_done, b * mt + m + 1)
                    dve.tensor_tensor(h_lo[:, m % 2, :], h[:, m % 2, :], h_hi[:, m % 2, :].bitcast(F32), ALU.subtract)\
                       .then_inc(h_lo_done, 1)
                    if isinstance(b, int):
                        for n in due(m):
                            split_low(n)
                    elif residual:
                        if m == SCALE_AT:
                            scale(b - 1)
                        if m == ADD_AT:
                            add(b - 1)

            for n in range(PER):
                split_low(n)
            batch(0)
            with dve.Fori(1, BATCH) as b:
                batch(b)
            if residual:
                scale(BATCH - 1)
                add(BATCH - 1)


def dynamics_phase(nc, xt_hi, xt_lo, w_bcdt, conv_bc, dt_prm, ident, causal, b_tok, c_t, cb_m, scratch):
    cum_d, ecum_d, last_d, tab_d = scratch
    with ExitStack() as ctx:
        sb = lambda n, s, d=F32: ctx.enter_context(nc.sbuf_tensor(f"dyn_{n}", s, d))
        sem = ctx.enter_context(phase_semaphores(nc, "dyn"))
        W = 3 * P
        w_raw = sb("w_raw", [P, KT, W])
        w_hi = sb("w_hi", [P, KT, W], F32R)
        w_lo = sb("w_lo", [P, KT, W], F32R)
        cp = sb("cp", [P, 2, 5])
        dp = sb("dp", [HEADS, 2])
        a_neg = sb("a_neg", [HEADS, 1])
        y = sb("y", [P, 2, SEQ])
        b_t = sb("b_t", [P, T])
        v = sb("v", [HEADS, T])
        av = sb("av", [HEADS, T])
        u = sb("u", [HEADS, T])
        z = sb("z", [HEADS, T])
        dt_t = sb("dt_t", [HEADS, T])
        keep = sb("keep", [HEADS, T])
        cum = sb("cum", [HEADS, T])
        ecum = sb("ecum", [HEADS, T])
        wst = sb("wst", [HEADS, T])
        last = sb("last", [HEADS, NT])
        last_b = sb("last_b", [P, HEADS, NT])
        tab = sb("tab", [P, PAIRS, BATCH, 4, CPB, 2])
        pp = [ctx.enter_context(nc.psum_tensor(f"dyn_pp{i}", [P, SEQ], F32)) for i in range(3)]
        pt = [ctx.enter_context(nc.psum_tensor(f"dyn_pt{i}", [P, SEQ], F32)) for i in range(4)]
        w_in, prm_in = sem("w_in"), sem("prm_in")
        whi, wlo, proj = sem("whi"), sem("wlo"), sem("proj")
        conv0, taps, bc_ready, v_ready = sem("conv0"), sem("taps"), sem("bc_ready"), sem("v_ready")
        scal, vec = sem("scal"), sem("vec")
        keep_done, tr, ev, cbd, cbe = sem("keep_done"), sem("tr"), sem("ev"), sem("cbd"), sem("cbe")
        out_c, last_in = sem("out_c"), sem("last_in")
        block = ctx.enter_context(nc.Block())
        chunks = lambda ap: ap.rearrange("p (c t) -> p c t", t=P)

        SC_AEXP, SC_ABS, SC_EXP, SC_LN, SC_ECUM, SC_WST, SC_LAST = range(1, 8)
        (VEC_ANEG, VEC_U, VEC_D, VEC_Z, VEC_NUM, VEC_DEN, VEC_REC, VEC_NUM2, VEC_Q, VEC_DT, VEC_DA,
         VEC_CUM, VEC_DIFF) = range(1, 14)

        @block.sync
        def _(sp):
            sp.dma_start(w_raw[:, :, :], w_bcdt.rearrange("(k p) n -> p k n", p=P)).then_inc(w_in, 16)
            sp.dma_start(cp[:, :, :], conv_bc.rearrange("(s p) n -> p s n", p=P)).then_inc(prm_in, 16)
            sp.dma_start(dp[:, :], dt_prm).then_inc(prm_in, 16)
            sp.wait_ge(vec, VEC_CUM)
            sp.dma_start(cum_d, cum[:, :]).then_inc(out_c, 16)
            sp.wait_ge(scal, SC_LAST)
            sp.dma_start(last_d, last[:, :]).then_inc(out_c, 16)
            sp.dma_start(ecum_d, ecum[:, :]).then_inc(out_c, 16)
            sp.wait_ge(out_c, 48)
            sp.dma_start(last_b[:, :, :].rearrange("p h c -> p (h c)"),
                         last_d.rearrange("(a h) c -> a (h c)", a=1).broadcast_to([P, HEADS * NT])).then_inc(last_in, 16)
            sp.wait_ge(ev, 4 * BATCH)
            sp.dma_start(tab_d, tab[:, :, :, :, :, :].rearrange("p k b f c e -> p (k b f c e)")).then_inc(out_c, 16)
            sp.wait_ge(out_c, 64)

        @block.gpsimd
        def _(pool):
            pool.memset(keep[:, :], 1.0).then_inc(keep_done, 1)
            pool.wait_ge(keep_done, 1)
            pool.memset(chunks(keep[:, :])[:, :, 0:1], 0.0).then_inc(keep_done, 1)

        @block.tensor
        def _(pe):
            pe.wait_ge(wlo, 1)
            for b in range(BATCH):
                xs = slice(b * SEQ, (b + 1) * SEQ)
                for s in range(3):
                    if b:
                        pe.wait_ge(*((taps, 3 * (2 * (b - 1) + s + 1)) if s < 2 else (v_ready, b)))
                    c = slice(s * P, (s + 1) * P)
                    split_matmuls(pe, pp[s][:, :], [w_hi[:, k, c] for k in range(KT)],
                                  [w_lo[:, k, c] for k in range(KT)], [xt_hi[:, k, xs] for k in range(KT)],
                                  [xt_lo[:, k, xs] for k in range(KT)]).then_inc(proj, 1)
            for b in range(BATCH):
                pe.wait_ge(bc_ready, 2 * b + 2)
                if b >= 2:
                    pe.wait_ge(cbe, 2 * (b - 1))
                for c in range(CPB):
                    t = slice((b * CPB + c) * P, (b * CPB + c + 1) * P)
                    m = pe.transpose(pt[b % 2][:, c * P:(c + 1) * P], b_t[:, t], ident[:, :])
                m.then_inc(cbd, 1)
                for c in range(CPB):
                    t = slice((b * CPB + c) * P, (b * CPB + c + 1) * P)
                    m = pe.matmul(pt[2 + b % 2][:, c * P:(c + 1) * P], b_t[:, t], c_t[:, t], start=True, stop=True)
                m.then_inc(cbd, 1)
            n = 0
            pe.wait_ge(cbe, 2 * BATCH)
            for f, (src, sm, at) in enumerate(((cum, vec, VEC_CUM), (dt_t, vec, VEC_DT), (wst, scal, SC_WST))):
                pe.wait_ge(sm, at)
                for b in range(BATCH):
                    if n >= 4:
                        pe.wait_ge(ev, n - 3)
                    for c in range(CPB):
                        t = slice((b * CPB + c) * P, (b * CPB + c + 1) * P)
                        m = pe.transpose(pt[n % 4][:, c * HEADS:(c + 1) * HEADS], src[:, t], ident[0:HEADS, 0:HEADS])
                    m.then_inc(tr, 1)
                    n += 1

        @block.scalar
        def _(act):
            act.wait_ge(w_in, 16)
            act.activation(w_hi[:, :, :], w_raw[:, :, :], ACT.Copy).then_inc(whi, 1)
            act.wait_ge(prm_in, 32)
            act.activation(a_neg[:, :], dp[:, 1:2], ACT.Exp).then_inc(scal, 1)

            def conv_silu(b, s):
                n = 2 * b + s
                act.wait_ge(taps, 3 * (n + 1))
                act.activation((b_t if s == 0 else c_t)[:, b * SEQ:(b + 1) * SEQ], y[:, s, :], ACT.Silu)\
                   .then_inc(bc_ready, 1)

            for b in range(BATCH):
                for s in range(2):
                    act.wait_ge(proj, 3 * b + s + 1)
                    if b:
                        act.wait_ge(bc_ready, 2 * (b - 1) + s + 1)
                    act.activation(y[:, s, :], pp[s][:, :], ACT.Identity, bias=cp[:, s, 4:5], scale=cp[:, s, 3:4])\
                       .then_inc(conv0, 1)
                act.wait_ge(proj, 3 * b + 3)
                act.activation(v[:, b * SEQ:(b + 1) * SEQ], pp[2][0:HEADS, :], ACT.Identity, bias=dp[:, 0:1])\
                   .then_inc(v_ready, 1)
                conv_silu(b, 0)
                conv_silu(b, 1)
            act.wait_ge(v_ready, BATCH)
            act.activation(av[:, :], v[:, :], ACT.Abs).then_inc(scal, 1)
            act.wait_ge(scal, SC_ABS)
            act.activation(av[:, :], av[:, :], ACT.Exp, scale=-1.0).then_inc(scal, 1)
            act.wait_ge(vec, VEC_U)
            act.activation(z[:, :], u[:, :], ACT.Ln).then_inc(scal, 1)
            act.wait_ge(vec, VEC_CUM)
            act.activation(ecum[:, :], cum[:, :], ACT.Exp).then_inc(scal, 1)
            act.wait_ge(vec, VEC_DIFF)
            act.activation(wst[:, :], wst[:, :], ACT.Exp).then_inc(scal, 1)
            act.activation(last[:, :], chunks(cum[:, :])[:, :, P - 1], ACT.Exp).then_inc(scal, 1)
            for n in range(BATCH):
                act.wait_ge(tr, n + 1)
                src = pt[n % 4][:, 0:CPB * HEADS].rearrange("p (c k e) -> p c k e", c=CPB, e=2)
                act.activation(tab[:, :, n, 0, :, :].rearrange("p k c e -> p c k e"), src, ACT.Copy, scale=-1.0)\
                   .then_inc(ev, 1)

        @block.vector
        def _(dve):
            dve.wait_ge(whi, 1)
            dve.tensor_tensor(w_lo[:, :, :], w_raw[:, :, :], w_hi[:, :, :].bitcast(F32), ALU.subtract).then_inc(wlo, 1)
            dve.wait_ge(scal, SC_AEXP)
            dve.tensor_scalar(a_neg[:, :], a_neg[:, :], -1.0, None, ALU.mult).then_inc(vec, 1)
            for b in range(BATCH):
                for s in range(2):
                    n = 2 * b + s
                    dve.wait_ge(conv0, n + 1)
                    for j in range(1, 4):
                        if j > 1:
                            dve.wait_ge(taps, 3 * n + j - 1)
                        dve.scalar_tensor_tensor(y[:, s, j:SEQ], pp[s][:, 0:SEQ - j], cp[:, s, 3 - j:4 - j],
                                                 y[:, s, j:SEQ], ALU.mult, ALU.add).then_inc(taps, 1)
            for b in range(BATCH):
                dve.wait_ge(cbd, 2 * b + 1)
                dve.tensor_copy(b_tok[:, b * CPB:(b + 1) * CPB, :],
                                pt[b % 2][:, :].rearrange("p (c n) -> p c n", n=NS)).then_inc(cbe, 1)
                dve.wait_ge(cbd, 2 * b + 2)
                dve.tensor_tensor(cb_m[:, b * CPB:(b + 1) * CPB, :],
                                  pt[2 + b % 2][:, :].rearrange("p (c n) -> p c n", n=P),
                                  causal[:, :].unsqueeze(1).broadcast_to([P, CPB, P]), ALU.mult).then_inc(cbe, 1)
            dve.wait_ge(scal, SC_EXP)
            dve.tensor_scalar(u[:, :], av[:, :], 1.0, None, ALU.add).then_inc(vec, 1)
            dve.wait_ge(scal, SC_LN)
            dve.wait_ge(vec, VEC_U)
            dve.tensor_scalar(u[:, :], u[:, :], 1.0, None, ALU.subtract).then_inc(vec, 1)
            dve.wait_ge(vec, VEC_D)
            dve.tensor_scalar(cum[:, :], u[:, :], 0.0, None, ALU.is_equal).then_inc(vec, 1)
            dve.wait_ge(vec, VEC_Z)
            dve.tensor_tensor(z[:, :], z[:, :], cum[:, :], ALU.add).then_inc(vec, 1)
            dve.tensor_tensor(u[:, :], u[:, :], cum[:, :], ALU.add).then_inc(vec, 1)
            dve.wait_ge(vec, VEC_DEN)
            dve.reciprocal(u[:, :], u[:, :]).then_inc(vec, 1)
            dve.tensor_tensor(z[:, :], z[:, :], av[:, :], ALU.mult).then_inc(vec, 1)
            dve.wait_ge(vec, VEC_NUM2)
            dve.tensor_tensor(z[:, :], z[:, :], u[:, :], ALU.mult).then_inc(vec, 1)
            dve.wait_ge(vec, VEC_Q)
            dve.scalar_tensor_tensor(dt_t[:, :], v[:, :], 0.0, z[:, :], ALU.max, ALU.add).then_inc(vec, 1)
            dve.wait_ge(vec, VEC_DT)
            dve.tensor_scalar(v[:, :], dt_t[:, :], a_neg[:, :], None, ALU.mult).then_inc(vec, 1)
            dve.wait_ge(vec, VEC_DA)
            dve.wait_ge(keep_done, 2)
            dve.tensor_tensor_scan(cum[:, :], keep[:, :], v[:, :], 0.0, ALU.mult, ALU.add).then_inc(vec, 1)
            dve.wait_ge(vec, VEC_CUM)
            cc = chunks(cum[:, :])
            dve.tensor_tensor(chunks(wst[:, :]), cc[:, :, P - 1:P].broadcast_to([HEADS, NT, P]), cc,
                              ALU.subtract).then_inc(vec, 1)
            for n in range(BATCH, 3 * BATCH):
                dve.wait_ge(tr, n + 1)
                dve.wait_ge(ev, n)
                src = pt[n % 4][:, 0:CPB * HEADS].rearrange("p (c k e) -> p c k e", c=CPB, e=2)
                dve.tensor_copy(tab[:, :, n % BATCH, n // BATCH, :, :].rearrange("p k c e -> p c k e"), src)\
                   .then_inc(ev, 1)
            dve.wait_ge(last_in, 16)
            for b in range(BATCH):
                src = last_b[:, :, b * CPB:(b + 1) * CPB].rearrange("p (k e) c -> p c k e", e=2)
                dve.tensor_copy(tab[:, :, b, 3, :, :].rearrange("p k c e -> p c k e"), src).then_inc(ev, 1)


def wait(eng, sem, count):
    if not isinstance(count, int) or count > 0:
        eng.wait_ge(sem, count)


def pipeline(eng, *stages):
    def slots(k):
        for j in range(UNITS):
            for stage, lag in stages:
                q, s = divmod(j - lag, UNITS)
                duo = k + q
                if not isinstance(k, int) or 0 <= duo < DUOS:
                    stage(duo, s)
    slots(-1)
    slots(0)
    with eng.Fori(1, DUOS - 1) as k:
        slots(k)
    slots(DUOS - 1)
    slots(DUOS)


def even(stage):
    def even_units(k, j):
        if j % 2 == 0:
            stage(k, j)
    return even_units


def odd(stage):
    def odd_units(k, j):
        if j % 2 == 1:
            stage(k, j)
    return odd_units


def ssm_phase(nc, xt_hi, xt_lo, w_dram, wo_dram, prm_dram, ident, b_tok, c_t, cb_m, scratch, out_acc, sq_acc):
    cum_d, ecum_d, last_d, tab_d = scratch
    with ExitStack() as ctx:
        sb = lambda n, s, d=F32: ctx.enter_context(nc.sbuf_tensor(f"ssm_{n}", s, d))
        sem = ctx.enter_context(phase_semaphores(nc, "ssm"))
        pb = lambda n, w=SEQ: ctx.enter_context(nc.psum_tensor(f"ssm_{n}", [P, w], F32))
        R = 4
        L = UNITS
        w_raw = sb("w_raw", [P, 2, KT, 2 * P])
        w_hi = sb("w_hi", [P, 2, KT, 2 * P], F32R)
        w_lo = sb("w_lo", [P, 2, KT, 2 * P], F32R)
        wo_raw = sb("wo_raw", [P, 2, DM + 1])
        wo = sb("wo", [P, 2, DM])
        prm = sb("prm", [P, L, 6])
        tab = sb("tab", [P, L, 4, CPB * 2])
        cm = sb("cm", [P, L, 2, SEQ])
        er = sb("er", [P, R, SEQ - P])
        y = sb("y", [P, R, SEQ])
        xs = sb("xs", [P, L, SEQ])
        sg = sb("sg", [P, L, SEQ])
        xdt = sb("xdt", [P, R, SEQ])
        xw = sb("xw", [P, 2, SEQ - P])
        S = sb("S", [P, 2, CPB - 1, P])
        t1 = sb("t1", [P, 2, SEQ - P])
        t2 = sb("t2", [P, 2, SEQ])
        h = sb("h", [P, 2, SEQ])
        sq = sb("sq", [P, 2, SEQ])
        px, pg, pt, pyd, pst, pyo = (pb(n) for n in ("px", "pg", "pt", "pyd", "pst", "pyo"))
        po = pb("po", CPB * DM)
        names = ("w_in wo_in w_hi_done w_ready wo_ready x_ready g_ready conv0_done taps_done gate_done xs_ready "
                 "tr_done xdt_ready xw_ready masked exp_done m_ready yd_done st_done s1_done rec_done yo_done "
                 "t2_done t1_done hs_done h_ready sq_done acc_done out_done oacc_done zeroed mask_begun")
        (w_in, wo_in, w_hi_done, w_ready, wo_ready, x_ready, g_ready, conv0_done, taps_done, gate_done, xs_ready,
         tr_done, xdt_ready, xw_ready, masked, exp_done, m_ready, yd_done, st_done, s1_done, rec_done, yo_done,
         t2_done, t1_done, hs_done, h_ready, sq_done, acc_done, out_done, oacc_done, zeroed, mask_begun) = map(sem, names.split())
        prm_in, tab_in, cm_in = ([sem(f"{n}{b}") for b in range(L)] for n in ("prm_in", "tab_in", "cm_in"))
        er_in = [sem(f"er_in{b}") for b in range(R)]
        block = ctx.enter_context(nc.Block())

        def N(k, j):
            return UNITS * k + j + 1

        def turn(k, j):
            return k + 1

        @block.sync
        def _(sp):
            def weights(k, j):
                if j == 0:
                    wait(sp, w_ready, 2 * k)
                    sp.dma_start(w_raw[:, :, :, :].rearrange("p e k n -> p e (k n)"),
                                 w_dram[bass.ds(2 * k, 2)].rearrange("e p n -> p e n")).then_inc(w_in, 16)

            def out_weights(k, j):
                if j == 1:
                    wait(sp, wo_ready, k)
                    sp.dma_start(wo_raw[:, :, :], wo_dram[bass.ds(2 * k, 2)].rearrange("e p n -> p e n"))\
                      .then_inc(wo_in, 16)

            def tables(k, j):
                n, b, e = N(k, j), j // 2, j % 2
                pair = 2 * k + e
                wait(sp, rec_done, 2 * (n - L))
                wait(sp, t2_done, n - L)
                sp.dma_start(prm[:, j, :], prm_dram[bass.ds(pair, 1)].rearrange("a p n -> (a p) n")).then_inc(prm_in[j], 16)
                sp.dma_start(tab[:, j].rearrange("p f n -> p (f n)"),
                             tab_d[:, bass.ds((pair * BATCH + b) * 32, 32)]).then_inc(tab_in[j], 16)
                wait(sp, yd_done, n - L)
                sp.dma_start(cm[:, j, :, :], cum_d[bass.ds(2 * pair, 2), b * SEQ:(b + 1) * SEQ].unsqueeze(0)
                             .broadcast_to([P, 2, SEQ])).then_inc(cm_in[j], 16)

            def exp_cum(k, j):
                r, b, pair = j % R, j // 2, 2 * k + j % 2
                wait(sp, t1_done, N(k, j) - R)
                for i in range(2):
                    sp.dma_start(er[i * HD:(i + 1) * HD, r, :],
                                 ecum_d[bass.ds(2 * pair + i, 1), b * SEQ + P:(b + 1) * SEQ].broadcast_to([HD, SEQ - P]))\
                      .then_inc(er_in[r], 16)

            pipeline(sp, (weights, -6), (out_weights, 0), (tables, 0), (exp_cum, 2))

        @block.tensor
        def _(pe):
            def project(k, j, s, bank, done, used, at):
                c = slice(s * P, (s + 1) * P)
                cols = slice(j // 2 * SEQ, (j // 2 + 1) * SEQ)
                if j < 2:
                    pe.wait_ge(w_ready, 2 * k + j + 1)
                wait(pe, used, at)
                split_matmuls(pe, bank[:, :], [w_hi[:, j % 2, i, c] for i in range(KT)],
                              [w_lo[:, j % 2, i, c] for i in range(KT)], [xt_hi[:, i, cols] for i in range(KT)],
                              [xt_lo[:, i, cols] for i in range(KT)]).then_inc(done, 1)

            def project_x(k, j):
                project(k, j, 0, px, x_ready, taps_done, 3 * (N(k, j) - 1))

            def project_gate(k, j):
                project(k, j, 1, pg, g_ready, gate_done, N(k, j) - 1)

            def transposes(k, j):
                n = N(k, j)
                pe.wait_ge(xs_ready, n)
                wait(pe, xdt_ready, n - 1)
                for c in range(CPB):
                    last = pe.transpose(pt[:, c * P:(c + 1) * P], xs[:, j, c * P:(c + 1) * P], ident[:, :])
                last.then_inc(tr_done, 1)

            def y_diag(k, j):
                n = N(k, j)
                pe.wait_ge(m_ready, n)
                pe.wait_ge(xdt_ready, n)
                wait(pe, t2_done, n - 1)
                for c in range(CPB):
                    for e in range(2):
                        t = slice(c * P, (c + 1) * P)
                        last = pe.matmul(pyd[e * HD:(e + 1) * HD, t], xdt[:, j % R, c * P + e * HD:c * P + (e + 1) * HD],
                                         cm[:, j, e, t], start=True, stop=True)
                last.then_inc(yd_done, 1)

            def states(k, j):
                n = N(k, j)
                pe.wait_ge(xw_ready, n)
                wait(pe, rec_done, 2 * (n - 1))
                wait(pe, s1_done, n - 1)
                for c in range(CPB - 1):
                    t = slice(c * P, (c + 1) * P)
                    last = pe.matmul(pst[:, t], b_tok[:, j // 2 * CPB + c, :], xw[:, j % 2, t], start=True, stop=True)
                last.then_inc(st_done, 1)

            def y_off(k, j):
                n = N(k, j)
                pe.wait_ge(rec_done, 2 * n)
                pe.wait_ge(s1_done, n)
                wait(pe, t1_done, n - 1)
                for c in range(1, CPB):
                    t = (j // 2 * CPB + c) * P
                    last = pe.matmul(pyo[:, (c - 1) * P:c * P], S[:, j % 2, c - 1, :], c_t[:, t:t + P],
                                     start=True, stop=True)
                last.then_inc(yo_done, 1)

            def project_out(k, j):
                n, e = N(k, j), j % 2
                if j == 0:
                    pe.wait_ge(wo_ready, k + 1)
                pe.wait_ge(h_ready, n)
                if e == 0:
                    wait(pe, oacc_done, BATCH * k + j // 2)
                for c in range(CPB):
                    last = pe.matmul(po[:, c * DM:(c + 1) * DM], h[:, j % 2, c * P:(c + 1) * P], wo[:, e, :],
                                     start=(e == 0 and c % 2 == 0), stop=(e == 1), skip_group_check=True)
                last.then_inc(out_done, 1)

            pipeline(pe, (project_x, 0), (odd(project_gate), 0), (y_off, 4), (states, 3), (transposes, 2), (y_diag, 3),
                     (project_out, 5), (even(project_gate), 0))

        @block.scalar
        def _(act):
            def split_high(k, j):
                if j < 2:
                    act.wait_ge(w_in, 16 * (k + 1))
                    wait(act, g_ready, UNITS * k - 1 + j)
                    act.activation(w_hi[:, j, :, :], w_raw[:, j, :, :], ACT.Copy).then_inc(w_hi_done, 1)

            def conv_first(k, j):
                n = N(k, j)
                act.wait_ge(x_ready, n)
                act.wait_ge(prm_in[j], 16 * turn(k, j))
                wait(act, xs_ready, n - R)
                act.activation(y[:, j % R, :], px[:, :], ACT.Identity, bias=prm[:, j, 4:5], scale=prm[:, j, 3:4])\
                   .then_inc(conv0_done, 1)

            def gate(k, j):
                n = N(k, j)
                act.wait_ge(g_ready, n)
                wait(act, h_ready, n - L)
                act.activation(sg[:, j, :], pg[:, :], ACT.Silu).then_inc(gate_done, 1)

            def conv_silu(k, j):
                n = N(k, j)
                act.wait_ge(taps_done, 3 * n)
                wait(act, t2_done, n - L)
                act.activation(xs[:, j, :], y[:, j % R, :], ACT.Silu).then_inc(xs_ready, 1)

            def decay(k, j, e):
                act.wait_ge(masked, N(k, j))
                act.wait_ge(tab_in[j], 16 * turn(k, j))
                for c in range(CPB):
                    t = slice(c * P, (c + 1) * P)
                    last = act.activation(cm[:, j, e, t], cm[:, j, e, t], ACT.Exp,
                                          bias=tab[:, j, 0, 2 * c + e:2 * c + e + 1])
                last.then_inc(exp_done, 1)

            def decay_first(k, j):
                decay(k, j, 0)

            def decay_second(k, j):
                decay(k, j, 1)

            def first_state(k, j):
                n = N(k, j)
                act.wait_ge(st_done, n)
                wait(act, yo_done, n - 2)
                act.activation(S[:, j % 2, 0, :], pst[:, 0:P], ACT.Copy).then_inc(s1_done, 1)

            def squares(k, j):
                n = N(k, j)
                act.wait_ge(h_ready, n)
                wait(act, acc_done, n - 2)
                act.activation(sq[:, j % 2, :], h[:, j % 2, :], ACT.Square).then_inc(sq_done, 1)

            pipeline(act, (split_high, -1), (even(conv_first), 0), (decay_first, 1), (first_state, 3), (decay_second, 1),
                     (squares, 5), (odd(conv_silu), 1), (even(gate), 0), (odd(conv_first), -1), (even(conv_silu), 0),
                     (odd(gate), -1))

        @block.vector
        def _(dve):
            def split_low(k, j):
                if j < 2:
                    dve.wait_ge(w_hi_done, 2 * k + j + 1)
                    dve.tensor_tensor(w_lo[:, j, :, :], w_raw[:, j, :, :], w_hi[:, j, :, :].bitcast(F32), ALU.subtract)\
                       .then_inc(w_ready, 1)

            def scale_out_weights(k, j):
                if j == 4:
                    dve.wait_ge(wo_in, 16 * (k + 1))
                    wait(dve, out_done, UNITS * k)
                    for e in range(2):
                        last = dve.tensor_scalar(wo[:, e, :], wo_raw[:, e, 0:DM], wo_raw[:, e, DM:DM + 1], None, ALU.mult)
                    last.then_inc(wo_ready, 1)

            def conv_taps(k, j):
                n = N(k, j)
                dve.wait_ge(conv0_done, n)
                for i in range(1, 4):
                    if i > 1:
                        dve.wait_ge(taps_done, 3 * (n - 1) + i - 1)
                    dve.scalar_tensor_tensor(y[:, j % R, i:SEQ], px[:, 0:SEQ - i], prm[:, j, 3 - i:4 - i],
                                             y[:, j % R, i:SEQ], ALU.mult, ALU.add).then_inc(taps_done, 1)

            def x_times_dt(k, j):
                n = N(k, j)
                dve.wait_ge(tr_done, n)
                dve.wait_ge(tab_in[j], 16 * turn(k, j))
                wait(dve, yd_done, n - R)
                wait(dve, xw_ready, n - R)
                dve.tensor_tensor(xdt[:, j % R, :].rearrange("p (n d) -> p n d", d=HD),
                                  pt[:, :].rearrange("p (n d) -> p n d", d=HD),
                                  tab[:, j, 1, :].unsqueeze(2).broadcast_to([P, 2 * CPB, HD]), ALU.mult)\
                   .then_inc(xdt_ready, 1)

            def scores(k, j):
                c = j // 2 * CPB
                for e in range(2):
                    dve.wait_ge(exp_done, 2 * N(k, j) - 1 + e)
                    last = dve.tensor_tensor(cm[:, j, e, :], cm[:, j, e, :],
                                             cb_m[:, c:c + CPB, :].rearrange("p c i -> p (c i)"), ALU.mult)
                last.then_inc(m_ready, 1)

            def direct_term(k, j):
                n = N(k, j)
                dve.wait_ge(yd_done, n)
                wait(dve, h_ready, n - 2)
                dve.scalar_tensor_tensor(t2[:, j % 2, :], xs[:, j, :], prm[:, j, 5:6], pyd[:, :], ALU.mult, ALU.add)\
                   .then_inc(t2_done, 1)

            def recurrence(k, j):
                n = N(k, j)
                dve.wait_ge(s1_done, n)
                for c in range(1, CPB - 1):
                    if c > 1:
                        dve.wait_ge(rec_done, 2 * (n - 1) + c - 1)
                    for e in range(2):
                        d = slice(e * HD, (e + 1) * HD)
                        last = dve.scalar_tensor_tensor(S[:, j % 2, c, d], S[:, j % 2, c - 1, d],
                                                        tab[:, j, 3, 2 * c + e:2 * c + e + 1],
                                                        pst[:, c * P + e * HD:c * P + (e + 1) * HD], ALU.mult, ALU.add)
                    last.then_inc(rec_done, 1)

            def off_term(k, j):
                n = N(k, j)
                dve.wait_ge(yo_done, n)
                dve.wait_ge(er_in[j % R], 32 * (2 * k + j // R + 1))
                wait(dve, hs_done, n - 2)
                dve.tensor_tensor(t1[:, j % 2, :], pyo[:, 0:SEQ - P], er[:, j % R, :], ALU.mult).then_inc(t1_done, 1)

            def add_out(k, j):
                if j % 2 == 0:
                    return
                dve.wait_ge(out_done, N(k, j))
                b = j // 2
                acc = out_acc[:, b * CPB:(b + 1) * CPB, :].rearrange("p c d -> p (c d)")
                dve.tensor_tensor(acc, po[:, :], acc, ALU.add).then_inc(oacc_done, 1)

            dve.memset(out_acc[:, :, :], 0.0).then_inc(zeroed, 1)
            dve.memset(sq_acc[:, :, :], 0.0).then_inc(zeroed, 1)
            dve.wait_ge(zeroed, 2)
            pipeline(dve, (direct_term, 4), (scores, 2), (split_low, -1), (conv_taps, 0), (off_term, 4), (x_times_dt, 2),
                     (recurrence, 3), (add_out, 5), (scale_out_weights, 0))

        @block.gpsimd
        def _(pool):
            def mask(k, j):
                pool.wait_ge(cm_in[j], 16 * turn(k, j))
                pool.sem_inc(mask_begun, 1)
                m = cm[:, j, :, :].rearrange("p e (c i) -> p (e c) i", i=P)
                pool.affine_select(out=m, in_=m, compare_op=ALU.is_ge, fill=masked_value, base=0,
                                   pattern=[[0, 2 * CPB], [1, P]], channel_multiplier=-1).then_inc(masked, 1)

            def x_to_state(k, j):
                n = N(k, j)
                pool.wait_ge(xdt_ready, n)
                wait(pool, st_done, n - 2)
                pool.tensor_tensor(xw[:, j % 2, :].rearrange("p (n d) -> p n d", d=HD),
                                   xdt[:, j % R, 0:SEQ - P].rearrange("p (n d) -> p n d", d=HD),
                                   tab[:, j, 2, 0:2 * (CPB - 1)].unsqueeze(2).broadcast_to([P, 2 * (CPB - 1), HD]),
                                   ALU.mult).then_inc(xw_ready, 1)

            def gated(k, j):
                n = N(k, j)
                pool.wait_ge(t1_done, n)
                pool.wait_ge(t2_done, n)
                pool.tensor_tensor(t2[:, j % 2, P:SEQ], t2[:, j % 2, P:SEQ], t1[:, j % 2, :], ALU.add).then_inc(hs_done, 1)
                pool.wait_ge(hs_done, n)
                pool.wait_ge(gate_done, n)
                wait(pool, out_done, n - 2)
                wait(pool, sq_done, n - 2)
                pool.tensor_tensor(h[:, j % 2, :], t2[:, j % 2, :], sg[:, j, :], ALU.mult).then_inc(h_ready, 1)

            def add_squares(k, j):
                pool.wait_ge(sq_done, N(k, j))
                wait(pool, acc_done, N(k, j) - 1)
                pool.tensor_tensor(sq_acc[:, j // 2, :], sq_acc[:, j // 2, :], sq[:, j % 2, :], ALU.add).then_inc(acc_done, 1)

            masked_value = pool.to_reg(MASKED)
            pool.wait_ge(zeroed, 2)
            pipeline(pool, (mask, 0), (gated, 4), (x_to_state, 2), (add_squares, 5))


def mamba_output_phase(nc, x_dram, gate_dram, out_acc, sq_acc, x1_dram):
    with ExitStack() as ctx:
        sb = lambda n, s, d=F32: ctx.enter_context(nc.sbuf_tensor(f"mo_{n}", s, d))
        sem = ctx.enter_context(phase_semaphores(nc, "mo"))
        x = sb("x", [P, NT, DM])
        g = sb("g", [P, NT, DM])
        ones = sb("ones", [P, 1])
        var = sb("var", [P, NT])
        std = sb("std", [P, NT])
        rstd = sb("rstd", [P, NT])
        pv = ctx.enter_context(nc.psum_tensor("mo_pv", [P, NT], F32))
        x_in, g_in, ones_done, sums, var_done, std_done = map(sem, "x_in g_in ones_done sums var_done std_done".split())
        rstd_done, scaled, added, stored = map(sem, "rstd_done scaled added stored".split())
        block = ctx.enter_context(nc.Block())

        @block.sync
        def _(sp):
            sp.dma_start(g[:, :, :], gate_dram.rearrange("(t p) d -> p t d", p=P)).then_inc(g_in, 16)
            sp.dma_start(x[:, :, :], x_dram.rearrange("(t p) d -> p t d", p=P)).then_inc(x_in, 16)
            ov = x1_dram.rearrange("(t p) d -> p t d", p=P)
            for q in range(4):
                sp.wait_ge(added, 4 * (q + 1))
                sp.dma_start(ov[:, 4 * q:4 * q + 4, :], x[:, 4 * q:4 * q + 4, :]).then_inc(stored, 16)
            sp.wait_ge(stored, 64)

        @block.tensor
        def _(pe):
            pe.wait_ge(ones_done, 1)
            for t in range(NT):
                m = pe.matmul(pv[:, t:t + 1], sq_acc[:, t // CPB, (t % CPB) * P:(t % CPB + 1) * P], ones[:, :],
                              start=True, stop=True)
            m.then_inc(sums, 1)

        @block.scalar
        def _(act):
            act.wait_ge(var_done, 1)
            act.activation(std[:, :], var[:, :], ACT.Sqrt).then_inc(std_done, 1)

        @block.vector
        def _(dve):
            dve.memset(ones[:, :], 1.0).then_inc(ones_done, 1)
            dve.wait_ge(sums, 1)
            dve.tensor_scalar(var[:, :], pv[:, :], 1.0 / DI, EPS, ALU.mult, ALU.add).then_inc(var_done, 1)
            dve.wait_ge(std_done, 1)
            dve.reciprocal(rstd[:, :], std[:, :]).then_inc(rstd_done, 1)
            dve.wait_ge(rstd_done, 1)
            dve.wait_ge(g_in, 16)
            for t in range(NT):
                dve.scalar_tensor_tensor(g[:, t, :], out_acc[:, t, :], rstd[:, t:t + 1], g[:, t, :], ALU.mult, ALU.mult)\
                   .then_inc(scaled, 1)
            dve.wait_ge(x_in, 16)
            for t in range(NT):
                dve.wait_ge(scaled, t + 1)
                dve.tensor_tensor(x[:, t, :], x[:, t, :], g[:, t, :], ALU.add).then_inc(added, 1)


def constants_phase(nc, ident, causal):
    with ExitStack() as ctx:
        ready = ctx.enter_context(phase_semaphores(nc, "const"))("ready")
        block = ctx.enter_context(nc.Block())

        @block.gpsimd
        def _(pool):
            pool.memset(ident[:, :], 0.0).then_inc(ready, 1)
            pool.memset(causal[:, :], 1.0).then_inc(ready, 1)
            pool.wait_ge(ready, 2)
            pool.affine_select(out=ident[:, :], in_=ident[:, :], compare_op=ALU.not_equal, fill=1.0, base=0,
                               pattern=[[-1, P]], channel_multiplier=1).then_inc(ready, 1)
            pool.affine_select(out=causal[:, :], in_=causal[:, :], compare_op=ALU.is_ge, fill=0.0, base=0,
                               pattern=[[1, P]], channel_multiplier=-1).then_inc(ready, 1)


HN, HW = 16, 16
GROUP = 4
MASK_SCORE = 10000.0


def attention_constants_phase(nc, ident_b, block_b, head_mask, later, ones, count, floor):
    with ExitStack() as ctx:
        sem = ctx.enter_context(phase_semaphores(nc, "ac"))
        s1, s2 = sem("ready"), sem("count")
        ci = ctx.enter_context(nc.sbuf_tensor("ac_ci", [P, CPB], mybir.dt.int32))
        block = ctx.enter_context(nc.Block())

        @block.gpsimd
        def _(pool):
            for m, value in ((ident_b, 0.0), (block_b, 0.0), (head_mask, 1.0), (later, 1.0), (ones, 1.0),
                             (floor, MASK_SCORE)):
                pool.memset(m[:, :], value).then_inc(s1, 1)
            pool.wait_ge(s1, 6)
            pool.affine_select(out=ident_b[:, :], in_=ident_b[:, :], compare_op=ALU.not_equal, fill=1.0, base=0,
                               pattern=[[-1, P]], channel_multiplier=1).then_inc(s1, 1)
            pool.affine_select(out=block_b[:, :], in_=block_b[:, :], compare_op=ALU.is_ge, fill=MASKED, base=0,
                               pattern=[[-1, P]], channel_multiplier=1).then_inc(s1, 1)
            pool.affine_select(out=later[:, :], in_=later[:, :], compare_op=ALU.is_ge, fill=0.0, base=-1,
                               pattern=[[-1, P]], channel_multiplier=1).then_inc(s1, 1)
            pool.affine_select(out=head_mask[:, :], in_=head_mask[:, :], compare_op=ALU.is_ge, fill=0.0, base=0,
                               pattern=[[-HW, P // HW]], channel_multiplier=1).then_inc(s1, 1)
            pool.wait_ge(s1, 10)
            pool.affine_select(out=head_mask[:, :], in_=head_mask[:, :], compare_op=ALU.is_ge, fill=0.0, base=HW - 1,
                               pattern=[[HW, P // HW]], channel_multiplier=-1).then_inc(s1, 1)
            pool.affine_select(out=floor[:, :], in_=floor[:, :], compare_op=ALU.is_ge, fill=-MASKED, base=SEQ - 2,
                               pattern=[[-P, CPB]], channel_multiplier=-1).then_inc(s1, 1)
            pool.iota(ci[:, :], pattern=[[-P, CPB]], base=SEQ - 1, channel_multiplier=-1).then_inc(s2, 1)

        @block.vector
        def _(dve):
            dve.wait_ge(s2, 1)
            dve.tensor_copy(count[:, :], ci[:, :]).then_inc(s2, 1)


def attention_phase(nc, xt_hi, xt_lo, w_dram, b_dram, bv_dram, wo_dram, bo_dram, ident, s1_dram):
    with ExitStack() as ctx:
        sb = lambda n, s, d=F32: ctx.enter_context(nc.sbuf_tensor(f"at_{n}", s, d))
        sem = ctx.enter_context(phase_semaphores(nc, "at"))
        BF = mybir.dt.bfloat16
        ident_b, block_b = sb("ident_b", [P, P], BF), sb("block_b", [P, P], BF)
        head_mask = sb("head_mask", [P, P // HW])
        later, ones = sb("later", [P, P]), sb("ones", [P, P])
        count, floor = sb("count", [P, CPB]), sb("floor", [P, CPB])
        attention_constants_phase(nc, ident_b, block_b, head_mask, later, ones, count, floor)
        W = 3 * DM
        GROUPS = HN // GROUP
        UNITS = HN * CPB
        w_raw = sb("w_raw", [P, KT, W])
        w_hi, w_lo = sb("w_hi", [P, KT, W], F32R), sb("w_lo", [P, KT, W], F32R)
        bias = sb("bias", [P, 2 * KT])
        bv, bo = sb("bv", [P, DM]), sb("bo", [P, DM])
        wo = sb("wo", [P, KT, DM])
        full = sb("full", [P, 2 * KT, SEQ])
        split = sb("split", [P, 4 * KT, SEQ], F32R)
        stack = sb("stack", [P, 4, 2, SEQ], F32R)
        q_lo, q_hi, k_hi, k_lo = (split[:, KT * i:KT * (i + 1), :] for i in range(4))
        vp = sb("vp", [P, CPB, HN, 32])
        sv = sb("sv", [P, CPB, DM])
        pe_ = sb("pe_", [P, 4, SEQ])
        pt_ = sb("pt_", [P, 2, GROUP, CPB, SEQ])
        mx = sb("mx", [P, CPB, HN])
        nm = sb("nm", [P, CPB, HN])
        rs = sb("rs", [P, CPB, HN])
        em = sb("em", [P, CPB, HN])
        den = sb("den", [P, CPB, HN])
        pvs = sb("pvs", [P, 2, SEQ])
        o = sb("o", [P, CPB, DM])
        s1 = sb("s1", [P, CPB, DM])
        ot = full[:, 0:KT, :]
        sc = [ctx.enter_context(nc.psum_tensor(f"at_sc{i}", [P, SEQ], F32)) for i in range(4)]
        tp = [ctx.enter_context(nc.psum_tensor(f"at_tp{i}", [P, SEQ], F32)) for i in range(2)]
        pv = ctx.enter_context(nc.psum_tensor("at_pv", [P, SEQ], F32))
        px = ctx.enter_context(nc.psum_tensor("at_px", [P, SEQ], F32))
        names = ("w_in prm_in w_hi_done w_lo_done bias_done pad_done qk_done full_done qk_hi_done qk_lo_done "
                 "v_done vp_done sv_done svs_done cleared score_done max_done nm_done exp_done tp_done pt_act pt_dve "
                 "pv_done pvs_done px_done em_in em_done den_done o_step ot_ready ot_act ot_dve proj_done s1_done s1_stored")
        (w_in, prm_in, w_hi_done, w_lo_done, bias_done, pad_done, qk_done, full_done, qk_hi_done, qk_lo_done,
         v_done, vp_done, sv_done, svs_done, cleared, score_done, max_done, nm_done, exp_done, tp_done, pt_act, pt_dve,
         pv_done, pvs_done, px_done, em_in, em_done, den_done, o_step, ot_ready, ot_act, ot_dve, proj_done,
         s1_done, s1_stored) = map(sem, names.split())
        stacked = [sem(f"stacked{i}") for i in range(4)]
        block = ctx.enter_context(nc.Block())
        def full_v(m):
            return pe_[:, m, :]

        LAG_T, LAG_PV, LAG_X = 3, 6, 11
        END = UNITS + LAG_X + 1

        @block.sync
        def _(sp):
            sp.dma_start(w_raw[:, :, :], w_dram.rearrange("(k p) n -> p k n", p=P)).then_inc(w_in, 16)
            sp.dma_start(bias[:, :], b_dram).then_inc(prm_in, 16)
            sp.dma_start(bv[:, :], bv_dram.broadcast_to([P, DM])).then_inc(prm_in, 16)
            sp.dma_start(bo[:, :], bo_dram.broadcast_to([P, DM])).then_inc(prm_in, 16)
            sp.dma_start(wo[:, :, :], wo_dram.rearrange("(k p) n -> p k n", p=P)).then_inc(prm_in, 16)

            def stack_head(b, h):
                if h >= 4:
                    sp.wait_ge(score_done, b * UNITS + (h - 3) * CPB)
                g, src = h // 8, slice(h % 8 * HW, (h % 8 + 1) * HW)
                for copy, (of_q, of_k) in enumerate(((KT, 2 * KT), (0, 2 * KT), (KT, 3 * KT))):
                    row = h % 2 * 4 * HW + copy * HW
                    sp.dma_start(stack[row:row + HW, h % 4, :, :].bitcast(F32),
                                 split[src, of_q + g:of_k + g + 1:of_k - of_q, :].bitcast(F32))\
                      .then_inc(stacked[h % 4], 16)

            sp.sem_inc(s1_stored, 16)
            sp.wait_ge(cleared, 1)
            with sp.Fori(0, BATCH) as b:
                sp.wait_ge(qk_hi_done, b * 2 * KT + 2 * KT)
                sp.wait_ge(qk_lo_done, b * 2 * KT + 2 * KT)
                for h in range(HN):
                    stack_head(b, h)
                sp.wait_ge(s1_done, b + 1)
                sp.dma_start(s1_dram.rearrange("(b t p) d -> b p t d", b=BATCH, p=P)[bass.ds(b, 1)]
                             .rearrange("b p t d -> (b p) t d"), s1[:, :, :]).then_inc(s1_stored, 16)
            sp.wait_ge(s1_stored, 16 * (BATCH + 1))

        @block.gpsimd
        def _(pool):
            pool.memset(stack[:, :, :, :].bitcast(F32), 0.0).then_inc(cleared, 1)

        @block.tensor
        def _(pe):
            pe.wait_ge(w_lo_done, 1)
            with pe.Fori(0, BATCH) as b:
                toks = bass.ds(b * SEQ, SEQ)
                for m in range(2 * KT):
                    c = slice(m * P, (m + 1) * P)
                    split_matmuls(pe, sc[m][:, :], [w_hi[:, j, c] for j in range(KT)], [w_lo[:, j, c] for j in range(KT)],
                                  [xt_hi[:, j, toks] for j in range(KT)], [xt_lo[:, j, toks] for j in range(KT)])\
                        .then_inc(qk_done, 1)
                for m in range(KT):
                    c = slice((2 * KT + m) * P, (2 * KT + m + 1) * P)
                    split_matmuls(pe, tp[m][:, :], [w_hi[:, j, c] for j in range(KT)], [w_lo[:, j, c] for j in range(KT)],
                                  [xt_hi[:, j, toks] for j in range(KT)], [xt_lo[:, j, toks] for j in range(KT)])\
                        .then_inc(qk_done, 1)
                for m in range(KT):
                    pe.wait_ge(v_done, 2 * b + m + 1)
                    for t in range(CPB):
                        last = pe.transpose((pv, px)[m][:, t * P:(t + 1) * P], full_v(m)[:, t * P:(t + 1) * P], ident[:, :])
                    last.then_inc(qk_done, 1)
                pe.wait_ge(vp_done, 2 * b + 2)
                pe.wait_ge(full_done, 4 * b + 4)
                for i in range(CPB):
                    for j in range(i, CPB):
                        last = pe.matmul(sc[i][:, 0:DM], (later if j == i else ones)[:, :], vp[:, j, :, 0:HW],
                                         start=(j == i), stop=(j == CPB - 1))
                last.then_inc(sv_done, 1)
                pe.wait_ge(svs_done, b + 1)

                def scores(u):
                    h, i = divmod(u, CPB)
                    if i == 0:
                        pe.wait_ge(stacked[h % 4], 48 * (b * HN // 4 + h // 4 + 1))
                    if u >= 4:
                        pe.wait_ge(exp_done, b * UNITS + u - 3)
                    n = (i + 1) * P
                    out, t = sc[u % 4][:, 0:n], slice(i * P, (i + 1) * P)
                    pe.matmul(sc[u % 4][:, i * P:n], ident_b[:, :], block_b[:, :], start=True, stop=False,
                              skip_group_check=True)
                    pe.matmul(out, stack[:, h % 4, 0, t], stack[:, h % 4, 1, 0:n], start=False, stop=True,
                              skip_group_check=True).then_inc(score_done, 1)

                def transposes(u):
                    h, i = divmod(u, CPB)
                    pe.wait_ge(exp_done, b * UNITS + u + 1)
                    if i < 2 and h:
                        pe.wait_ge(pt_act, b * UNITS // 2 + 2 * h + i - 1)
                    if i >= 2:
                        pe.wait_ge(pt_dve, b * UNITS // 2 + 2 * h + i - 1)
                    for j in range(i + 1):
                        last = pe.transpose(tp[u % 2][:, j * P:(j + 1) * P], pe_[:, u % 4, j * P:(j + 1) * P], ident[:, :])
                    last.then_inc(tp_done, 1)

                def products(g, j):
                    if j == 0:
                        pe.wait_ge(pt_act, b * UNITS // 2 + 2 * GROUP * (g + 1))
                        pe.wait_ge(pt_dve, b * UNITS // 2 + 2 * GROUP * (g + 1))
                        if g:
                            pe.wait_ge(pvs_done, b * GROUPS + g)
                    for q in range(GROUP):
                        last = pe.matmul(pv[32 * q:32 * q + 32, j * P:SEQ], vp[:, j, GROUP * g + q, :],
                                         pt_[:, g % 2, q, j, j * P:SEQ], start=(j == 0), stop=(j == CPB - 1))
                    if j == CPB - 1:
                        last.then_inc(pv_done, 1)

                def turn_back(g):
                    pe.wait_ge(pvs_done, b * GROUPS + g + 1)
                    if g:
                        pe.wait_ge(o_step, 3 * (b * GROUPS + g - 1) + 2)
                    for i in range(CPB):
                        last = pe.transpose(px[:, i * P:(i + 1) * P], pvs[:, g % 2, i * P:(i + 1) * P], ident[:, :])
                    last.then_inc(px_done, 1)

                for n in range(END):
                    if n < UNITS:
                        scores(n)
                    if 0 <= n - LAG_T < UNITS:
                        transposes(n - LAG_T)
                    g, r = divmod(n - LAG_PV + 1, GROUP * CPB)
                    if r < CPB and 0 < g <= GROUPS:
                        products(g - 1, r)
                    g, r = divmod(n - LAG_X + 1, GROUP * CPB)
                    if r == 0 and 0 < g <= GROUPS:
                        turn_back(g - 1)
                pe.wait_ge(o_step, 3 * (b * GROUPS + GROUPS))
                for k in range(KT):
                    for i in range(CPB):
                        last = pe.transpose(sc[k][:, i * P:(i + 1) * P], o[:, i, k * P:(k + 1) * P], ident[:, :])
                    last.then_inc(ot_ready, 1)
                pe.wait_ge(ot_act, b + 1)
                pe.wait_ge(ot_dve, b + 1)
                for i in range(CPB):
                    for k in range(KT):
                        last = pe.matmul((sc[2], sc[3], tp[0], tp[1])[i][:, 0:DM],
                                         ot[:, k, i * P:(i + 1) * P], wo[:, k, :], start=(k == 0), stop=(k == KT - 1))
                last.then_inc(proj_done, 1)
                pe.wait_ge(s1_done, b + 1)

        def p_tile(u):
            h, i = divmod(u, CPB)
            return (pt_[:, h // GROUP % 2, h % GROUP, 0:i + 1, i * P:(i + 1) * P],
                    tp[u % 2][:, 0:(i + 1) * P].rearrange("p (j t) -> p j t", t=P))

        @block.scalar
        def _(act):
            act.wait_ge(w_in, 16)
            act.activation(w_hi[:, :, :], w_raw[:, :, :], ACT.Copy).then_inc(w_hi_done, 1)
            act.wait_ge(bias_done, 1)
            with act.Fori(0, BATCH) as b:
                for m in range(2 * KT):
                    act.wait_ge(qk_done, b * 4 * KT + m + 1)
                    act.activation(full[:, m, :], sc[m][:, :], ACT.Identity, bias=bias[:, m:m + 1],
                                   scale=0.25 if m < KT else 1.0).then_inc(full_done, 1)
                for m in range(KT):
                    act.wait_ge(qk_done, b * 4 * KT + 2 * KT + m + 1)
                    act.activation(full_v(m), tp[m][:, :], ACT.Copy).then_inc(v_done, 1)
                for m in range(2 * KT):
                    act.wait_ge(full_done, b * 2 * KT + m + 1)
                    act.activation((q_hi if m < KT else k_hi)[:, m % KT, :], full[:, m, :], ACT.Copy).then_inc(qk_hi_done, 1)
                act.wait_ge(sv_done, b + 1)
                for i in range(CPB):
                    last = act.activation(sv[:, i, :], sc[i][:, 0:DM], ACT.Copy)
                last.then_inc(svs_done, 1)

                def exps(u):
                    h, i = divmod(u, CPB)
                    act.wait_ge(nm_done, b * UNITS + u + 1)
                    if u >= 4:
                        act.wait_ge(tp_done, b * UNITS + u - 3)
                    n = (i + 1) * P
                    act.activation(pe_[:, u % 4, 0:n], sc[u % 4][:, 0:n], ACT.Exp, bias=nm[:, i, h:h + 1],
                                   accum_out=rs[:, i, h:h + 1]).then_inc(exp_done, 1)

                def evacuate(u):
                    h, i = divmod(u, CPB)
                    if i >= 2:
                        act.wait_ge(tp_done, b * UNITS + u + 1)
                        if h >= 2 * GROUP and h % GROUP == 0:
                            act.wait_ge(pv_done, b * GROUPS + h // GROUP - 1)
                        act.activation(*p_tile(u), ACT.Copy).then_inc(pt_act, 1)

                def mask_shares(g):
                    act.wait_ge(em_in, b * GROUPS + g + 1)
                    hs = slice(g * GROUP, (g + 1) * GROUP)
                    act.activation(em[:, :, hs], em[:, :, hs], ACT.Exp).then_inc(em_done, 1)

                for n in range(END):
                    if n < UNITS:
                        exps(n)
                    if 0 <= n - LAG_T < UNITS:
                        evacuate(n - LAG_T)
                    g, r = divmod(n - LAG_PV - CPB + 2, GROUP * CPB)
                    if r == 0 and 0 < g <= GROUPS:
                        mask_shares(g - 1)
                        act.wait_ge(pv_done, b * GROUPS + g)
                        if g >= 3:
                            act.wait_ge(px_done, b * GROUPS + g - 2)
                        act.activation(pvs[:, (g - 1) % 2, :], pv[:, :], ACT.Copy).then_inc(pvs_done, 1)
                act.wait_ge(ot_ready, 2 * b + 1)
                act.activation(ot[:, 0, :], sc[0][:, :], ACT.Copy).then_inc(ot_act, 1)

        @block.vector
        def _(dve):
            dve.memset(vp[:, :, :, :], 0.0).then_inc(pad_done, 1)
            dve.wait_ge(w_hi_done, 1)
            dve.tensor_tensor(w_lo[:, :, :], w_raw[:, :, :], w_hi[:, :, :].bitcast(F32), ALU.subtract).then_inc(w_lo_done, 1)
            dve.wait_ge(prm_in, 64)
            dve.tensor_scalar(bias[:, 0:KT], bias[:, 0:KT], 0.25, None, ALU.mult).then_inc(bias_done, 1)
            dve.wait_ge(pad_done, 1)
            with dve.Fori(0, BATCH) as b:
                for m in range(KT):
                    dve.wait_ge(qk_done, b * 4 * KT + 3 * KT + m + 1)
                    hs = slice(m * HN // 2, (m + 1) * HN // 2)
                    dve.tensor_tensor(vp[:, :, hs, 0:HW],
                                      (pv, px)[m][:, :].rearrange("p (t h d) -> p t h d", t=CPB, d=HW),
                                      bv[:, m * P:(m + 1) * P].rearrange("p (h d) -> p h d", d=HW).unsqueeze(1)
                                      .broadcast_to([P, CPB, HN // 2, HW]), ALU.add).then_inc(vp_done, 1)
                for m in range(2 * KT):
                    dve.wait_ge(qk_hi_done, b * 2 * KT + m + 1)
                    hi, lo = (q_hi, q_lo) if m < KT else (k_hi, k_lo)
                    dve.tensor_tensor(lo[:, m % KT, :], full[:, m, :], hi[:, m % KT, :].bitcast(F32), ALU.subtract)\
                       .then_inc(qk_lo_done, 1)
                def maxima(u):
                    h, i = divmod(u, CPB)
                    dve.wait_ge(score_done, b * UNITS + u + 1)
                    dve.reduce_max(mx[:, i, h:h + 1], sc[u % 4][:, 0:(i + 1) * P], AX.X).then_inc(max_done, 1)

                def negate(u):
                    h, i = divmod(u, CPB)
                    dve.wait_ge(max_done, b * UNITS + u + 1)
                    dve.scalar_tensor_tensor(nm[:, i, h:h + 1], mx[:, i, h:h + 1], -1.0, floor[:, i:i + 1],
                                             ALU.mult, ALU.min).then_inc(nm_done, 1)

                def evacuate(u):
                    h, i = divmod(u, CPB)
                    if i < 2:
                        dve.wait_ge(tp_done, b * UNITS + u + 1)
                        if h >= 2 * GROUP and h % GROUP == 0:
                            dve.wait_ge(pv_done, b * GROUPS + h // GROUP - 1)
                        dve.tensor_copy(*p_tile(u)).then_inc(pt_dve, 1)

                def shares_in(g):
                    hs = slice(g * GROUP, (g + 1) * GROUP)
                    dve.wait_ge(nm_done, b * UNITS + (g + 1) * GROUP * CPB)
                    dve.tensor_scalar(em[:, :, hs], nm[:, :, hs], MASK_SCORE, MASK_SCORE, ALU.min, ALU.subtract)\
                       .then_inc(em_in, 1)

                def combine(g):
                    n = b * GROUPS + g
                    hs = slice(g * GROUP, (g + 1) * GROUP)
                    cols = slice(g * GROUP * HW, (g + 1) * GROUP * HW)
                    quad = [P, CPB, GROUP, HW]
                    dve.wait_ge(em_done, n + 1)
                    dve.tensor_tensor(den[:, :, hs], em[:, :, hs], count[:, :].unsqueeze(2).broadcast_to([P, CPB, GROUP]),
                                      ALU.mult).then_inc(den_done, 1)
                    ov = o[:, :, cols].rearrange("p i (h d) -> p i h d", d=HW)
                    dve.tensor_tensor(ov, sv[:, :, cols].rearrange("p i (h d) -> p i h d", d=HW),
                                      em[:, :, hs].unsqueeze(3).broadcast_to(quad), ALU.mult).then_inc(o_step, 1)
                    dve.wait_ge(den_done, 3 * n + 1)
                    dve.tensor_tensor(den[:, :, hs], den[:, :, hs], rs[:, :, hs], ALU.add).then_inc(den_done, 1)
                    dve.wait_ge(px_done, n + 1)
                    dve.wait_ge(o_step, 3 * n + 1)
                    dve.tensor_tensor(ov, px[:, :].rearrange("p (i h d) -> p i h d", i=CPB, h=GROUP)[:, :, :, 0:HW],
                                      ov, ALU.add).then_inc(o_step, 1)
                    dve.wait_ge(den_done, 3 * n + 2)
                    dve.reciprocal(den[:, :, hs], den[:, :, hs]).then_inc(den_done, 1)
                    dve.wait_ge(den_done, 3 * n + 3)
                    dve.wait_ge(o_step, 3 * n + 2)
                    dve.tensor_tensor(ov, ov, den[:, :, hs].unsqueeze(3).broadcast_to(quad), ALU.mult).then_inc(o_step, 1)

                for n in range(END):
                    if n < UNITS:
                        maxima(n)
                    if 0 <= n - LAG_T < UNITS:
                        evacuate(n - LAG_T)
                    if n < UNITS:
                        negate(n)
                    g, r = divmod(n + 1, GROUP * CPB)
                    if r == 0 and 0 < g <= GROUPS:
                        shares_in(g - 1)
                    g, r = divmod(n - LAG_X + 1, GROUP * CPB)
                    if r == 0 and 0 < g <= GROUPS:
                        combine(g - 1)
                dve.wait_ge(ot_ready, 2 * b + 2)
                dve.tensor_copy(ot[:, 1, :], sc[1][:, :]).then_inc(ot_dve, 1)
                dve.wait_ge(proj_done, b + 1)
                dve.wait_ge(s1_stored, 16 * b + 16)
                for i in range(CPB):
                    last = dve.tensor_tensor(s1[:, i, :], (sc[2], sc[3], tp[0], tp[1])[i][:, 0:DM], bo[:, :], ALU.add)
                last.then_inc(s1_done, 1)


EXPERTS, TOPK, FW = 32, 4, 96
INTER = 1024


def router_phase(nc, xt_hi, xt_lo, wg_dram, ident, wt_dram):
    with ExitStack() as ctx:
        sb = lambda n, s, d=F32: ctx.enter_context(nc.sbuf_tensor(f"ro_{n}", s, d))
        sem = ctx.enter_context(phase_semaphores(nc, "ro"))
        wr = sb("wr", [P, KT, EXPERTS])
        w_hi, w_lo = sb("w_hi", [P, KT, EXPERTS], F32R), sb("w_lo", [P, KT, EXPERTS], F32R)
        full = [P, NT, EXPERTS]
        l, gt, eq, pre = sb("l", full), sb("gt", full), sb("eq", full), sb("pre", full)
        keep = sb("keep", full)
        m8 = sb("m8", [P, NT, 8])
        m, s, need = sb("m", [P, NT]), sb("s", [P, NT]), sb("need", [P, NT])
        wt = sb("wt", [EXPERTS, T])
        pl = ctx.enter_context(nc.psum_tensor("ro_pl", full, F32))
        pw = [ctx.enter_context(nc.psum_tensor(f"ro_pw{i}", [EXPERTS, SEQ], F32)) for i in range(4)]
        bc = lambda ap: ap.unsqueeze(2).broadcast_to([P, NT, EXPERTS])
        STEP_WT = 19
        w_in, w_hi_done, w_lo_done, logits, step, max_done, exp_done, keep_done, turned, wt_done, stored = map(
            sem, "w_in w_hi_done w_lo_done logits step max_done exp_done keep_done turned wt_done stored".split())
        block = ctx.enter_context(nc.Block())

        @block.sync
        def _(sp):
            sp.dma_start(wr[:, :, :], wg_dram.rearrange("(k p) n -> p k n", p=P)).then_inc(w_in, 16)
            sp.wait_ge(wt_done, 4)
            sp.dma_start(wt_dram, wt[:, :]).then_inc(stored, 16)
            sp.wait_ge(stored, 16)

        @block.gpsimd
        def _(pool):
            pool.memset(keep[:, :, :], 1.0).then_inc(keep_done, 1)
            pool.wait_ge(keep_done, 1)
            pool.memset(keep[:, :, 0:1], 0.0).then_inc(keep_done, 1)

        @block.tensor
        def _(pe):
            pe.wait_ge(w_lo_done, 1)
            for t in range(NT):
                ts = slice(t * P, (t + 1) * P)
                last = split_matmuls(pe, pl[:, t, :], [xt_hi[:, k, ts] for k in range(KT)], [xt_lo[:, k, ts] for k in range(KT)],
                                     [w_hi[:, k, :] for k in range(KT)], [w_lo[:, k, :] for k in range(KT)])
            last.then_inc(logits, 1)
            pe.wait_ge(step, STEP_WT)
            for t in range(NT):
                last = pe.transpose(pw[t // 4][:, (t % 4) * P:(t % 4 + 1) * P], l[:, t, :], ident[:, :])
                if t % 4 == 3:
                    last.then_inc(turned, 1)

        @block.scalar
        def _(act):
            act.wait_ge(w_in, 16)
            act.activation(w_hi[:, :, :], wr[:, :, :], ACT.Copy).then_inc(w_hi_done, 1)
            act.wait_ge(step, 2)
            act.activation(l[:, :, :], l[:, :, :], ACT.Exp).then_inc(exp_done, 1)
            for q in range(4):
                act.wait_ge(turned, q + 1)
                act.activation(wt[:, q * SEQ:(q + 1) * SEQ], pw[q][:, :], ACT.Copy).then_inc(wt_done, 1)

        @block.vector
        def _(dve):
            n = [0]

            def then(ins):
                n[0] += 1
                ins.then_inc(step, 1)
                dve.wait_ge(step, n[0])

            dve.wait_ge(w_hi_done, 1)
            dve.tensor_tensor(w_lo[:, :, :], wr[:, :, :], w_hi[:, :, :].bitcast(F32), ALU.subtract).then_inc(w_lo_done, 1)
            dve.wait_ge(logits, 1)
            then(dve.reduce_max(m[:, :], pl[:, :, :], AX.X))
            then(dve.tensor_tensor(l[:, :, :], pl[:, :, :], bc(m[:, :]), ALU.subtract))
            dve.wait_ge(exp_done, 1)
            then(dve.reduce_sum(s[:, :], l[:, :, :], AX.X))
            then(dve.reciprocal(s[:, :], s[:, :]))
            then(dve.tensor_tensor(l[:, :, :], l[:, :, :], bc(s[:, :]), ALU.mult))
            for t in range(NT):
                last = dve.max(m8[:, t, :], l[:, t, :])
            then(last)
            fourth = m8[:, :, TOPK - 1]
            then(dve.tensor_copy(m[:, :], fourth))
            then(dve.tensor_tensor(gt[:, :, :], l[:, :, :], bc(m[:, :]), ALU.is_gt))
            then(dve.tensor_tensor(eq[:, :, :], l[:, :, :], bc(m[:, :]), ALU.is_equal))
            then(dve.reduce_sum(need[:, :], gt[:, :, :], AX.X))
            then(dve.tensor_scalar(need[:, :], need[:, :], -1.0, float(TOPK), ALU.mult, ALU.add))
            dve.wait_ge(keep_done, 2)
            flat = lambda ap: ap[:, :, :].rearrange("p t e -> p (t e)")
            then(dve.tensor_tensor_scan(flat(pre), flat(keep), flat(eq), 0.0, ALU.mult, ALU.add))
            then(dve.tensor_tensor(pre[:, :, :], pre[:, :, :], bc(need[:, :]), ALU.is_le))
            then(dve.tensor_tensor(eq[:, :, :], eq[:, :, :], pre[:, :, :], ALU.mult))
            then(dve.tensor_tensor(gt[:, :, :], gt[:, :, :], eq[:, :, :], ALU.add))
            then(dve.tensor_tensor(l[:, :, :], l[:, :, :], gt[:, :, :], ALU.mult))
            then(dve.reduce_sum(s[:, :], l[:, :, :], AX.X))
            then(dve.reciprocal(s[:, :], s[:, :]))
            then(dve.tensor_tensor(l[:, :, :], l[:, :, :], bc(s[:, :]), ALU.mult))
            assert n[0] == STEP_WT


def recurrent_layers(nc, x, w_xg, w_bcdt, conv_bc, dt_prm, prm, w_out, f0_gate, f0_up, f0_down,
                     w_qkv, b_qk, b_v, w_o, b_o, w_router, f1_gate, f1_up, f1_down, out):
    dram = lambda n, s: nc.dram_tensor(n, s, F32).ap()
    scratch = (dram("cum", [HEADS, T]), dram("ecum", [HEADS, T]), dram("last", [HEADS, NT]),
               dram("tables", [P, PAIRS * BATCH * 4 * CPB * 2]))
    gate0, s1, x1, w_tok = dram("gate0", [T, DM]), dram("s1", [T, DM]), dram("x1", [T, DM]), dram("w_tok", [EXPERTS, T])
    with ExitStack() as ctx:
        sb = lambda c, n, s, d=F32: c.enter_context(nc.sbuf_tensor(n, s, d))
        ident, causal = sb(ctx, "ident", [P, P]), sb(ctx, "causal", [P, P])
        xt_hi, xt_lo = sb(ctx, "xt_hi", [P, KT, T], F32R), sb(ctx, "xt_lo", [P, KT, T], F32R)
        constants_phase(nc, ident, causal)
        layernorm_phase(nc, "ln0", x, ident, xt_hi, xt_lo)
        gated_ffn_phase(nc, "ffn", INTER // P, f0_gate, f0_up, f0_down, xt_hi, xt_lo, gate0)
        with ExitStack() as mamba:
            out_acc, sq_acc = sb(mamba, "out_acc", [P, NT, DM]), sb(mamba, "sq_acc", [P, BATCH, SEQ])
            with ExitStack() as ssm:
                b_tok, c_t, cb_m = sb(ssm, "b_tok", [P, NT, NS]), sb(ssm, "c_t", [P, T]), sb(ssm, "cb_m", [P, NT, P])
                dynamics_phase(nc, xt_hi, xt_lo, w_bcdt, conv_bc, dt_prm, ident, causal, b_tok, c_t, cb_m, scratch)
                ssm_phase(nc, xt_hi, xt_lo, w_xg, w_out, prm, ident, b_tok, c_t, cb_m, scratch, out_acc, sq_acc)
            mamba_output_phase(nc, x, gate0, out_acc, sq_acc, x1)
        layernorm_phase(nc, "ln1", x1, ident, xt_hi, xt_lo)
        attention_phase(nc, xt_hi, xt_lo, w_qkv, b_qk, b_v, w_o, b_o, ident, s1)
        router_phase(nc, xt_hi, xt_lo, w_router, ident, w_tok)
        gated_ffn_phase(nc, "moe", EXPERTS * FW // P, f1_gate, f1_up, f1_down, xt_hi, xt_lo, out, router=(w_tok, FW),
                        residual=(x1, s1))


def kernel(**inputs):
    import numpy as np
    import concourse.bacc as bacc
    from concourse.bass_utils import run_bass_kernel_spmd

    a = {n: np.asarray(v) for n, v in inputs.items()}
    w = a["L0_attn_in_proj_w"]
    conv = np.concatenate([a["L0_attn_conv_w"], a["L0_attn_conv_b"][:, None]], 1)
    xg = np.concatenate([w[:, DI:2 * DI].reshape(KT, P, PAIRS, P), w[:, :DI].reshape(KT, P, PAIRS, P)], 3)
    w_dt = w[:, 2 * DI + 2 * NS:]
    d_rows = np.repeat(a["L0_attn_D_param"], HD)[:, None]
    gu0, gu1 = a["L0_ffn_w_gate_up"], a["L1_ffn_gate_up_proj"]
    laid = {
        "x": a["L0_attn_hidden_states"].reshape(T, DM),
        "w_xg": xg.transpose(2, 1, 0, 3).reshape(PAIRS, P, KT * 2 * P),
        "w_bcdt": np.concatenate([w[:, 2 * DI:2 * DI + 2 * NS], w_dt, w_dt], 1),
        "conv_bc": conv[DI:],
        "dt_prm": np.stack([a["L0_attn_dt_bias"], a["L0_attn_A_log"]], 1),
        "prm": np.concatenate([conv[:DI], d_rows], 1).reshape(PAIRS, P, 6),
        "w_out": np.concatenate([a["L0_attn_out_proj_w"], a["L0_attn_norm_w"][:, None]], 1).reshape(PAIRS, P, DM + 1),
        "f0_gate": gu0[:INTER].T, "f0_up": gu0[INTER:].T, "f0_down": a["L0_ffn_w_down"].T,
        "w_qkv": a["L1_attn_Wqkv"],
        "b_qk": a["L1_attn_bqkv"][:2 * DM].reshape(2 * KT, P).T, "b_v": a["L1_attn_bqkv"][2 * DM:][None],
        "w_o": a["L1_attn_Wo"], "b_o": a["L1_attn_bo"][None],
        "w_router": a["L1_ffn_gate"],
        "f1_gate": gu1[:, :, :FW].transpose(1, 0, 2).reshape(DM, EXPERTS * FW),
        "f1_up": gu1[:, :, FW:].transpose(1, 0, 2).reshape(DM, EXPERTS * FW),
        "f1_down": a["L1_ffn_down_proj"].reshape(EXPERTS * FW, DM),
    }
    nc = bacc.Bacc("TRN2", target_bir_lowering=False, num_devices=1)
    arrays, args = {}, []
    for name, v in laid.items():
        v = np.ascontiguousarray(v)
        arrays[f"in_{name}"] = v
        args.append(nc.dram_tensor(f"in_{name}", v.shape, mybir.dt.from_np(v.dtype), kind="ExternalInput").ap())
    args.append(nc.dram_tensor("result", (T, DM), F32, kind="ExternalOutput").ap())
    recurrent_layers(nc, *args)
    r = run_bass_kernel_spmd(nc, [arrays], core_ids=[0])
    return r.results[0]["result"].reshape(BATCH, SEQ, DM)
```

```python
import concourse.bass as bass
from concourse import mybir
from contextlib import ExitStack, contextmanager

F32 = mybir.dt.float32
F32R = mybir.dt.float32r
ALU = mybir.AluOpType
ACT = mybir.ActivationFunctionType
AX = mybir.AxisListType

P = 128
BATCH, SEQ, DM = 4, 512, 256
T = BATCH * SEQ
NT = T // P
KT = DM // P
CPB = SEQ // P
HEADS, HD, NS = 64, 64, 128
DI = HEADS * HD
PAIRS = HEADS // 2
DUOS = PAIRS // 2
UNITS = 2 * BATCH
EPS = 1e-5
MASKED = -3.0e38


@contextmanager
def phase_semaphores(nc, tag):
    taken = []

    def sem(name):
        taken.append(nc.alloc_semaphore(f"{tag}_{name}"))
        return taken[-1]
    yield sem
    nc.clear_and_free_semaphores(taken)
    nc.all_engine_barrier()


def split_matmuls(pe, out, w_hi, w_lo, x_hi, x_lo, seeded=False, more=False):
    n = len(w_hi)
    part = seeded or more
    for k in range(n):
        pe.matmul(out, w_hi[k], x_hi[k], start=(k == 0 and not seeded), stop=False, skip_group_check=part)
        pe.matmul(out, w_hi[k], x_lo[k], start=False, stop=False, skip_group_check=part)
        last = pe.matmul(out, w_lo[k], x_hi[k], start=False, stop=(k == n - 1 and not more), skip_group_check=part)
    return last


def layernorm_phase(nc, tag, x_dram, ident, xt_hi, xt_lo, x=None):
    G = 4
    PAIRT = NT // 2
    with ExitStack() as ctx:
        sb = lambda n, s, d=F32: ctx.enter_context(nc.sbuf_tensor(f"{tag}_{n}", s, d))
        sem = ctx.enter_context(phase_semaphores(nc, tag))
        loads = x is None
        if loads:
            x = sb("x", [P, NT, DM])
        xn = sb("xn", [P, NT, DM])
        stats = sb("stats", [P, NT, 6])
        mv = sb("mv", [P, NT, 2])
        veps = sb("veps", [P, NT])
        std = sb("std", [P, NT])
        rstd = sb("rstd", [P, NT])
        shift = sb("shift", [P, NT])
        pt = ctx.enter_context(nc.psum_tensor(f"{tag}_pt", [P, 4, KT, 2 * P], F32))
        x_in = [sem(f"x_in{g}") for g in range(NT // G)]
        stats_done, veps_done, std_done = sem("stats_done"), sem("veps_done"), sem("std_done")
        xn_odd_done = sem("xn_odd_done")
        xn_done, transposed, hi_done, lo_done = sem("xn_done"), sem("transposed"), sem("hi_done"), sem("lo_done")
        block = ctx.enter_context(nc.Block())
        xv = x_dram.rearrange("(t p) d -> p t d", p=P) if loads else None

        @block.sync
        def _(sp):
            for g in range(NT // G if loads else 0):
                sp.dma_start(x[:, g * G:(g + 1) * G, :], xv[:, g * G:(g + 1) * G, :]).then_inc(x_in[g], 16)

        @block.vector
        def _(dve):
            for t in range(NT):
                if loads and t % G == 0:
                    dve.wait_ge(x_in[t // G], 16)
                dve.bn_stats(stats[:, t, :], x[:, t, :]).then_inc(stats_done, 1)
            dve.wait_ge(stats_done, NT)
            for t in range(NT):
                dve.bn_aggr(mv[:, t, :], stats[:, t, :]).then_inc(stats_done, 1)
            dve.wait_ge(stats_done, 2 * NT)
            dve.tensor_scalar(veps[:, :], mv[:, :, 1], EPS, None, ALU.add).then_inc(veps_done, 1)
            dve.wait_ge(std_done, 1)
            dve.reciprocal(rstd[:, :], std[:, :]).then_inc(veps_done, 1)
            dve.wait_ge(veps_done, 2)
            dve.scalar_tensor_tensor(shift[:, :], mv[:, :, 0], -1.0, rstd[:, :], ALU.mult, ALU.mult).then_inc(veps_done, 1)

            def low_part(g):
                dve.wait_ge(hi_done, g + 1)
                dve.tensor_tensor(xt_lo[:, :, g * 2 * P:(g + 1) * 2 * P], pt[:, g % 4, :, :],
                                  xt_hi[:, :, g * 2 * P:(g + 1) * 2 * P].bitcast(F32),
                                  ALU.subtract).then_inc(lo_done, 1)

            for g in range(PAIRT):
                dve.tensor_scalar(xn[:, 2 * g, :], x[:, 2 * g, :], mv[:, 2 * g, 0:1], rstd[:, 2 * g:2 * g + 1],
                                  ALU.subtract, ALU.mult).then_inc(xn_done, 1)
                if g:
                    low_part(g - 1)
            low_part(PAIRT - 1)

        @block.tensor
        def _(pe):
            for g in range(PAIRT):
                pe.wait_ge(xn_done, g + 1)
                pe.wait_ge(xn_odd_done, g + 1)
                if g >= 4:
                    pe.wait_ge(lo_done, g - 3)
                for k in range(KT):
                    for t in range(2):
                        last = pe.transpose(pt[:, g % 4, k, t * P:(t + 1) * P],
                                            xn[:, 2 * g + t, k * P:(k + 1) * P], ident[:, :])
                last.then_inc(transposed, 1)

        @block.scalar
        def _(act):
            act.wait_ge(veps_done, 1)
            act.activation(std[:, :], veps[:, :], ACT.Sqrt).then_inc(std_done, 1)
            act.wait_ge(veps_done, 3)

            def odd_tile(g):
                t = 2 * g + 1
                act.activation(xn[:, t, :], x[:, t, :], ACT.Identity, bias=shift[:, t:t + 1], scale=rstd[:, t:t + 1])\
                   .then_inc(xn_odd_done, 1)

            odd_tile(0)
            odd_tile(1)
            for g in range(PAIRT):
                act.wait_ge(transposed, g + 1)
                act.activation(xt_hi[:, :, g * 2 * P:(g + 1) * 2 * P], pt[:, g % 4, :, :],
                               ACT.Copy).then_inc(hi_done, 1)
                if g + 2 < PAIRT:
                    odd_tile(g + 2)


def gated_ffn_phase(nc, tag, mt, wg_dram, wu_dram, wd_dram, xt_hi, xt_lo, gate_out, router=None, residual=None):
    with ExitStack() as ctx:
        sb = lambda n, s, d=F32: ctx.enter_context(nc.sbuf_tensor(f"{tag}_{n}", s, d))
        sem = ctx.enter_context(phase_semaphores(nc, tag))
        CH = 512
        TILES = CH // P
        w_hi = sb("w_hi", [P, 2 * KT, mt * P], F32R)
        w_lo = sb("w_lo", [P, 2 * KT, mt * P], F32R)
        wd_hi = sb("wd_hi", [P, mt, DM], F32R)
        wd_lo = sb("wd_lo", [P, mt, DM], F32R)
        RAW = 3
        w_raw = sb("w_raw", [P, RAW, CH])
        h = sb("h", [P, 2, SEQ])
        h_hi = sb("h_hi", [P, 2, SEQ], F32R)
        h_lo = sb("h_lo", [P, 2, SEQ], F32R)
        og = sb("og", [P, CPB, DM])
        wb = sb("wb", [P, 2, SEQ]) if router else None
        res = sb("res", [P, CPB, DM]) if residual else None
        pg = ctx.enter_context(nc.psum_tensor(f"{tag}_pg", [P, 2, SEQ], F32))
        pu = ctx.enter_context(nc.psum_tensor(f"{tag}_pu", [P, 2, SEQ], F32))
        po = ctx.enter_context(nc.psum_tensor(f"{tag}_po", [P, CPB, 512], F32))
        raw_in = [sem(f"raw_in{i}") for i in range(RAW)]
        w_hi_done, w_lo_done = sem("w_hi_done"), sem("w_lo_done")
        gate_ready, up_ready = sem("gate_ready"), sem("up_ready")
        silu_done = sem("silu_done")
        up_used = sem("up_used")
        h_ready = sem("h_ready") if router else up_used
        h_hi_done = sem("h_hi_done")
        h_lo_done = sem("h_lo_done")
        down_done = sem("down_done")
        out_used = sem("out_used")
        out_stored = sem("out_stored")
        wb_in = [sem(f"wb_in{i}") for i in range(2)] if router else None
        s_in, x_in, scaled, added = (sem(n) for n in ("s_in", "x_in", "scaled", "added"))
        block = ctx.enter_context(nc.Block())

        loads = []
        for c in range(mt // TILES):
            cols = slice(c * CH, (c + 1) * CH)
            for s in range(2):
                for k in range(KT):
                    i = s * KT + k
                    loads.append(((wg_dram, wu_dram)[s][k * P:(k + 1) * P, cols], w_hi[:, i, cols], w_lo[:, i, cols]))
            for m in range(c * TILES, (c + 1) * TILES, CH // DM):
                ms = slice(m, m + CH // DM)
                loads.append((wd_dram.rearrange("(m p) d -> p m d", p=P)[:, ms, :],
                              wd_hi[:, ms, :].rearrange("p m d -> p (m d)"), wd_lo[:, ms, :].rearrange("p m d -> p (m d)")))
        PER = len(loads) * TILES // mt
        batch_of = lambda dram, b: (dram.rearrange("(b t p) d -> b p t d", b=BATCH, p=P)[bass.ds(b, 1)]
                                    .rearrange("b p t d -> (b p) t d"))

        def due(m):
            c, q = divmod(m, TILES)
            return range(min(len(loads), PER * (c + 1) + -(-PER * q // TILES)),
                         min(len(loads), PER * (c + 1) + -(-PER * (q + 1) // TILES)))

        def pieces(m):
            width, r, out = router[1], m * P, []
            while r < (m + 1) * P:
                e = r // width
                end = min((e + 1) * width, (m + 1) * P)
                out.append((r - m * P, end - r, e))
                r = end
            return out

        arrived = [0, 0]
        wb_at = []
        for m in range(mt if router else 0):
            arrived[m % 2] += 16 * len(pieces(m))
            wb_at.append(arrived[m % 2])

        SCALE_AT, X_AT, ADD_AT, STORE_AT, S_AT = 0, 2, 4, 6, 8

        @block.sync
        def _(sp):
            def load(n):
                if n >= RAW:
                    sp.wait_ge(w_lo_done, n - RAW + 1)
                dst = w_raw[:, n % RAW, :]
                if n % PER >= 2 * KT:
                    dst = dst.rearrange("p (m d) -> p m d", d=DM)
                sp.dma_start(dst, loads[n][0]).then_inc(raw_in[n % RAW], 16)

            def router_weights(b, m):
                sp.wait_ge(h_ready, b * mt + m + 1)
                for r, n, e in pieces(m):
                    sp.dma_start(wb[r:r + n, m % 2, :], router[0][e:e + 1, bass.ds(b * SEQ, SEQ)].broadcast_to([n, SEQ]))\
                      .then_inc(wb_in[m % 2], 16)

            for n in range(PER):
                load(n)
            for m in range(mt):
                for n in due(m):
                    load(n)
                if router:
                    router_weights(0, m)
            if router:
                with sp.Fori(1, BATCH) as b:
                    for m in range(mt):
                        router_weights(b, m)

        @block.tensor
        def _(pe):
            pe.sem_inc(silu_done, 2)
            pe.sem_inc(up_used, 2)
            pe.sem_inc(down_done, 2)
            pe.sem_inc(h_lo_done, 2)
            pe.sem_inc(out_used, 1)
            if router:
                pe.sem_inc(h_ready, 2)

            def hidden(b, m):
                c = slice(m * P, (m + 1) * P)
                xs_hi = [xt_hi[:, k, bass.ds(b * SEQ, SEQ)] for k in range(KT)]
                xs_lo = [xt_lo[:, k, bass.ds(b * SEQ, SEQ)] for k in range(KT)]
                for s, (bank, used, ready) in enumerate(((pg, silu_done, gate_ready), (pu, up_used, up_ready))):
                    if isinstance(b, int) and m % TILES == 0:
                        pe.wait_ge(w_lo_done, PER * (m // TILES) + (s + 1) * KT)
                    pe.wait_ge(used, b * mt + m + 1)
                    split_matmuls(pe, bank[:, m % 2, :], [w_hi[:, s * KT + k, c] for k in range(KT)],
                                  [w_lo[:, s * KT + k, c] for k in range(KT)], xs_hi, xs_lo).then_inc(ready, 1)

            def down(b, m):
                if isinstance(b, int):
                    pe.wait_ge(w_lo_done, PER * (m // TILES) + 2 * KT + m % TILES * DM // CH + 1)
                pe.wait_ge(h_lo_done, b * mt + m + 3)
                if m == 0:
                    pe.wait_ge(out_used, b + 1)
                for t in range(CPB):
                    ts = slice(t * P, (t + 1) * P)
                    last = split_matmuls(pe, po[:, t, 0:DM], [h_hi[:, m % 2, ts]], [h_lo[:, m % 2, ts]],
                                         [wd_hi[:, m, :]], [wd_lo[:, m, :]], seeded=(m > 0), more=(m < mt - 1))
                last.then_inc(down_done, 1)

            def batch(b):
                for m in range(mt):
                    hidden(b, m)
                    if m:
                        down(b, m - 1)
                down(b, mt - 1)

            batch(0)
            with pe.Fori(1, BATCH) as b:
                batch(b)

        @block.scalar
        def _(act):
            def split_high(n):
                act.wait_ge(raw_in[n % RAW], 16 * (n // RAW + 1))
                act.activation(loads[n][1], w_raw[:, n % RAW, :], ACT.Copy).then_inc(w_hi_done, 1)

            def load_s(b):
                if not isinstance(b, int) or b > 0:
                    act.wait_ge(added, b)
                act.dma_start(res[:, :, :], batch_of(residual[1], b)).then_inc(s_in, 16)

            def load_x(b):
                act.wait_ge(scaled, b + 1)
                act.dma_start(res[:, :, :], batch_of(residual[0], b)).then_inc(x_in, 16)

            def store(b):
                act.wait_ge(added if residual else out_used, b + (1 if residual else 2))
                act.dma_start(batch_of(gate_out, b), og[:, :, :]).then_inc(out_stored, 16)

            def batch(b):
                for m in range(mt):
                    act.wait_ge(gate_ready, b * mt + m + 1)
                    act.wait_ge(h_lo_done, b * mt + m + 1)
                    act.activation(h[:, m % 2, :], pg[:, m % 2, :], ACT.Silu).then_inc(silu_done, 1)
                    act.wait_ge(h_ready, b * mt + m + 3)
                    act.wait_ge(down_done, b * mt + m + 1)
                    act.activation(h_hi[:, m % 2, :], h[:, m % 2, :], ACT.Copy).then_inc(h_hi_done, 1)
                    if isinstance(b, int):
                        for n in due(m):
                            split_high(n)
                    if residual:
                        if m == X_AT and not isinstance(b, int):
                            load_x(b - 1)
                        if m == STORE_AT and not isinstance(b, int):
                            store(b - 1)
                        if m == S_AT:
                            load_s(b)
                act.wait_ge(down_done, b * mt + mt + 2)
                act.wait_ge(out_stored, 16 * b + 16)
                act.activation(og[:, :, :], po[:, :, 0:DM], ACT.Silu).then_inc(out_used, 1)
                if not residual:
                    store(b)

            act.sem_inc(out_stored, 16)
            for n in range(PER):
                split_high(n)
            batch(0)
            with act.Fori(1, BATCH) as b:
                batch(b)
            if residual:
                load_x(BATCH - 1)
                store(BATCH - 1)
            act.wait_ge(out_stored, 16 * (BATCH + 1))

        @block.vector
        def _(dve):
            def split_low(n):
                dve.wait_ge(w_hi_done, n + 1)
                dve.tensor_tensor(loads[n][2], w_raw[:, n % RAW, :], loads[n][1].bitcast(F32), ALU.subtract)\
                   .then_inc(w_lo_done, 1)

            def scale(b):
                dve.wait_ge(out_used, b + 2)
                dve.wait_ge(s_in, 16 * (b + 1))
                dve.tensor_tensor(og[:, :, :], og[:, :, :], res[:, :, :], ALU.mult).then_inc(scaled, 1)

            def add(b):
                dve.wait_ge(scaled, b + 1)
                dve.wait_ge(x_in, 16 * (b + 1))
                dve.tensor_tensor(og[:, :, :], og[:, :, :], res[:, :, :], ALU.add).then_inc(added, 1)

            def batch(b):
                for m in range(mt):
                    dve.wait_ge(up_ready, b * mt + m + 1)
                    dve.wait_ge(silu_done, b * mt + m + 3)
                    dve.tensor_tensor(h[:, m % 2, :], pu[:, m % 2, :], h[:, m % 2, :], ALU.mult).then_inc(up_used, 1)
                    if router:
                        dve.wait_ge(up_used, b * mt + m + 3)
                        dve.wait_ge(wb_in[m % 2], b * arrived[m % 2] + wb_at[m])
                        dve.tensor_tensor(h[:, m % 2, :], h[:, m % 2, :], wb[:, m % 2, :], ALU.mult)\
                           .then_inc(h_ready, 1)
                    dve.wait_ge(h_hi_done, b * mt + m + 1)
                    dve.wait_ge(down_done, b * mt + m + 1)
                    dve.tensor_tensor(h_lo[:, m % 2, :], h[:, m % 2, :], h_hi[:, m % 2, :].bitcast(F32), ALU.subtract)\
                       .then_inc(h_lo_done, 1)
                    if isinstance(b, int):
                        for n in due(m):
                            split_low(n)
                    elif residual:
                        if m == SCALE_AT:
                            scale(b - 1)
                        if m == ADD_AT:
                            add(b - 1)

            for n in range(PER):
                split_low(n)
            batch(0)
            with dve.Fori(1, BATCH) as b:
                batch(b)
            if residual:
                scale(BATCH - 1)
                add(BATCH - 1)


def dynamics_phase(nc, xt_hi, xt_lo, w_bcdt, conv_bc, dt_prm, ident, causal, b_tok, c_t, cb_m, scratch, out_acc, sq_acc):
    cum_d, ecum_d, last_d, tab_d = scratch
    with ExitStack() as ctx:
        sb = lambda n, s, d=F32: ctx.enter_context(nc.sbuf_tensor(f"dyn_{n}", s, d))
        sem = ctx.enter_context(phase_semaphores(nc, "dyn"))
        W = 3 * P
        w_raw = sb("w_raw", [P, KT, W])
        w_hi = sb("w_hi", [P, KT, W], F32R)
        w_lo = sb("w_lo", [P, KT, W], F32R)
        cp = sb("cp", [P, 2, 5])
        dp = sb("dp", [P, 2])
        a_neg = sb("a_neg", [P, 1])
        y = sb("y", [P, 2, SEQ])
        b_t = sb("b_t", [P, T])
        v = sb("v", [P, T // 2])
        av = sb("av", [P, T // 2])
        u = sb("u", [P, T // 2])
        z = sb("z", [P, T // 2])
        dt_t = sb("dt_t", [P, T // 2])
        keep = sb("keep", [P, T // 2])
        cum = sb("cum", [P, T // 2])
        ecum = sb("ecum", [P, T // 2])
        wst = sb("wst", [P, T // 2])
        last = sb("last", [P, NT // 2])
        last_b = sb("last_b", [P, HEADS, NT])
        tab = sb("tab", [P, PAIRS, BATCH, 4, CPB, 2])
        pp = [ctx.enter_context(nc.psum_tensor(f"dyn_pp{i}", [P, SEQ], F32)) for i in range(3)]
        pt = [ctx.enter_context(nc.psum_tensor(f"dyn_pt{i}", [P, SEQ], F32)) for i in range(4)]
        w_in, prm_in = sem("w_in"), sem("prm_in")
        whi, wlo, proj = sem("whi"), sem("wlo"), sem("proj")
        conv0, taps, bc_ready, v_ready = sem("conv0"), sem("taps"), sem("bc_ready"), sem("v_ready")
        scal, vec = sem("scal"), sem("vec")
        keep_done, tr, ev, cbd, cbe = sem("keep_done"), sem("tr"), sem("ev"), sem("cbd"), sem("cbe")
        out_c, last_out, last_in, zeroed = sem("out_c"), sem("last_out"), sem("last_in"), sem("zeroed")
        block = ctx.enter_context(nc.Block())
        halves = [(slice(i * HEADS, (i + 1) * HEADS), slice(i * T // 2, (i + 1) * T // 2)) for i in range(2)]
        chunks = lambda ap: ap.rearrange("p (c t) -> p c t", t=P)

        SC_AEXP, SC_ABS, SC_EXP, SC_LN, SC_LAST, SC_ECUM, SC_WST = range(1, 8)
        (VEC_ANEG, VEC_U, VEC_D, VEC_Z, VEC_NUM, VEC_DEN, VEC_REC, VEC_NUM2, VEC_Q, VEC_DT, VEC_DA,
         VEC_CUM, VEC_DIFF) = range(1, 14)

        @block.sync
        def _(sp):
            sp.dma_start(w_raw[:, :, :], w_bcdt.rearrange("(k p) n -> p k n", p=P)).then_inc(w_in, 16)
            sp.dma_start(cp[:, :, :], conv_bc.rearrange("(s p) n -> p s n", p=P)).then_inc(prm_in, 16)
            for rows, _ in halves:
                sp.dma_start(dp[rows, :], dt_prm).then_inc(prm_in, 16)
            sp.wait_ge(scal, SC_LAST)
            for i, (rows, _) in enumerate(halves):
                sp.dma_start(last_d[:, i * NT // 2:(i + 1) * NT // 2], last[rows, :]).then_inc(last_out, 16)
            sp.wait_ge(last_out, 32)
            sp.dma_start(last_b[:, :, :].rearrange("p h c -> p (h c)"),
                         last_d.rearrange("(a h) c -> a (h c)", a=1).broadcast_to([P, HEADS * NT])).then_inc(last_in, 16)
            sp.wait_ge(vec, VEC_CUM)
            for rows, cols in halves:
                sp.dma_start(cum_d[:, cols], cum[rows, :]).then_inc(out_c, 16)
            sp.wait_ge(scal, SC_ECUM)
            for rows, cols in halves:
                sp.dma_start(ecum_d[:, cols], ecum[rows, :]).then_inc(out_c, 16)
            sp.wait_ge(ev, 4 * BATCH)
            sp.dma_start(tab_d, tab[:, :, :, :, :, :].rearrange("p k b f c e -> p (k b f c e)")).then_inc(out_c, 16)
            sp.wait_ge(out_c, 80)

        @block.gpsimd
        def _(pool):
            pool.memset(keep[:, :], 1.0).then_inc(keep_done, 1)
            pool.wait_ge(keep_done, 1)
            pool.memset(chunks(keep[:, :])[:, :, 0:1], 0.0).then_inc(keep_done, 1)
            pool.memset(out_acc[:, :, :], 0.0).then_inc(zeroed, 1)
            pool.memset(sq_acc[:, :, :], 0.0).then_inc(zeroed, 1)

        @block.tensor
        def _(pe):
            pe.wait_ge(wlo, 1)
            for b in range(BATCH):
                xs = slice(b * SEQ, (b + 1) * SEQ)
                for s in range(3):
                    if b:
                        pe.wait_ge(*((taps, 3 * (2 * (b - 1) + s + 1)) if s < 2 else (v_ready, b)))
                    c = slice(s * P, (s + 1) * P)
                    split_matmuls(pe, pp[s][:, :], [w_hi[:, k, c] for k in range(KT)],
                                  [w_lo[:, k, c] for k in range(KT)], [xt_hi[:, k, xs] for k in range(KT)],
                                  [xt_lo[:, k, xs] for k in range(KT)]).then_inc(proj, 1)
            for b in range(BATCH):
                pe.wait_ge(bc_ready, 2 * b + 2)
                if b >= 2:
                    pe.wait_ge(cbe, 2 * (b - 1))
                for c in range(CPB):
                    t = slice((b * CPB + c) * P, (b * CPB + c + 1) * P)
                    m = pe.transpose(pt[b % 2][:, c * P:(c + 1) * P], b_t[:, t], ident[:, :])
                m.then_inc(cbd, 1)
                for c in range(CPB):
                    t = slice((b * CPB + c) * P, (b * CPB + c + 1) * P)
                    m = pe.matmul(pt[2 + b % 2][:, c * P:(c + 1) * P], b_t[:, t], c_t[:, t], start=True, stop=True)
                m.then_inc(cbd, 1)
            n = 0
            pe.wait_ge(cbe, 2 * BATCH)
            for f, (src, sm, at) in enumerate(((cum, vec, VEC_CUM), (dt_t, vec, VEC_DT), (wst, scal, SC_WST))):
                pe.wait_ge(sm, at)
                for q in range(BATCH // 2):
                    if n >= 4:
                        pe.wait_ge(ev, 2 * (n - 3))
                    for c in range(CPB):
                        t = slice((q * CPB + c) * P, (q * CPB + c + 1) * P)
                        m = pe.transpose(pt[n % 4][:, c * P:(c + 1) * P], src[:, t], ident[:, :])
                    m.then_inc(tr, 1)
                    n += 1

        def field(f, q, i):
            src = pt[(2 * f + q) % 4][:, :].rearrange("p (c i k e) -> p c i k e", c=CPB, i=2, e=2)[:, :, i, :, :]
            return tab[:, :, q + 2 * i, f, :, :].rearrange("p k c e -> p c k e"), src

        @block.scalar
        def _(act):
            act.wait_ge(w_in, 16)
            act.activation(w_hi[:, :, :], w_raw[:, :, :], ACT.Copy).then_inc(whi, 1)
            act.wait_ge(prm_in, 48)
            act.activation(a_neg[:, :], dp[:, 1:2], ACT.Exp).then_inc(scal, 1)

            def conv_silu(b, s):
                n = 2 * b + s
                act.wait_ge(taps, 3 * (n + 1))
                act.activation((b_t if s == 0 else c_t)[:, b * SEQ:(b + 1) * SEQ], y[:, s, :], ACT.Silu)\
                   .then_inc(bc_ready, 1)

            for b in range(BATCH):
                for s in range(2):
                    act.wait_ge(proj, 3 * b + s + 1)
                    if b:
                        act.wait_ge(bc_ready, 2 * (b - 1) + s + 1)
                    act.activation(y[:, s, :], pp[s][:, :], ACT.Identity, bias=cp[:, s, 4:5], scale=cp[:, s, 3:4])\
                       .then_inc(conv0, 1)
                act.wait_ge(proj, 3 * b + 3)
                rows = halves[b // 2][0]
                act.activation(v[rows, b % 2 * SEQ:(b % 2 + 1) * SEQ], pp[2][rows, :], ACT.Identity, bias=dp[rows, 0:1])\
                   .then_inc(v_ready, 1)
                conv_silu(b, 0)
                conv_silu(b, 1)
            act.wait_ge(v_ready, BATCH)
            act.activation(av[:, :], v[:, :], ACT.Abs).then_inc(scal, 1)
            act.wait_ge(scal, SC_ABS)
            act.activation(av[:, :], av[:, :], ACT.Exp, scale=-1.0).then_inc(scal, 1)
            act.wait_ge(vec, VEC_U)
            act.activation(z[:, :], u[:, :], ACT.Ln).then_inc(scal, 1)
            act.wait_ge(vec, VEC_CUM)
            act.activation(last[:, :], chunks(cum[:, :])[:, :, P - 1], ACT.Exp).then_inc(scal, 1)
            act.activation(ecum[:, :], cum[:, :], ACT.Exp).then_inc(scal, 1)
            act.wait_ge(vec, VEC_DIFF)
            act.activation(wst[:, :], wst[:, :], ACT.Exp).then_inc(scal, 1)
            for q in range(BATCH // 2):
                act.wait_ge(tr, q + 1)
                for i in range(2):
                    act.activation(*field(0, q, i), ACT.Copy, scale=-1.0).then_inc(ev, 1)

        @block.vector
        def _(dve):
            dve.wait_ge(whi, 1)
            dve.tensor_tensor(w_lo[:, :, :], w_raw[:, :, :], w_hi[:, :, :].bitcast(F32), ALU.subtract).then_inc(wlo, 1)
            dve.wait_ge(scal, SC_AEXP)
            dve.tensor_scalar(a_neg[:, :], a_neg[:, :], -1.0, None, ALU.mult).then_inc(vec, 1)
            for b in range(BATCH):
                for s in range(2):
                    n = 2 * b + s
                    dve.wait_ge(conv0, n + 1)
                    for j in range(1, 4):
                        if j > 1:
                            dve.wait_ge(taps, 3 * n + j - 1)
                        dve.scalar_tensor_tensor(y[:, s, j:SEQ], pp[s][:, 0:SEQ - j], cp[:, s, 3 - j:4 - j],
                                                 y[:, s, j:SEQ], ALU.mult, ALU.add).then_inc(taps, 1)
            def take_b(b):
                dve.wait_ge(cbd, 2 * b + 1)
                dve.tensor_copy(b_tok[:, b * CPB:(b + 1) * CPB, :],
                                pt[b % 2][:, :].rearrange("p (c n) -> p c n", n=NS)).then_inc(cbe, 1)
                dve.wait_ge(cbd, 2 * b + 2)
                dve.tensor_tensor(cb_m[:, b * CPB:(b + 1) * CPB, :],
                                  pt[2 + b % 2][:, :].rearrange("p (c n) -> p c n", n=P),
                                  causal[:, :].unsqueeze(1).broadcast_to([P, CPB, P]), ALU.mult).then_inc(cbe, 1)

            take_b(0)
            take_b(1)
            dve.wait_ge(scal, SC_EXP)
            dve.tensor_scalar(u[:, :], av[:, :], 1.0, None, ALU.add).then_inc(vec, 1)
            take_b(2)
            take_b(3)
            dve.wait_ge(scal, SC_LN)
            dve.wait_ge(vec, VEC_U)
            dve.tensor_scalar(u[:, :], u[:, :], 1.0, None, ALU.subtract).then_inc(vec, 1)
            dve.wait_ge(vec, VEC_D)
            dve.tensor_scalar(cum[:, :], u[:, :], 0.0, None, ALU.is_equal).then_inc(vec, 1)
            dve.wait_ge(vec, VEC_Z)
            dve.tensor_tensor(z[:, :], z[:, :], cum[:, :], ALU.add).then_inc(vec, 1)
            dve.tensor_tensor(u[:, :], u[:, :], cum[:, :], ALU.add).then_inc(vec, 1)
            dve.wait_ge(vec, VEC_DEN)
            dve.reciprocal(u[:, :], u[:, :]).then_inc(vec, 1)
            dve.tensor_tensor(z[:, :], z[:, :], av[:, :], ALU.mult).then_inc(vec, 1)
            dve.wait_ge(vec, VEC_NUM2)
            dve.tensor_tensor(z[:, :], z[:, :], u[:, :], ALU.mult).then_inc(vec, 1)
            dve.wait_ge(vec, VEC_Q)
            dve.scalar_tensor_tensor(dt_t[:, :], v[:, :], 0.0, z[:, :], ALU.max, ALU.add).then_inc(vec, 1)
            dve.wait_ge(vec, VEC_DT)
            dve.tensor_scalar(v[:, :], dt_t[:, :], a_neg[:, :], None, ALU.mult).then_inc(vec, 1)
            dve.wait_ge(vec, VEC_DA)
            dve.wait_ge(keep_done, 2)
            dve.tensor_tensor_scan(cum[:, :], keep[:, :], v[:, :], 0.0, ALU.mult, ALU.add).then_inc(vec, 1)
            dve.wait_ge(vec, VEC_CUM)
            cc = chunks(cum[:, :])
            dve.tensor_tensor(chunks(wst[:, :]), cc[:, :, P - 1:P].broadcast_to([P, NT // 2, P]), cc,
                              ALU.subtract).then_inc(vec, 1)
            for n in range(2, 6):
                dve.wait_ge(tr, n + 1)
                dve.wait_ge(ev, 2 * n)
                for i in range(2):
                    dve.tensor_copy(*field(n // 2, n % 2, i)).then_inc(ev, 1)
            dve.wait_ge(last_in, 16)
            for b in range(BATCH):
                src = last_b[:, :, b * CPB:(b + 1) * CPB].rearrange("p (k e) c -> p c k e", e=2)
                dve.tensor_copy(tab[:, :, b, 3, :, :].rearrange("p k c e -> p c k e"), src).then_inc(ev, 1)


def wait(eng, sem, count):
    if not isinstance(count, int) or count > 0:
        eng.wait_ge(sem, count)


def pipeline(eng, *stages):
    def slots(k):
        for j in range(UNITS):
            for stage, lag in stages:
                q, s = divmod(j - lag, UNITS)
                duo = k + q
                if not isinstance(k, int) or 0 <= duo < DUOS:
                    stage(duo, s)
    slots(-1)
    slots(0)
    with eng.Fori(1, DUOS - 1) as k:
        slots(k)
    slots(DUOS - 1)
    slots(DUOS)


def even(stage):
    def even_units(k, j):
        if j % 2 == 0:
            stage(k, j)
    return even_units


def odd(stage):
    def odd_units(k, j):
        if j % 2 == 1:
            stage(k, j)
    return odd_units


def ssm_phase(nc, xt_hi, xt_lo, w_dram, wo_dram, prm_dram, ident, b_tok, c_t, cb_m, scratch, out_acc, sq_acc):
    cum_d, ecum_d, last_d, tab_d = scratch
    with ExitStack() as ctx:
        sb = lambda n, s, d=F32: ctx.enter_context(nc.sbuf_tensor(f"ssm_{n}", s, d))
        sem = ctx.enter_context(phase_semaphores(nc, "ssm"))
        pb = lambda n, w=SEQ: ctx.enter_context(nc.psum_tensor(f"ssm_{n}", [P, w], F32))
        R = 4
        L = UNITS
        w_raw = sb("w_raw", [P, 2, KT, 2 * P])
        w_hi = sb("w_hi", [P, 2, KT, 2 * P], F32R)
        w_lo = sb("w_lo", [P, 2, KT, 2 * P], F32R)
        wo_raw = sb("wo_raw", [P, 2, DM + 1])
        wo_hi, wo_lo = sb("wo_hi", [P, 2, DM], F32R), sb("wo_lo", [P, 2, DM], F32R)
        prm = sb("prm", [P, L, 6])
        tab = sb("tab", [P, L, 4, CPB * 2])
        cm = sb("cm", [P, L, 2, SEQ])
        er = sb("er", [P, R, SEQ - P])
        y = sb("y", [P, 2, SEQ])
        xs = sb("xs", [P, R, SEQ])
        sg = sb("sg", [P, L, SEQ])
        xdt = sb("xdt", [P, R, SEQ])
        xw = sb("xw", [P, 2, SEQ - P])
        S = sb("S", [P, 2, CPB - 1, P])
        t1 = sb("t1", [P, 2, SEQ - P])
        t2 = sb("t2", [P, R, SEQ])
        h = t2
        h_hi, h_lo = sb("h_hi", [P, 2, SEQ], F32R), sb("h_lo", [P, 2, SEQ], F32R)
        sq = sb("sq", [P, 2, SEQ])
        px, pg, pt, pyd, pst, pyo = (pb(n) for n in ("px", "pg", "pt", "pyd", "pst", "pyo"))
        po = pb("po", CPB * DM)
        names = ("w_in wo_in w_hi_done w_ready wo_ready x_ready g_ready conv0_done taps_done gate_done xs_ready "
                 "tr_done xdt_ready xw_ready masked exp_done m_ready yd_done st_done s1_done rec_done yo_done "
                 "t2_done t1_done hs_done h_ready sq_done acc_done out_done oacc_done mask_begun "
                 "wo_scaled wo_hi_done h_hi_done h_lo_done")
        (w_in, wo_in, w_hi_done, w_ready, wo_ready, x_ready, g_ready, conv0_done, taps_done, gate_done, xs_ready,
         tr_done, xdt_ready, xw_ready, masked, exp_done, m_ready, yd_done, st_done, s1_done, rec_done, yo_done,
         t2_done, t1_done, hs_done, h_ready, sq_done, acc_done, out_done, oacc_done, mask_begun,
         wo_scaled, wo_hi_done, h_hi_done, h_lo_done) = map(sem, names.split())
        prm_in, tab_in, cm_in = ([sem(f"{n}{b}") for b in range(L)] for n in ("prm_in", "tab_in", "cm_in"))
        er_in = [sem(f"er_in{b}") for b in range(R)]
        block = ctx.enter_context(nc.Block())

        def N(k, j):
            return UNITS * k + j + 1

        def turn(k, j):
            return k + 1

        @block.sync
        def _(sp):
            def weights(k, j):
                if j == 0:
                    wait(sp, w_ready, 2 * k)
                    sp.dma_start(w_raw[:, :, :, :].rearrange("p e k n -> p e (k n)"),
                                 w_dram[bass.ds(2 * k, 2)].rearrange("e p n -> p e n")).then_inc(w_in, 16)

            def out_weights(k, j):
                if j == 1:
                    wait(sp, wo_ready, k)
                    sp.dma_start(wo_raw[:, :, :], wo_dram[bass.ds(2 * k, 2)].rearrange("e p n -> p e n"))\
                      .then_inc(wo_in, 16)

            def tables(k, j):
                n, b, e = N(k, j), j // 2, j % 2
                pair = 2 * k + e
                wait(sp, rec_done, 2 * (n - L))
                wait(sp, t2_done, n - L)
                sp.dma_start(prm[:, j, :], prm_dram[bass.ds(pair, 1)].rearrange("a p n -> (a p) n")).then_inc(prm_in[j], 16)
                sp.dma_start(tab[:, j].rearrange("p f n -> p (f n)"),
                             tab_d[:, bass.ds((pair * BATCH + b) * 32, 32)]).then_inc(tab_in[j], 16)
                wait(sp, yd_done, n - L)
                sp.dma_start(cm[:, j, :, :], cum_d[bass.ds(2 * pair, 2), b * SEQ:(b + 1) * SEQ].unsqueeze(0)
                             .broadcast_to([P, 2, SEQ])).then_inc(cm_in[j], 16)

            def exp_cum(k, j):
                r, b, pair = j % R, j // 2, 2 * k + j % 2
                wait(sp, t1_done, N(k, j) - R)
                for i in range(2):
                    sp.dma_start(er[i * HD:(i + 1) * HD, r, :],
                                 ecum_d[bass.ds(2 * pair + i, 1), b * SEQ + P:(b + 1) * SEQ].broadcast_to([HD, SEQ - P]))\
                      .then_inc(er_in[r], 16)

            pipeline(sp, (weights, -6), (out_weights, 0), (tables, 0), (exp_cum, 2))

        @block.tensor
        def _(pe):
            def project(k, j, s, bank, done, used, at):
                c = slice(s * P, (s + 1) * P)
                cols = slice(j // 2 * SEQ, (j // 2 + 1) * SEQ)
                if j < 2:
                    pe.wait_ge(w_ready, 2 * k + j + 1)
                wait(pe, used, at)
                split_matmuls(pe, bank[:, :], [w_hi[:, j % 2, i, c] for i in range(KT)],
                              [w_lo[:, j % 2, i, c] for i in range(KT)], [xt_hi[:, i, cols] for i in range(KT)],
                              [xt_lo[:, i, cols] for i in range(KT)]).then_inc(done, 1)

            def project_x(k, j):
                project(k, j, 0, px, x_ready, taps_done, 3 * (N(k, j) - 1))

            def project_gate(k, j):
                project(k, j, 1, pg, g_ready, gate_done, N(k, j) - 1)

            def transposes(k, j):
                n = N(k, j)
                pe.wait_ge(xs_ready, n)
                wait(pe, xdt_ready, n - 1)
                for c in range(CPB):
                    last = pe.transpose(pt[:, c * P:(c + 1) * P], xs[:, j % R, c * P:(c + 1) * P], ident[:, :])
                last.then_inc(tr_done, 1)

            def y_diag(k, j):
                n = N(k, j)
                pe.wait_ge(m_ready, n)
                pe.wait_ge(xdt_ready, n)
                wait(pe, t2_done, n - 1)
                for c in range(CPB):
                    for e in range(2):
                        t = slice(c * P, (c + 1) * P)
                        last = pe.matmul(pyd[e * HD:(e + 1) * HD, t], xdt[:, j % R, c * P + e * HD:c * P + (e + 1) * HD],
                                         cm[:, j, e, t], start=True, stop=True)
                last.then_inc(yd_done, 1)

            def states(k, j):
                n = N(k, j)
                pe.wait_ge(xw_ready, n)
                wait(pe, rec_done, 2 * (n - 1))
                wait(pe, s1_done, n - 1)
                for c in range(CPB - 1):
                    t = slice(c * P, (c + 1) * P)
                    last = pe.matmul(pst[:, t], b_tok[:, j // 2 * CPB + c, :], xw[:, j % 2, t], start=True, stop=True)
                last.then_inc(st_done, 1)

            def y_off(k, j):
                n = N(k, j)
                pe.wait_ge(rec_done, 2 * n)
                pe.wait_ge(s1_done, n)
                wait(pe, t1_done, n - 1)
                for c in range(1, CPB):
                    t = (j // 2 * CPB + c) * P
                    last = pe.matmul(pyo[:, (c - 1) * P:c * P], S[:, j % 2, c - 1, :], c_t[:, t:t + P],
                                     start=True, stop=True)
                last.then_inc(yo_done, 1)

            def project_out(k, j):
                n, e = N(k, j), j % 2
                if j == 0:
                    pe.wait_ge(wo_ready, k + 1)
                pe.wait_ge(h_lo_done, n)
                if e == 0:
                    wait(pe, oacc_done, BATCH * k + j // 2)
                for c in range(CPB):
                    cs = slice(c * P, (c + 1) * P)
                    last = split_matmuls(pe, po[:, c * DM:(c + 1) * DM], [h_hi[:, j % 2, cs]], [h_lo[:, j % 2, cs]],
                                         [wo_hi[:, e, :]], [wo_lo[:, e, :]], seeded=(e == 1 or c % 2 == 1), more=(e == 0))
                last.then_inc(out_done, 1)

            pipeline(pe, (project_x, 0), (odd(project_gate), 0), (y_off, 4), (states, 3), (transposes, 2), (y_diag, 3),
                     (project_out, 6), (even(project_gate), 0))

        @block.scalar
        def _(act):
            def split_high(k, j):
                if j < 2:
                    act.wait_ge(w_in, 16 * (k + 1))
                    wait(act, g_ready, UNITS * k - 1 + j)
                    act.activation(w_hi[:, j, :, :], w_raw[:, j, :, :], ACT.Copy).then_inc(w_hi_done, 1)

            def conv_first(k, j):
                n = N(k, j)
                act.wait_ge(x_ready, n)
                act.wait_ge(prm_in[j], 16 * turn(k, j))
                wait(act, xs_ready, n - 2)
                act.activation(y[:, j % 2, :], px[:, :], ACT.Identity, bias=prm[:, j, 4:5], scale=prm[:, j, 3:4])\
                   .then_inc(conv0_done, 1)

            def gate(k, j):
                n = N(k, j)
                act.wait_ge(g_ready, n)
                wait(act, h_ready, n - L)
                act.activation(sg[:, j, :], pg[:, :], ACT.Silu).then_inc(gate_done, 1)

            def conv_silu(k, j):
                n = N(k, j)
                act.wait_ge(taps_done, 3 * n)
                wait(act, t2_done, n - R)
                act.activation(xs[:, j % R, :], y[:, j % 2, :], ACT.Silu).then_inc(xs_ready, 1)

            def decay(k, j, e):
                act.wait_ge(masked, N(k, j))
                act.wait_ge(tab_in[j], 16 * turn(k, j))
                for c in range(CPB):
                    t = slice(c * P, (c + 1) * P)
                    last = act.activation(cm[:, j, e, t], cm[:, j, e, t], ACT.Exp,
                                          bias=tab[:, j, 0, 2 * c + e:2 * c + e + 1])
                last.then_inc(exp_done, 1)

            def decay_first(k, j):
                decay(k, j, 0)

            def decay_second(k, j):
                decay(k, j, 1)

            def first_state(k, j):
                n = N(k, j)
                act.wait_ge(st_done, n)
                wait(act, yo_done, n - 2)
                act.activation(S[:, j % 2, 0, :], pst[:, 0:P], ACT.Copy).then_inc(s1_done, 1)

            def out_weights_high(k, j):
                if j == 6:
                    act.wait_ge(wo_scaled, 2 * (k + 1))
                    wait(act, out_done, UNITS * k)
                    act.activation(wo_hi[:, :, :], wo_raw[:, :, 0:DM], ACT.Copy).then_inc(wo_hi_done, 1)

            def h_high(k, j):
                n = N(k, j)
                act.wait_ge(h_ready, n)
                wait(act, out_done, n - 2)
                act.activation(h_hi[:, j % 2, :], h[:, j % R, :], ACT.Copy).then_inc(h_hi_done, 1)

            def squares(k, j):
                n = N(k, j)
                act.wait_ge(h_ready, n)
                wait(act, acc_done, n - 2)
                act.activation(sq[:, j % 2, :], h[:, j % R, :], ACT.Square).then_inc(sq_done, 1)

            pipeline(act, (split_high, -1), (out_weights_high, 0), (even(conv_first), 0), (h_high, 5), (decay_first, 1),
                     (first_state, 3), (decay_second, 1), (squares, 5), (odd(conv_silu), 1), (even(gate), 0),
                     (odd(conv_first), -1), (even(conv_silu), 0), (odd(gate), -1))

        @block.vector
        def _(dve):
            def split_low(k, j):
                if j < 2:
                    dve.wait_ge(w_hi_done, 2 * k + j + 1)
                    dve.tensor_tensor(w_lo[:, j, :, :], w_raw[:, j, :, :], w_hi[:, j, :, :].bitcast(F32), ALU.subtract)\
                       .then_inc(w_ready, 1)

            def scale_out_weights(k, j):
                if j == 4:
                    dve.wait_ge(wo_in, 16 * (k + 1))
                    for e in range(2):
                        dve.tensor_scalar(wo_raw[:, e, 0:DM], wo_raw[:, e, 0:DM], wo_raw[:, e, DM:DM + 1], None, ALU.mult)\
                           .then_inc(wo_scaled, 1)

            def out_weights_low(k, j):
                if j == 6:
                    dve.wait_ge(wo_hi_done, k + 1)
                    dve.tensor_tensor(wo_lo[:, :, :], wo_raw[:, :, 0:DM], wo_hi[:, :, :].bitcast(F32), ALU.subtract)\
                       .then_inc(wo_ready, 1)

            def conv_taps(k, j):
                n = N(k, j)
                dve.wait_ge(conv0_done, n)
                for i in range(1, 4):
                    if i > 1:
                        dve.wait_ge(taps_done, 3 * (n - 1) + i - 1)
                    dve.scalar_tensor_tensor(y[:, j % 2, i:SEQ], px[:, 0:SEQ - i], prm[:, j, 3 - i:4 - i],
                                             y[:, j % 2, i:SEQ], ALU.mult, ALU.add).then_inc(taps_done, 1)

            def x_times_dt(k, j):
                n = N(k, j)
                dve.wait_ge(tr_done, n)
                dve.wait_ge(tab_in[j], 16 * turn(k, j))
                wait(dve, yd_done, n - R)
                wait(dve, xw_ready, n - R)
                dve.tensor_tensor(xdt[:, j % R, :].rearrange("p (n d) -> p n d", d=HD),
                                  pt[:, :].rearrange("p (n d) -> p n d", d=HD),
                                  tab[:, j, 1, :].unsqueeze(2).broadcast_to([P, 2 * CPB, HD]), ALU.mult)\
                   .then_inc(xdt_ready, 1)

            def scores(k, j):
                c = j // 2 * CPB
                for e in range(2):
                    dve.wait_ge(exp_done, 2 * N(k, j) - 1 + e)
                    last = dve.tensor_tensor(cm[:, j, e, :], cm[:, j, e, :],
                                             cb_m[:, c:c + CPB, :].rearrange("p c i -> p (c i)"), ALU.mult)
                last.then_inc(m_ready, 1)

            def direct_term(k, j):
                n = N(k, j)
                dve.wait_ge(yd_done, n)
                wait(dve, h_lo_done, n - R)
                wait(dve, sq_done, n - R)
                dve.scalar_tensor_tensor(t2[:, j % R, :], xs[:, j % R, :], prm[:, j, 5:6], pyd[:, :], ALU.mult, ALU.add)\
                   .then_inc(t2_done, 1)

            def recurrence(k, j):
                n = N(k, j)
                dve.wait_ge(s1_done, n)
                for c in range(1, CPB - 1):
                    if c > 1:
                        dve.wait_ge(rec_done, 2 * (n - 1) + c - 1)
                    for e in range(2):
                        d = slice(e * HD, (e + 1) * HD)
                        last = dve.scalar_tensor_tensor(S[:, j % 2, c, d], S[:, j % 2, c - 1, d],
                                                        tab[:, j, 3, 2 * c + e:2 * c + e + 1],
                                                        pst[:, c * P + e * HD:c * P + (e + 1) * HD], ALU.mult, ALU.add)
                    last.then_inc(rec_done, 1)

            def off_term(k, j):
                n = N(k, j)
                dve.wait_ge(yo_done, n)
                dve.wait_ge(er_in[j % R], 32 * (2 * k + j // R + 1))
                wait(dve, hs_done, n - 2)
                dve.tensor_tensor(t1[:, j % 2, :], pyo[:, 0:SEQ - P], er[:, j % R, :], ALU.mult).then_inc(t1_done, 1)

            def add_out(k, j):
                if j % 2 == 0:
                    return
                dve.wait_ge(out_done, N(k, j))
                b = j // 2
                acc = out_acc[:, b * CPB:(b + 1) * CPB, :].rearrange("p c d -> p (c d)")
                dve.tensor_tensor(acc, po[:, :], acc, ALU.add).then_inc(oacc_done, 1)

            pipeline(dve, (direct_term, 4), (scores, 2), (split_low, -1), (out_weights_low, 0), (off_term, 4),
                     (conv_taps, 0), (x_times_dt, 2), (recurrence, 3), (add_out, 6), (scale_out_weights, 0))

        @block.gpsimd
        def _(pool):
            def mask(k, j):
                pool.wait_ge(cm_in[j], 16 * turn(k, j))
                pool.sem_inc(mask_begun, 1)
                m = cm[:, j, :, :].rearrange("p e (c i) -> p (e c) i", i=P)
                pool.affine_select(out=m, in_=m, compare_op=ALU.is_ge, fill=masked_value, base=0,
                                   pattern=[[0, 2 * CPB], [1, P]], channel_multiplier=-1).then_inc(masked, 1)

            def x_to_state(k, j):
                n = N(k, j)
                pool.wait_ge(xdt_ready, n)
                wait(pool, st_done, n - 2)
                pool.tensor_tensor(xw[:, j % 2, :].rearrange("p (n d) -> p n d", d=HD),
                                   xdt[:, j % R, 0:SEQ - P].rearrange("p (n d) -> p n d", d=HD),
                                   tab[:, j, 2, 0:2 * (CPB - 1)].unsqueeze(2).broadcast_to([P, 2 * (CPB - 1), HD]),
                                   ALU.mult).then_inc(xw_ready, 1)

            def gated(k, j):
                n = N(k, j)
                pool.wait_ge(t1_done, n)
                pool.wait_ge(t2_done, n)
                pool.tensor_tensor(t2[:, j % R, P:SEQ], t2[:, j % R, P:SEQ], t1[:, j % 2, :], ALU.add).then_inc(hs_done, 1)
                pool.wait_ge(hs_done, n)
                pool.wait_ge(gate_done, n)
                pool.tensor_tensor(h[:, j % R, :], t2[:, j % R, :], sg[:, j, :], ALU.mult).then_inc(h_ready, 1)

            def h_low(k, j):
                n = N(k, j)
                pool.wait_ge(h_hi_done, n)
                wait(pool, out_done, n - 2)
                pool.tensor_tensor(h_lo[:, j % 2, :], h[:, j % R, :], h_hi[:, j % 2, :].bitcast(F32), ALU.subtract)\
                    .then_inc(h_lo_done, 1)

            def add_squares(k, j):
                pool.wait_ge(sq_done, N(k, j))
                wait(pool, acc_done, N(k, j) - 1)
                pool.tensor_tensor(sq_acc[:, j // 2, :], sq_acc[:, j // 2, :], sq[:, j % 2, :], ALU.add).then_inc(acc_done, 1)

            masked_value = pool.to_reg(MASKED)
            pipeline(pool, (mask, 0), (h_low, 5), (gated, 4), (x_to_state, 2), (add_squares, 5))


def mamba_output_phase(nc, x_dram, gate_dram, out_acc, sq_acc, x, x1_dram):
    with ExitStack() as ctx:
        sb = lambda n, s, d=F32: ctx.enter_context(nc.sbuf_tensor(f"mo_{n}", s, d))
        sem = ctx.enter_context(phase_semaphores(nc, "mo"))
        g = sb("g", [P, NT, DM])
        ones = sb("ones", [P, 1])
        var = sb("var", [P, NT])
        std = sb("std", [P, NT])
        rstd = sb("rstd", [P, NT])
        pv = ctx.enter_context(nc.psum_tensor("mo_pv", [P, NT], F32))
        ones_done, sums, var_done, std_done = map(sem, "ones_done sums var_done std_done".split())
        x_in, g_in = [sem(f"x_in{q}") for q in range(4)], [sem(f"g_in{q}") for q in range(4)]
        rstd_done, scaled, added, stored = map(sem, "rstd_done scaled added stored".split())
        block = ctx.enter_context(nc.Block())

        @block.sync
        def _(sp):
            for q in range(4):
                ts = slice(4 * q, 4 * q + 4)
                sp.dma_start(g[:, ts, :], gate_dram.rearrange("(t p) d -> p t d", p=P)[:, ts, :]).then_inc(g_in[q], 16)
                sp.dma_start(x[:, ts, :], x_dram.rearrange("(t p) d -> p t d", p=P)[:, ts, :]).then_inc(x_in[q], 16)
            ov = x1_dram.rearrange("(t p) d -> p t d", p=P)
            for q in range(4):
                sp.wait_ge(added, 4 * (q + 1))
                sp.dma_start(ov[:, 4 * q:4 * q + 4, :], x[:, 4 * q:4 * q + 4, :]).then_inc(stored, 16)
            sp.wait_ge(stored, 64)

        @block.tensor
        def _(pe):
            pe.wait_ge(ones_done, 1)
            for t in range(NT):
                m = pe.matmul(pv[:, t:t + 1], sq_acc[:, t // CPB, (t % CPB) * P:(t % CPB + 1) * P], ones[:, :],
                              start=True, stop=True)
            m.then_inc(sums, 1)

        @block.scalar
        def _(act):
            act.wait_ge(var_done, 1)
            act.activation(std[:, :], var[:, :], ACT.Sqrt).then_inc(std_done, 1)

        @block.vector
        def _(dve):
            dve.memset(ones[:, :], 1.0).then_inc(ones_done, 1)
            dve.wait_ge(sums, 1)
            dve.tensor_scalar(var[:, :], pv[:, :], 1.0 / DI, EPS, ALU.mult, ALU.add).then_inc(var_done, 1)
            dve.wait_ge(std_done, 1)
            dve.reciprocal(rstd[:, :], std[:, :]).then_inc(rstd_done, 1)
            dve.wait_ge(rstd_done, 1)
            for q in range(4):
                ts = range(4 * q, 4 * q + 4)
                dve.wait_ge(g_in[q], 16)
                for t in ts:
                    dve.scalar_tensor_tensor(g[:, t, :], out_acc[:, t, :], rstd[:, t:t + 1], g[:, t, :], ALU.mult, ALU.mult)\
                       .then_inc(scaled, 1)
                dve.wait_ge(x_in[q], 16)
                for t in ts:
                    dve.wait_ge(scaled, t + 1)
                    dve.tensor_tensor(x[:, t, :], x[:, t, :], g[:, t, :], ALU.add).then_inc(added, 1)


def constants_phase(nc, ident, causal):
    with ExitStack() as ctx:
        ready = ctx.enter_context(phase_semaphores(nc, "const"))("ready")
        block = ctx.enter_context(nc.Block())

        @block.gpsimd
        def _(pool):
            pool.memset(ident[:, :], 0.0).then_inc(ready, 1)
            pool.memset(causal[:, :], 1.0).then_inc(ready, 1)
            pool.wait_ge(ready, 2)
            pool.affine_select(out=ident[:, :], in_=ident[:, :], compare_op=ALU.not_equal, fill=1.0, base=0,
                               pattern=[[-1, P]], channel_multiplier=1).then_inc(ready, 1)
            pool.affine_select(out=causal[:, :], in_=causal[:, :], compare_op=ALU.is_ge, fill=0.0, base=0,
                               pattern=[[1, P]], channel_multiplier=-1).then_inc(ready, 1)


HN, HW = 16, 16
GROUP = 4
MASK_SCORE = 10000.0


def attention_constants_phase(nc, ident_b, block_b, head_mask, later, ones, count, floor):
    with ExitStack() as ctx:
        sem = ctx.enter_context(phase_semaphores(nc, "ac"))
        s1, s2 = sem("ready"), sem("count")
        ci = ctx.enter_context(nc.sbuf_tensor("ac_ci", [P, CPB], mybir.dt.int32))
        block = ctx.enter_context(nc.Block())

        @block.gpsimd
        def _(pool):
            for m, value in ((ident_b, 0.0), (block_b, 0.0), (head_mask, 1.0), (later, 1.0), (ones, 1.0),
                             (floor, MASK_SCORE)):
                pool.memset(m[:, :], value).then_inc(s1, 1)
            pool.wait_ge(s1, 6)
            pool.affine_select(out=ident_b[:, :], in_=ident_b[:, :], compare_op=ALU.not_equal, fill=1.0, base=0,
                               pattern=[[-1, P]], channel_multiplier=1).then_inc(s1, 1)
            pool.affine_select(out=block_b[:, :], in_=block_b[:, :], compare_op=ALU.is_ge, fill=MASKED, base=0,
                               pattern=[[-1, P]], channel_multiplier=1).then_inc(s1, 1)
            pool.affine_select(out=later[:, :], in_=later[:, :], compare_op=ALU.is_ge, fill=0.0, base=-1,
                               pattern=[[-1, P]], channel_multiplier=1).then_inc(s1, 1)
            pool.affine_select(out=head_mask[:, :], in_=head_mask[:, :], compare_op=ALU.is_ge, fill=0.0, base=0,
                               pattern=[[-HW, P // HW]], channel_multiplier=1).then_inc(s1, 1)
            pool.wait_ge(s1, 10)
            pool.affine_select(out=head_mask[:, :], in_=head_mask[:, :], compare_op=ALU.is_ge, fill=0.0, base=HW - 1,
                               pattern=[[HW, P // HW]], channel_multiplier=-1).then_inc(s1, 1)
            pool.affine_select(out=floor[:, :], in_=floor[:, :], compare_op=ALU.is_ge, fill=-MASKED, base=SEQ - 2,
                               pattern=[[-P, CPB]], channel_multiplier=-1).then_inc(s1, 1)
            pool.iota(ci[:, :], pattern=[[-P, CPB]], base=SEQ - 1, channel_multiplier=-1).then_inc(s2, 1)

        @block.vector
        def _(dve):
            dve.wait_ge(s2, 1)
            dve.tensor_copy(count[:, :], ci[:, :]).then_inc(s2, 1)


def attention_phase(nc, xt_hi, xt_lo, w_dram, b_dram, bv_dram, wo_dram, bo_dram, ident, s1_dram):
    with ExitStack() as ctx:
        sb = lambda n, s, d=F32: ctx.enter_context(nc.sbuf_tensor(f"at_{n}", s, d))
        sem = ctx.enter_context(phase_semaphores(nc, "at"))
        BF = mybir.dt.bfloat16
        ident_b, block_b = sb("ident_b", [P, P], BF), sb("block_b", [P, P], BF)
        head_mask = sb("head_mask", [P, P // HW])
        later, ones = sb("later", [P, P]), sb("ones", [P, P])
        count, floor = sb("count", [P, CPB]), sb("floor", [P, CPB])
        attention_constants_phase(nc, ident_b, block_b, head_mask, later, ones, count, floor)
        W = 3 * DM
        GROUPS = HN // GROUP
        UNITS = HN * CPB
        w_raw = sb("w_raw", [P, KT, W])
        w_hi, w_lo = sb("w_hi", [P, KT, W], F32R), sb("w_lo", [P, KT, W], F32R)
        bias = sb("bias", [P, 2 * KT])
        bv, bo = sb("bv", [P, DM]), sb("bo", [P, DM])
        wo = sb("wo", [P, KT, DM])
        full = sb("full", [P, 2 * KT, SEQ])
        split = sb("split", [P, 4 * KT, SEQ], F32R)
        stack = sb("stack", [P, 4, 2, SEQ], F32R)
        q_lo, q_hi, k_hi, k_lo = (split[:, KT * i:KT * (i + 1), :] for i in range(4))
        vp = sb("vp", [P, CPB, HN, 32])
        sv = sb("sv", [P, CPB, DM])
        pe_ = sb("pe_", [P, 4, SEQ])
        pt_ = sb("pt_", [P, 2, GROUP, CPB, SEQ])
        mx = sb("mx", [P, CPB, HN])
        nm = sb("nm", [P, CPB, HN])
        rs = sb("rs", [P, CPB, HN])
        em = sb("em", [P, CPB, HN])
        den = sb("den", [P, CPB, HN])
        pvs = sb("pvs", [P, 2, SEQ])
        o = sb("o", [P, CPB, DM])
        s1 = sb("s1", [P, CPB, DM])
        ot = sb("ot", [P, KT, SEQ])
        vt = sb("vt", [P, KT, SEQ])
        sc = [ctx.enter_context(nc.psum_tensor(f"at_sc{i}", [P, SEQ], F32)) for i in range(4)]
        tp = [ctx.enter_context(nc.psum_tensor(f"at_tp{i}", [P, SEQ], F32)) for i in range(3)]
        pv = ctx.enter_context(nc.psum_tensor("at_pv", [P, SEQ], F32))
        names = ("w_in prm_in w_hi_done w_lo_done bias_done pad_done qk_done full_done qk_hi_done qk_lo_done "
                 "v_done vp_done sv_done svs_done cleared score_done max_done nm_done exp_done tp_done pt_act pt_dve "
                 "pv_done pvs_done turned_done em_in em_done den_done o_step ot_ready ot_act ot_dve proj_done s1_done s1_stored")
        (w_in, prm_in, w_hi_done, w_lo_done, bias_done, pad_done, qk_done, full_done, qk_hi_done, qk_lo_done,
         v_done, vp_done, sv_done, svs_done, cleared, score_done, max_done, nm_done, exp_done, tp_done, pt_act, pt_dve,
         pv_done, pvs_done, turned_done, em_in, em_done, den_done, o_step, ot_ready, ot_act, ot_dve, proj_done,
         s1_done, s1_stored) = map(sem, names.split())
        stacked = [sem(f"stacked{i}") for i in range(4)]
        block = ctx.enter_context(nc.Block())
        LAG_T, LAG_PV, LAG_X = 4, 7, 14
        END = UNITS + LAG_X + 1
        SV_AT = (4, 6, 11, 13)

        def p_tile(u):
            h, i = divmod(u, CPB)
            return (pt_[:, h // GROUP % 2, h % GROUP, 0:i + 1, i * P:(i + 1) * P],
                    tp[u % 3][:, 0:(i + 1) * P].rearrange("p (j t) -> p j t", t=P))

        def taken(b, u):
            h, i = divmod(u, CPB)
            return (pt_dve, pt_act)[i // 2], b * UNITS // 2 + 2 * h + i % 2 + 1

        @block.sync
        def _(sp):
            sp.dma_start(w_raw[:, :, :], w_dram.rearrange("(k p) n -> p k n", p=P)).then_inc(w_in, 16)
            sp.dma_start(bias[:, :], b_dram).then_inc(prm_in, 16)
            sp.dma_start(bv[:, :], bv_dram.broadcast_to([P, DM])).then_inc(prm_in, 16)
            sp.dma_start(bo[:, :], bo_dram.broadcast_to([P, DM])).then_inc(prm_in, 16)
            sp.dma_start(wo[:, :, :], wo_dram.rearrange("(k p) n -> p k n", p=P)).then_inc(prm_in, 16)

            def stack_head(b, h):
                if h >= 4:
                    sp.wait_ge(score_done, b * UNITS + (h - 3) * CPB)
                g, src = h // 8, slice(h % 8 * HW, (h % 8 + 1) * HW)
                for copy, (of_q, of_k) in enumerate(((KT, 2 * KT), (0, 2 * KT), (KT, 3 * KT))):
                    row = h % 2 * 4 * HW + copy * HW
                    sp.dma_start(stack[row:row + HW, h % 4, :, :].bitcast(F32),
                                 split[src, of_q + g:of_k + g + 1:of_k - of_q, :].bitcast(F32))\
                      .then_inc(stacked[h % 4], 16)

            def store(b):
                sp.wait_ge(s1_done, b + 2)
                sp.dma_start(s1_dram.rearrange("(b t p) d -> b p t d", b=BATCH, p=P)[bass.ds(b, 1)]
                             .rearrange("b p t d -> (b p) t d"), s1[:, :, :]).then_inc(s1_stored, 16)

            def batch(b, more):
                for h in range(4, HN):
                    stack_head(b, h)
                if more:
                    first_heads(b + 1)
                store(b)

            def first_heads(b):
                sp.wait_ge(qk_hi_done, b * 2 * KT + 2 * KT)
                sp.wait_ge(qk_lo_done, b * 2 * KT + 2 * KT)
                for h in range(4):
                    stack_head(b, h)

            sp.sem_inc(s1_stored, 16)
            sp.wait_ge(cleared, 1)
            first_heads(0)
            with sp.Fori(0, BATCH - 1) as b:
                batch(b, True)
            batch(BATCH - 1, False)
            sp.wait_ge(s1_stored, 16 * (BATCH + 1))

        @block.gpsimd
        def _(pool):
            pool.memset(stack[:, :, :, :].bitcast(F32), 0.0).then_inc(cleared, 1)

            def mask_terms(b, g):
                n = b * GROUPS + g
                hs = slice(g * GROUP, (g + 1) * GROUP)
                cols = slice(g * GROUP * HW, (g + 1) * GROUP * HW)
                pool.wait_ge(em_done, n + 1)
                pool.tensor_tensor(den[:, :, hs], em[:, :, hs], count[:, :].unsqueeze(2).broadcast_to([P, CPB, GROUP]),
                                   ALU.mult).then_inc(den_done, 1)
                pool.tensor_tensor(o[:, :, cols].rearrange("p i (h d) -> p i h d", d=HW),
                                   sv[:, :, cols].rearrange("p i (h d) -> p i h d", d=HW),
                                   em[:, :, hs].unsqueeze(3).broadcast_to([P, CPB, GROUP, HW]), ALU.mult).then_inc(o_step, 1)
                pool.wait_ge(den_done, 3 * n + 1)
                pool.tensor_tensor(den[:, :, hs], den[:, :, hs], rs[:, :, hs], ALU.add).then_inc(den_done, 1)

            with pool.Fori(0, BATCH) as b:
                for n in range(END):
                    g, r = divmod(n - LAG_PV - CPB + 2, GROUP * CPB)
                    if r == 0 and 0 < g <= GROUPS:
                        mask_terms(b, g - 1)

        @block.tensor
        def _(pe):
            def operands(b, m):
                c, toks = slice(m * P, (m + 1) * P), bass.ds(b * SEQ, SEQ)
                return ([w_hi[:, j, c] for j in range(KT)], [w_lo[:, j, c] for j in range(KT)],
                        [xt_hi[:, j, toks] for j in range(KT)], [xt_lo[:, j, toks] for j in range(KT)])

            def project_qk(b, m):
                wait(pe, exp_done, (b - 1) * UNITS + UNITS - 3 + m)
                split_matmuls(pe, sc[m][:, :], *operands(b, m)).then_inc(qk_done, 1)

            def project_v(b, m):
                if m == 0:
                    wait(pe, pt_act, b * UNITS // 2)
                    wait(pe, pt_dve, b * UNITS // 2)
                split_matmuls(pe, tp[m][:, :], *operands(b, 2 * KT + m)).then_inc(qk_done, 1)

            def turn_v(b, m):
                if m == 0:
                    pe.wait_ge(full_done, b * 2 * KT + 2 * KT)
                pe.wait_ge(v_done, KT * b + m + 1)
                for t in range(CPB):
                    last = pe.transpose(sc[2 + m][:, t * P:(t + 1) * P], vt[:, m, t * P:(t + 1) * P], ident[:, :])
                last.then_inc(qk_done, 1)

            def later_v(b, i):
                if i == 2:
                    pe.wait_ge(svs_done, KT * b + 1)
                for j in range(i, CPB):
                    last = pe.matmul(pv[:, i % 2 * DM:(i % 2 + 1) * DM], (later if j == i else ones)[:, :],
                                     vp[:, j, :, 0:HW], start=(j == i and i % 2 == 0), stop=(j == CPB - 1),
                                     skip_group_check=True)
                last.then_inc(sv_done, 1)

            def next_batch(b, q):
                if q < 2 * KT:
                    project_qk(b, q)
                elif q < 3 * KT:
                    project_v(b, q - 2 * KT)
                elif q == 9:
                    turn_v(b, 0)
                    turn_v(b, 1)

            def batch(b, more):
                pe.wait_ge(vp_done, KT * b + KT)

                def scores(u):
                    h, i = divmod(u, CPB)
                    if i == 0:
                        pe.wait_ge(stacked[h % 4], 48 * (b * HN // 4 + h // 4 + 1))
                    if u >= 4:
                        pe.wait_ge(exp_done, b * UNITS + u - 3)
                    n = (i + 1) * P
                    out, t = sc[u % 4][:, 0:n], slice(i * P, (i + 1) * P)
                    pe.matmul(sc[u % 4][:, i * P:n], ident_b[:, :], block_b[:, :], start=True, stop=False,
                              skip_group_check=True)
                    pe.matmul(out, stack[:, h % 4, 0, t], stack[:, h % 4, 1, 0:n], start=False, stop=True,
                              skip_group_check=True).then_inc(score_done, 1)

                def transposes(u):
                    h, i = divmod(u, CPB)
                    pe.wait_ge(exp_done, b * UNITS + u + 1)
                    if u == 0:
                        pe.wait_ge(s1_done, b + 1)
                    if u >= 3:
                        pe.wait_ge(*taken(b, u - 3))
                    for j in range(i + 1):
                        last = pe.transpose(tp[u % 3][:, j * P:(j + 1) * P], pe_[:, u % 4, j * P:(j + 1) * P], ident[:, :])
                    last.then_inc(tp_done, 1)

                def products(g, j):
                    if j == 0:
                        pe.wait_ge(pt_act, b * UNITS // 2 + 2 * GROUP * (g + 1))
                        pe.wait_ge(pt_dve, b * UNITS // 2 + 2 * GROUP * (g + 1))
                        if g:
                            pe.wait_ge(o_step, 3 * (b * GROUPS + g - 1) + 2)
                        else:
                            pe.wait_ge(svs_done, KT * b + KT)
                    for q in range(GROUP):
                        last = pe.matmul(pv[32 * q:32 * q + 32, j * P:SEQ], vp[:, j, GROUP * g + q, :],
                                         pt_[:, g % 2, q, j, j * P:SEQ], start=(j == 0), stop=(j == CPB - 1))
                    if j == CPB - 1:
                        last.then_inc(pv_done, 1)

                def turn_back(g):
                    pe.wait_ge(pvs_done, b * GROUPS + g + 1)
                    for i in range(CPB):
                        last = pe.transpose(pv[:, i * P:(i + 1) * P], pvs[:, g % 2, i * P:(i + 1) * P], ident[:, :])
                    last.then_inc(turned_done, 1)

                for n in range(END):
                    if n < UNITS:
                        scores(n)
                    if n in SV_AT:
                        later_v(b, SV_AT.index(n))
                    if 0 <= n - LAG_T < UNITS:
                        transposes(n - LAG_T)
                    g, r = divmod(n - LAG_PV + 1, GROUP * CPB)
                    if r < CPB and 0 < g <= GROUPS:
                        products(g - 1, r)
                    g, r = divmod(n - LAG_X + 1, GROUP * CPB)
                    if r == 0 and 0 < g <= GROUPS:
                        turn_back(g - 1)
                    if more and n >= UNITS:
                        next_batch(b + 1, n - UNITS)
                if more:
                    pe.wait_ge(full_done, (b + 2) * 2 * KT)
                pe.wait_ge(o_step, 3 * (b * GROUPS + GROUPS))
                for k in range(KT):
                    for i in range(CPB):
                        last = pe.transpose(sc[k][:, i * P:(i + 1) * P], o[:, i, k * P:(k + 1) * P], ident[:, :])
                    last.then_inc(ot_ready, 1)
                pe.wait_ge(ot_act, b + 1)
                pe.wait_ge(ot_dve, b + 1)
                for i in range(CPB):
                    for k in range(KT):
                        last = pe.matmul(tp[i // 2][:, i % 2 * DM:(i % 2 + 1) * DM], ot[:, k, i * P:(i + 1) * P], wo[:, k, :],
                                         start=(k == 0 and i % 2 == 0), stop=(k == KT - 1), skip_group_check=True)
                last.then_inc(proj_done, 1)

            pe.sem_inc(s1_done, 1)
            pe.wait_ge(w_lo_done, 1)
            for q in range(10):
                next_batch(0, q)
            with pe.Fori(0, BATCH - 1) as b:
                batch(b, True)
            batch(BATCH - 1, False)

        @block.scalar
        def _(act):
            act.wait_ge(w_in, 16)
            act.activation(w_hi[:, :, :], w_raw[:, :, :], ACT.Copy).then_inc(w_hi_done, 1)
            act.wait_ge(bias_done, 1)

            def take(b, m):
                act.wait_ge(qk_done, b * 4 * KT + m + 1)
                wait(act, qk_lo_done, b * 2 * KT)
                act.activation(full[:, m, :], sc[m][:, :], ACT.Identity, bias=bias[:, m:m + 1],
                               scale=0.25 if m < KT else 1.0).then_inc(full_done, 1)

            def high(b, m):
                act.wait_ge(full_done, b * 2 * KT + m + 1)
                act.activation((q_hi if m < KT else k_hi)[:, m % KT, :], full[:, m, :], ACT.Copy).then_inc(qk_hi_done, 1)

            def take_v(b, m):
                act.wait_ge(qk_done, b * 4 * KT + 2 * KT + m + 1)
                act.activation(vt[:, m, :], tp[m][:, :], ACT.Copy).then_inc(v_done, 1)

            def take_later_v(b, m):
                act.wait_ge(sv_done, CPB * b + 2 * m + 2)
                act.activation(sv[:, 2 * m:2 * m + 2, :].rearrange("p i d -> p (i d)"), pv[:, :], ACT.Copy)\
                   .then_inc(svs_done, 1)

            def next_batch(b, q):
                if q < 2 * KT:
                    take(b, q)
                elif q < 3 * KT:
                    high(b, 2 * q - 8)
                    high(b, 2 * q - 7)
                elif q < 4 * KT:
                    take_v(b, q - 3 * KT)

            def batch(b, more):
                def exps(u):
                    h, i = divmod(u, CPB)
                    act.wait_ge(nm_done, b * UNITS + u + 1)
                    if u >= 4:
                        act.wait_ge(tp_done, b * UNITS + u - 3)
                    n = (i + 1) * P
                    act.activation(pe_[:, u % 4, 0:n], sc[u % 4][:, 0:n], ACT.Exp, bias=nm[:, i, h:h + 1],
                                   accum_out=rs[:, i, h:h + 1]).then_inc(exp_done, 1)

                def evacuate(u):
                    h, i = divmod(u, CPB)
                    if i >= 2:
                        act.wait_ge(tp_done, b * UNITS + u + 1)
                        if h >= 2 * GROUP and h % GROUP == 0:
                            act.wait_ge(pv_done, b * GROUPS + h // GROUP - 1)
                        act.activation(*p_tile(u), ACT.Copy).then_inc(pt_act, 1)

                def mask_shares(g):
                    act.wait_ge(em_in, b * GROUPS + g + 1)
                    hs = slice(g * GROUP, (g + 1) * GROUP)
                    act.activation(em[:, :, hs], em[:, :, hs], ACT.Exp).then_inc(em_done, 1)

                for n in range(END):
                    if 0 <= n - LAG_T < UNITS:
                        evacuate(n - LAG_T)
                    if n < UNITS:
                        exps(n)
                    if n - 2 in SV_AT[1::2]:
                        take_later_v(b, SV_AT[1::2].index(n - 2))
                    g, r = divmod(n - LAG_PV - CPB + 2, GROUP * CPB)
                    if r == 0 and 0 < g <= GROUPS:
                        mask_shares(g - 1)
                        act.wait_ge(pv_done, b * GROUPS + g)
                        if g >= 3:
                            act.wait_ge(turned_done, b * GROUPS + g - 2)
                        act.activation(pvs[:, (g - 1) % 2, :], pv[:, :], ACT.Copy).then_inc(pvs_done, 1)
                    if more and n >= UNITS:
                        next_batch(b + 1, n - UNITS)
                act.wait_ge(ot_ready, 2 * b + 1)
                act.activation(ot[:, 0, :], sc[0][:, :], ACT.Copy).then_inc(ot_act, 1)

            for q in range(10):
                next_batch(0, q)
            with act.Fori(0, BATCH - 1) as b:
                batch(b, True)
            batch(BATCH - 1, False)

        @block.vector
        def _(dve):
            dve.memset(vp[:, :, :, :], 0.0).then_inc(pad_done, 1)
            dve.wait_ge(w_hi_done, 1)
            dve.tensor_tensor(w_lo[:, :, :], w_raw[:, :, :], w_hi[:, :, :].bitcast(F32), ALU.subtract).then_inc(w_lo_done, 1)
            dve.wait_ge(prm_in, 64)
            dve.tensor_scalar(bias[:, 0:KT], bias[:, 0:KT], 0.25, None, ALU.mult).then_inc(bias_done, 1)
            dve.wait_ge(pad_done, 1)

            def low(b, m):
                dve.wait_ge(qk_hi_done, b * 2 * KT + m + 1)
                hi, lo = (q_hi, q_lo) if m < KT else (k_hi, k_lo)
                dve.tensor_tensor(lo[:, m % KT, :], full[:, m, :], hi[:, m % KT, :].bitcast(F32), ALU.subtract)\
                   .then_inc(qk_lo_done, 1)

            def pad_v(b, m):
                dve.wait_ge(qk_done, b * 4 * KT + 3 * KT + m + 1)
                wait(dve, pv_done, b * GROUPS)
                hs = slice(m * HN // 2, (m + 1) * HN // 2)
                dve.tensor_tensor(vp[:, :, hs, 0:HW], sc[2 + m][:, :].rearrange("p (t h d) -> p t h d", t=CPB, d=HW),
                                  bv[:, m * P:(m + 1) * P].rearrange("p (h d) -> p h d", d=HW).unsqueeze(1)
                                  .broadcast_to([P, CPB, HN // 2, HW]), ALU.add).then_inc(vp_done, 1)

            def next_batch(b, q):
                if 4 <= q < 8:
                    low(b, q - 4)
                elif q == 9:
                    pad_v(b, 0)
                    pad_v(b, 1)

            def batch(b, more):
                def maxima(u):
                    h, i = divmod(u, CPB)
                    dve.wait_ge(score_done, b * UNITS + u + 1)
                    dve.reduce_max(mx[:, i, h:h + 1], sc[u % 4][:, 0:(i + 1) * P], AX.X).then_inc(max_done, 1)

                def negate(u):
                    h, i = divmod(u, CPB)
                    dve.wait_ge(max_done, b * UNITS + u + 1)
                    dve.scalar_tensor_tensor(nm[:, i, h:h + 1], mx[:, i, h:h + 1], -1.0, floor[:, i:i + 1],
                                             ALU.mult, ALU.min).then_inc(nm_done, 1)

                def evacuate(u):
                    h, i = divmod(u, CPB)
                    if i < 2:
                        dve.wait_ge(tp_done, b * UNITS + u + 1)
                        if h >= 2 * GROUP and h % GROUP == 0:
                            dve.wait_ge(pv_done, b * GROUPS + h // GROUP - 1)
                        dve.tensor_copy(*p_tile(u)).then_inc(pt_dve, 1)

                def shares_in(g):
                    hs = slice(g * GROUP, (g + 1) * GROUP)
                    dve.wait_ge(nm_done, b * UNITS + (g + 1) * GROUP * CPB)
                    dve.tensor_scalar(em[:, :, hs], nm[:, :, hs], MASK_SCORE, MASK_SCORE, ALU.min, ALU.subtract)\
                       .then_inc(em_in, 1)

                def combine(g):
                    n = b * GROUPS + g
                    hs = slice(g * GROUP, (g + 1) * GROUP)
                    cols = slice(g * GROUP * HW, (g + 1) * GROUP * HW)
                    quad = [P, CPB, GROUP, HW]
                    ov = o[:, :, cols].rearrange("p i (h d) -> p i h d", d=HW)
                    dve.wait_ge(turned_done, n + 1)
                    dve.wait_ge(o_step, 3 * n + 1)
                    dve.tensor_tensor(ov, pv[:, :].rearrange("p (i h d) -> p i h d", i=CPB, h=GROUP)[:, :, :, 0:HW],
                                      ov, ALU.add).then_inc(o_step, 1)
                    dve.wait_ge(den_done, 3 * n + 2)
                    dve.reciprocal(den[:, :, hs], den[:, :, hs]).then_inc(den_done, 1)
                    dve.wait_ge(den_done, 3 * n + 3)
                    dve.wait_ge(o_step, 3 * n + 2)
                    dve.tensor_tensor(ov, ov, den[:, :, hs].unsqueeze(3).broadcast_to(quad), ALU.mult).then_inc(o_step, 1)

                for n in range(END):
                    if n < UNITS:
                        maxima(n)
                    if 0 <= n - LAG_T < UNITS:
                        evacuate(n - LAG_T)
                    if n < UNITS:
                        negate(n)
                    g, r = divmod(n + 1, GROUP * CPB)
                    if r == 0 and 0 < g <= GROUPS:
                        shares_in(g - 1)
                    g, r = divmod(n - LAG_X + 1, GROUP * CPB)
                    if r == 0 and 0 < g <= GROUPS:
                        combine(g - 1)
                    if more and n >= UNITS:
                        next_batch(b + 1, n - UNITS)
                dve.wait_ge(ot_ready, 2 * b + 2)
                dve.tensor_copy(ot[:, 1, :], sc[1][:, :]).then_inc(ot_dve, 1)
                dve.wait_ge(proj_done, b + 1)
                dve.wait_ge(s1_stored, 16 * b + 16)
                for i in range(KT):
                    last = dve.tensor_tensor(s1[:, 2 * i:2 * i + 2, :], tp[i][:, :].rearrange("p (i d) -> p i d", d=DM),
                                             bo[:, :].unsqueeze(1).broadcast_to([P, 2, DM]), ALU.add)
                last.then_inc(s1_done, 1)

            for q in range(10):
                next_batch(0, q)
            with dve.Fori(0, BATCH - 1) as b:
                batch(b, True)
            batch(BATCH - 1, False)


EXPERTS, TOPK, FW = 32, 4, 96
INTER = 1024


def router_phase(nc, xt_hi, xt_lo, wg_dram, ident, wt_dram):
    with ExitStack() as ctx:
        sb = lambda n, s, d=F32: ctx.enter_context(nc.sbuf_tensor(f"ro_{n}", s, d))
        sem = ctx.enter_context(phase_semaphores(nc, "ro"))
        wr = sb("wr", [P, KT, P])
        w_hi, w_lo = sb("w_hi", [P, KT, P], F32R), sb("w_lo", [P, KT, P], F32R)
        full = [P, NT, EXPERTS]
        l, gt, eq, pre = sb("l", full), sb("gt", full), sb("eq", full), sb("pre", full)
        keep = sb("keep", full)
        m8 = sb("m8", [P, NT, 8])
        m, s, need = sb("m", [P, NT]), sb("s", [P, NT]), sb("need", [P, NT])
        wt = sb("wt", [EXPERTS, T])
        pl = ctx.enter_context(nc.psum_tensor("ro_pl", full, F32))
        pw = [ctx.enter_context(nc.psum_tensor(f"ro_pw{i}", [P, SEQ], F32)) for i in range(4)]
        bc = lambda ap: ap.unsqueeze(2).broadcast_to([P, NT, EXPERTS])
        STEP_WT = 19
        w_in, w_hi_done, w_lo_done, product, taken, logits, step, max_done, exp_done, keep_done, turned, wt_done, stored = map(
            sem, "w_in w_hi_done w_lo_done product taken logits step max_done exp_done keep_done turned wt_done stored".split())
        block = ctx.enter_context(nc.Block())

        @block.sync
        def _(sp):
            sp.dma_start(wr[:, :, :], wg_dram.rearrange("(k p) n -> p k n", p=P)).then_inc(w_in, 16)
            sp.wait_ge(wt_done, 4)
            sp.dma_start(wt_dram, wt[:, :]).then_inc(stored, 16)
            sp.wait_ge(stored, 16)

        @block.gpsimd
        def _(pool):
            pool.memset(keep[:, :, :], 1.0).then_inc(keep_done, 1)
            pool.wait_ge(keep_done, 1)
            pool.memset(keep[:, :, 0:1], 0.0).then_inc(keep_done, 1)

        @block.tensor
        def _(pe):
            pe.wait_ge(w_lo_done, 1)
            for q in range(4):
                qs = slice(q * SEQ, (q + 1) * SEQ)
                split_matmuls(pe, pw[q][:, :], [w_hi[:, k, :] for k in range(KT)], [w_lo[:, k, :] for k in range(KT)],
                              [xt_hi[:, k, qs] for k in range(KT)], [xt_lo[:, k, qs] for k in range(KT)]).then_inc(product, 1)
            for t in range(NT):
                if t % 4 == 0:
                    pe.wait_ge(taken, t // 4 + 1)
                last = pe.transpose(pl[:, t, :], wt[:, t * P:(t + 1) * P], ident[0:EXPERTS, 0:EXPERTS])
            last.then_inc(logits, 1)
            pe.wait_ge(step, STEP_WT)
            for t in range(NT):
                last = pe.transpose(pw[t // 4][0:EXPERTS, (t % 4) * P:(t % 4 + 1) * P], l[:, t, :], ident[:, :])
                if t % 4 == 3:
                    last.then_inc(turned, 1)

        @block.scalar
        def _(act):
            act.wait_ge(w_in, 16)
            act.activation(w_hi[:, :, :], wr[:, :, :], ACT.Copy).then_inc(w_hi_done, 1)
            for q in range(4):
                act.wait_ge(product, q + 1)
                act.activation(wt[:, q * SEQ:(q + 1) * SEQ], pw[q][0:EXPERTS, :], ACT.Copy).then_inc(taken, 1)
            act.wait_ge(step, 2)
            act.activation(l[:, :, :], l[:, :, :], ACT.Exp).then_inc(exp_done, 1)
            for q in range(4):
                act.wait_ge(turned, q + 1)
                act.activation(wt[:, q * SEQ:(q + 1) * SEQ], pw[q][0:EXPERTS, :], ACT.Copy).then_inc(wt_done, 1)

        @block.vector
        def _(dve):
            n = [0]

            def then(ins):
                n[0] += 1
                ins.then_inc(step, 1)
                dve.wait_ge(step, n[0])

            dve.wait_ge(w_hi_done, 1)
            dve.tensor_tensor(w_lo[:, :, :], wr[:, :, :], w_hi[:, :, :].bitcast(F32), ALU.subtract).then_inc(w_lo_done, 1)
            dve.wait_ge(logits, 1)
            then(dve.reduce_max(m[:, :], pl[:, :, :], AX.X))
            then(dve.tensor_tensor(l[:, :, :], pl[:, :, :], bc(m[:, :]), ALU.subtract))
            dve.wait_ge(exp_done, 1)
            then(dve.reduce_sum(s[:, :], l[:, :, :], AX.X))
            then(dve.reciprocal(s[:, :], s[:, :]))
            then(dve.tensor_tensor(l[:, :, :], l[:, :, :], bc(s[:, :]), ALU.mult))
            for t in range(NT):
                last = dve.max(m8[:, t, :], l[:, t, :])
            then(last)
            fourth = m8[:, :, TOPK - 1]
            then(dve.tensor_copy(m[:, :], fourth))
            then(dve.tensor_tensor(gt[:, :, :], l[:, :, :], bc(m[:, :]), ALU.is_gt))
            then(dve.tensor_tensor(eq[:, :, :], l[:, :, :], bc(m[:, :]), ALU.is_equal))
            then(dve.reduce_sum(need[:, :], gt[:, :, :], AX.X))
            then(dve.tensor_scalar(need[:, :], need[:, :], -1.0, float(TOPK), ALU.mult, ALU.add))
            dve.wait_ge(keep_done, 2)
            flat = lambda ap: ap[:, :, :].rearrange("p t e -> p (t e)")
            then(dve.tensor_tensor_scan(flat(pre), flat(keep), flat(eq), 0.0, ALU.mult, ALU.add))
            then(dve.tensor_tensor(pre[:, :, :], pre[:, :, :], bc(need[:, :]), ALU.is_le))
            then(dve.tensor_tensor(eq[:, :, :], eq[:, :, :], pre[:, :, :], ALU.mult))
            then(dve.tensor_tensor(gt[:, :, :], gt[:, :, :], eq[:, :, :], ALU.add))
            then(dve.tensor_tensor(l[:, :, :], l[:, :, :], gt[:, :, :], ALU.mult))
            then(dve.reduce_sum(s[:, :], l[:, :, :], AX.X))
            then(dve.reciprocal(s[:, :], s[:, :]))
            then(dve.tensor_tensor(l[:, :, :], l[:, :, :], bc(s[:, :]), ALU.mult))
            assert n[0] == STEP_WT


def recurrent_layers(nc, x, w_xg, w_bcdt, conv_bc, dt_prm, prm, w_out, f0_gate, f0_up, f0_down,
                     w_qkv, b_qk, b_v, w_o, b_o, w_router, f1_gate, f1_up, f1_down, out):
    dram = lambda n, s: nc.dram_tensor(n, s, F32).ap()
    scratch = (dram("cum", [HEADS, T]), dram("ecum", [HEADS, T]), dram("last", [HEADS, NT]),
               dram("tables", [P, PAIRS * BATCH * 4 * CPB * 2]))
    gate0, s1, x1, w_tok = dram("gate0", [T, DM]), dram("s1", [T, DM]), dram("x1", [T, DM]), dram("w_tok", [EXPERTS, T])
    with ExitStack() as ctx:
        sb = lambda c, n, s, d=F32: c.enter_context(nc.sbuf_tensor(n, s, d))
        ident, causal = sb(ctx, "ident", [P, P]), sb(ctx, "causal", [P, P])
        xt_hi, xt_lo = sb(ctx, "xt_hi", [P, KT, T], F32R), sb(ctx, "xt_lo", [P, KT, T], F32R)
        constants_phase(nc, ident, causal)
        layernorm_phase(nc, "ln0", x, ident, xt_hi, xt_lo)
        gated_ffn_phase(nc, "ffn", INTER // P, f0_gate, f0_up, f0_down, xt_hi, xt_lo, gate0)
        with ExitStack() as mamba:
            out_acc, sq_acc = sb(mamba, "out_acc", [P, NT, DM]), sb(mamba, "sq_acc", [P, BATCH, SEQ])
            with ExitStack() as ssm:
                b_tok, c_t, cb_m = sb(ssm, "b_tok", [P, NT, NS]), sb(ssm, "c_t", [P, T]), sb(ssm, "cb_m", [P, NT, P])
                dynamics_phase(nc, xt_hi, xt_lo, w_bcdt, conv_bc, dt_prm, ident, causal, b_tok, c_t, cb_m, scratch,
                               out_acc, sq_acc)
                ssm_phase(nc, xt_hi, xt_lo, w_xg, w_out, prm, ident, b_tok, c_t, cb_m, scratch, out_acc, sq_acc)
            x1_sb = sb(mamba, "x1_sb", [P, NT, DM])
            mamba_output_phase(nc, x, gate0, out_acc, sq_acc, x1_sb, x1)
            layernorm_phase(nc, "ln1", None, ident, xt_hi, xt_lo, x=x1_sb)
        attention_phase(nc, xt_hi, xt_lo, w_qkv, b_qk, b_v, w_o, b_o, ident, s1)
        router_phase(nc, xt_hi, xt_lo, w_router, ident, w_tok)
        gated_ffn_phase(nc, "moe", EXPERTS * FW // P, f1_gate, f1_up, f1_down, xt_hi, xt_lo, out, router=(w_tok, FW),
                        residual=(x1, s1))


def kernel(**inputs):
    import numpy as np
    import concourse.bacc as bacc
    from concourse.bass_utils import run_bass_kernel_spmd

    a = {n: np.asarray(v) for n, v in inputs.items()}
    w = a["L0_attn_in_proj_w"]
    conv = np.concatenate([a["L0_attn_conv_w"], a["L0_attn_conv_b"][:, None]], 1)
    xg = np.concatenate([w[:, DI:2 * DI].reshape(KT, P, PAIRS, P), w[:, :DI].reshape(KT, P, PAIRS, P)], 3)
    w_dt = w[:, 2 * DI + 2 * NS:]
    d_rows = np.repeat(a["L0_attn_D_param"], HD)[:, None]
    gu0, gu1 = a["L0_ffn_w_gate_up"], a["L1_ffn_gate_up_proj"]
    laid = {
        "x": a["L0_attn_hidden_states"].reshape(T, DM),
        "w_xg": xg.transpose(2, 1, 0, 3).reshape(PAIRS, P, KT * 2 * P),
        "w_bcdt": np.concatenate([w[:, 2 * DI:2 * DI + 2 * NS], w_dt, w_dt], 1),
        "conv_bc": conv[DI:],
        "dt_prm": np.stack([a["L0_attn_dt_bias"], a["L0_attn_A_log"]], 1),
        "prm": np.concatenate([conv[:DI], d_rows], 1).reshape(PAIRS, P, 6),
        "w_out": np.concatenate([a["L0_attn_out_proj_w"], a["L0_attn_norm_w"][:, None]], 1).reshape(PAIRS, P, DM + 1),
        "f0_gate": gu0[:INTER].T, "f0_up": gu0[INTER:].T, "f0_down": a["L0_ffn_w_down"].T,
        "w_qkv": a["L1_attn_Wqkv"],
        "b_qk": a["L1_attn_bqkv"][:2 * DM].reshape(2 * KT, P).T, "b_v": a["L1_attn_bqkv"][2 * DM:][None],
        "w_o": a["L1_attn_Wo"], "b_o": a["L1_attn_bo"][None],
        "w_router": np.tile(a["L1_ffn_gate"], (1, P // EXPERTS)),
        "f1_gate": gu1[:, :, :FW].transpose(1, 0, 2).reshape(DM, EXPERTS * FW),
        "f1_up": gu1[:, :, FW:].transpose(1, 0, 2).reshape(DM, EXPERTS * FW),
        "f1_down": a["L1_ffn_down_proj"].reshape(EXPERTS * FW, DM),
    }
    nc = bacc.Bacc("TRN2", target_bir_lowering=False, num_devices=1)
    arrays, args = {}, []
    for name, v in laid.items():
        v = np.ascontiguousarray(v)
        arrays[f"in_{name}"] = v
        args.append(nc.dram_tensor(f"in_{name}", v.shape, mybir.dt.from_np(v.dtype), kind="ExternalInput").ap())
    args.append(nc.dram_tensor("result", (T, DM), F32, kind="ExternalOutput").ap())
    recurrent_layers(nc, *args)
    r = run_bass_kernel_spmd(nc, [arrays], core_ids=[0])
    return r.results[0]["result"].reshape(BATCH, SEQ, DM)
```
